# Optimizing a Trainium2 kernel written in Bass

```python
import numpy as np
import jax
import jax.numpy as jnp

def _softmax(x, axis=-1):
    return jax.nn.softmax(x, axis=axis)

def _gelu(x):
    return jax.nn.gelu(x, approximate=True)

def _silu(x):
    return jax.nn.silu(x)

def _sigmoid(x):
    return jax.nn.sigmoid(x)

def _layernorm(x, axis=-1, eps=1e-05):
    m = jnp.mean(x, axis=axis, keepdims=True)
    v = jnp.var(x, axis=axis, keepdims=True)
    return (x - m) / jnp.sqrt(v + eps)

def _scatter_add(tgt, idx, src, axis=0):
    return tgt.at[idx].add(src)

def _segment_sum(src, seg, n):
    return jax.ops.segment_sum(src, seg, n)
kernel_name = 'mk_gnn_resnorm_d4_gnn_r32_8c142a'

def setup_inputs(seed: int=0):
    np.random.seed(seed)
    _w = jnp.asarray

    def _rec_inputs():
        import jax
        import jax.numpy as jnp
        _gk = jax.random.key(seed)
        x = -0.0006008 + 1.001 * jax.random.normal(jax.random.fold_in(_gk, 1), (3125, 256), jnp.float32)
        _s = jax.random.randint(jax.random.fold_in(_gk, 2), (25000,), 0, 3125, jnp.int32)
        _d = jax.random.randint(jax.random.fold_in(_gk, 3), (25000,), 0, 3125, jnp.int32)
        _loop = jnp.arange(3125, dtype=jnp.int32)
        src = jnp.concatenate([_s, _d, _loop])
        dst = jnp.concatenate([_d, _s, _loop])
        _o = jnp.argsort(dst, stable=True)
        src = src[_o]
        dst = dst[_o]
        edge_attr_3 = -1.09012e-05 + 0.99985 * jax.random.normal(jax.random.fold_in(_gk, 12), (53125, 3), jnp.float32)
        edge_type_16 = jax.random.randint(jax.random.fold_in(_gk, 14), (53125,), 0, 16, jnp.int32)
        return (x, src, dst, edge_attr_3, edge_type_16)
    x, src, dst, edge_attr_3, edge_type_16 = _rec_inputs()

    def _L0_gnn_setup():
        import jax, jax.numpy as jnp
        import numpy as np
        from jax.ops import segment_sum
        N_NODES = 10000
        N_EDGES = 5000
        IN_FEAT = 256
        OUT_FEAT = 256
        NUM_RELS = 16

        def _inv_degree(idx, n):
            deg = segment_sum(jnp.ones(idx.shape[0], dtype=jnp.float32), idx, num_segments=n)
            return jnp.where(deg > 0, 1.0 / deg, 0.0)

        def _typed_pass(feat, W, bias, src_idx, dst_idx, etypes, norm_per_edge, n):
            proj = jnp.einsum('ni,rio->rno', feat, W)
            m = proj[etypes, src_idx] + bias
            m = m * norm_per_edge[:, None]
            return segment_sum(m, dst_idx, num_segments=n)
        key = jax.random.key(seed)
        ks = jax.random.split(key, 8)
        feat = jax.random.normal(ks[0], (N_NODES, IN_FEAT), dtype=jnp.float32)
        Wf = jax.random.normal(ks[1], (NUM_RELS, IN_FEAT, OUT_FEAT), dtype=jnp.float32)
        Wb = jax.random.normal(ks[2], (NUM_RELS, IN_FEAT, OUT_FEAT), dtype=jnp.float32)
        loop_weight = jax.random.normal(ks[3], (IN_FEAT, OUT_FEAT), dtype=jnp.float32)
        forward_bias = jnp.zeros((OUT_FEAT,), dtype=jnp.float32)
        backward_bias = jnp.zeros((OUT_FEAT,), dtype=jnp.float32)
        self_bias = jnp.zeros((OUT_FEAT,), dtype=jnp.float32)
        src = jax.random.randint(ks[4], (N_EDGES,), 0, N_NODES, dtype=jnp.int32)
        dst = jax.random.randint(ks[5], (N_EDGES,), 0, N_NODES, dtype=jnp.int32)
        etypes = jax.random.randint(ks[6], (N_EDGES,), 0, NUM_RELS, dtype=jnp.int32)
        return {'feat': feat, 'Wf': Wf, 'Wb': Wb, 'loop_weight': loop_weight, 'forward_bias': forward_bias, 'backward_bias': backward_bias, 'self_bias': self_bias, 'src': src, 'dst': dst, 'etypes': etypes, 'use_dis_weight': 0, 'drop_out': 0}
    _L0_gnn_all = _L0_gnn_setup()
    _L0_gnn_in = {k: v for k, v in _L0_gnn_all.items() if k in ('Wf', 'Wb', 'loop_weight', 'forward_bias', 'backward_bias', 'self_bias')}
    del _L0_gnn_all

    def _L1_gnn_setup():
        import jax, jax.numpy as jnp
        import numpy as np
        N = 50000
        E = 12500
        IN = 256
        H = 8
        D = 32
        EF = 3
        key = jax.random.key(seed)
        ks = jax.random.split(key, 8)
        x = jax.random.normal(ks[0], (N, IN), dtype=jnp.float32)
        edge_index = jax.random.randint(ks[1], (2, E), 0, N, dtype=jnp.int64)
        edge_attr = jax.random.normal(ks[2], (E, EF), dtype=jnp.float32)
        W = jax.random.normal(ks[3], (H * D, IN), dtype=jnp.float32) * np.float32(np.sqrt(2.0 / (IN + H * D)))
        a_src = jax.random.normal(ks[4], (H, D), dtype=jnp.float32) * np.float32(np.sqrt(2.0 / (H + D)))
        a_dst = jax.random.normal(ks[5], (H, D), dtype=jnp.float32) * np.float32(np.sqrt(2.0 / (H + D)))
        edge_W = jax.random.normal(ks[6], (H * D, EF), dtype=jnp.float32) * np.float32(np.sqrt(2.0 / (EF + H * D)))
        edge_b = jnp.zeros((H * D,), dtype=jnp.float32)
        bias = jnp.zeros((H * D,), dtype=jnp.float32)
        return {'x': x, 'W': W, 'a_src': a_src, 'a_dst': a_dst, 'edge_W': edge_W, 'edge_b': edge_b, 'bias': bias, 'edge_attr': edge_attr, 'edge_index': edge_index}
    _L1_gnn_all = _L1_gnn_setup()
    _L1_gnn_in = {k: v for k, v in _L1_gnn_all.items() if k in ('W', 'a_src', 'a_dst', 'edge_W', 'edge_b', 'bias')}
    del _L1_gnn_all

    def _L2_gnn_setup():
        import jax, jax.numpy as jnp
        import numpy as np
        N_NODES = 50000
        N_EDGES = 25000
        HEADS = 4
        OUT_CH = 64
        NEG_SLOPE = 0.2

        def gat_conv(x, edge_index, W, att_src, att_dst, bias):
            n = x.shape[0]
            loops = jnp.arange(n, dtype=edge_index.dtype)
            src = jnp.concatenate([edge_index[0], loops])
            dst = jnp.concatenate([edge_index[1], loops])
            h = (x @ W).reshape(n, HEADS, OUT_CH)
            a_src = jnp.sum(h * att_src, axis=-1)
            a_dst = jnp.sum(h * att_dst, axis=-1)
            e = a_src[src] + a_dst[dst]
            e = jax.nn.leaky_relu(e, NEG_SLOPE)
            e_max = jax.ops.segment_max(e, dst, num_segments=n)
            e_exp = jnp.exp(e - e_max[dst])
            denom = jax.ops.segment_sum(e_exp, dst, num_segments=n)
            alpha = e_exp / (denom[dst] + 1e-16)
            msg = h[src] * alpha[:, :, None]
            out = jax.ops.segment_sum(msg, dst, num_segments=n)
            return out.reshape(n, HEADS * OUT_CH) + bias
        key = jax.random.key(seed)
        ks = jax.random.split(key, 10)
        d_in = 256
        d_hid = HEADS * OUT_CH
        s_in = 1.0 / np.sqrt(d_in)
        s_hid = 1.0 / np.sqrt(d_hid)
        return {'x': jax.random.normal(ks[0], (N_NODES, d_in), dtype=jnp.float32), 'edge_index': jax.random.randint(ks[1], (2, N_EDGES), 0, N_NODES, dtype=jnp.int32), 'W1': jax.random.normal(ks[2], (d_in, d_hid), dtype=jnp.float32) * s_in, 'att_src1': jax.random.normal(ks[3], (1, HEADS, OUT_CH), dtype=jnp.float32) * s_hid, 'att_dst1': jax.random.normal(ks[4], (1, HEADS, OUT_CH), dtype=jnp.float32) * s_hid, 'b1': jnp.zeros((d_hid,), dtype=jnp.float32), 'W2': jax.random.normal(ks[5], (d_hid, d_hid), dtype=jnp.float32) * s_hid, 'att_src2': jax.random.normal(ks[6], (1, HEADS, OUT_CH), dtype=jnp.float32) * s_hid, 'att_dst2': jax.random.normal(ks[7], (1, HEADS, OUT_CH), dtype=jnp.float32) * s_hid, 'b2': jnp.zeros((d_hid,), dtype=jnp.float32)}
    _L2_gnn_all = _L2_gnn_setup()
    _L2_gnn_in = {k: v for k, v in _L2_gnn_all.items() if k in ('W1', 'att_src1', 'att_dst1', 'b1', 'W2', 'att_src2', 'att_dst2', 'b2')}
    del _L2_gnn_all

    def _L3_gnn_setup():
        import jax, jax.numpy as jnp
        import numpy as np
        N_NODES = 50000
        N_EDGES = 25000
        IN_FEAT = 256
        HEADS = 8
        OUT_FEAT = 32
        key = jax.random.key(seed)
        k = jax.random.split(key, 6)
        x = jax.random.normal(k[0], (N_NODES, IN_FEAT), dtype=jnp.float32)
        edge_index = jax.random.randint(k[1], (2, N_EDGES), 0, N_NODES, dtype=jnp.int64)
        gain = np.sqrt(2.0)
        std_w = gain * np.sqrt(2.0 / (IN_FEAT + HEADS * OUT_FEAT))
        W = jax.random.normal(k[2], (HEADS * OUT_FEAT, IN_FEAT), dtype=jnp.float32) * std_w
        std_a = gain * np.sqrt(2.0 / (HEADS + OUT_FEAT))
        a_src = jax.random.normal(k[3], (HEADS, OUT_FEAT), dtype=jnp.float32) * std_a
        a_dst = jax.random.normal(k[4], (HEADS, OUT_FEAT), dtype=jnp.float32) * std_a
        bias = jax.random.normal(k[5], (HEADS * OUT_FEAT,), dtype=jnp.float32) * 0.02
        return {'x': x, 'edge_index': edge_index, 'W': W, 'a_src': a_src, 'a_dst': a_dst, 'bias': bias}
    _L3_gnn_all = _L3_gnn_setup()
    _L3_gnn_in = {k: v for k, v in _L3_gnn_all.items() if k in ('W', 'a_src', 'a_dst', 'bias')}
    del _L3_gnn_all
    return {'x': x, 'src': src, 'dst': dst, 'edge_attr_3': edge_attr_3, 'edge_type_16': edge_type_16, 'L0_gnn_Wf': _L0_gnn_in['Wf'], 'L0_gnn_Wb': _L0_gnn_in['Wb'], 'L0_gnn_loop_weight': _L0_gnn_in['loop_weight'], 'L0_gnn_forward_bias': _L0_gnn_in['forward_bias'], 'L0_gnn_backward_bias': _L0_gnn_in['backward_bias'], 'L0_gnn_self_bias': _L0_gnn_in['self_bias'], 'L1_gnn_W': _L1_gnn_in['W'], 'L1_gnn_a_src': _L1_gnn_in['a_src'], 'L1_gnn_a_dst': _L1_gnn_in['a_dst'], 'L1_gnn_edge_W': _L1_gnn_in['edge_W'], 'L1_gnn_edge_b': _L1_gnn_in['edge_b'], 'L1_gnn_bias': _L1_gnn_in['bias'], 'L2_gnn_W1': _L2_gnn_in['W1'], 'L2_gnn_att_src1': _L2_gnn_in['att_src1'], 'L2_gnn_att_dst1': _L2_gnn_in['att_dst1'], 'L2_gnn_b1': _L2_gnn_in['b1'], 'L2_gnn_W2': _L2_gnn_in['W2'], 'L2_gnn_att_src2': _L2_gnn_in['att_src2'], 'L2_gnn_att_dst2': _L2_gnn_in['att_dst2'], 'L2_gnn_b2': _L2_gnn_in['b2'], 'L3_gnn_W': _L3_gnn_in['W'], 'L3_gnn_a_src': _L3_gnn_in['a_src'], 'L3_gnn_a_dst': _L3_gnn_in['a_dst'], 'L3_gnn_bias': _L3_gnn_in['bias']}

def reference(x, src, dst, edge_attr_3, edge_type_16, L0_gnn_Wf, L0_gnn_Wb, L0_gnn_loop_weight, L0_gnn_forward_bias, L0_gnn_backward_bias, L0_gnn_self_bias, L1_gnn_W, L1_gnn_a_src, L1_gnn_a_dst, L1_gnn_edge_W, L1_gnn_edge_b, L1_gnn_bias, L2_gnn_W1, L2_gnn_att_src1, L2_gnn_att_dst1, L2_gnn_b1, L2_gnn_W2, L2_gnn_att_src2, L2_gnn_att_dst2, L2_gnn_b2, L3_gnn_W, L3_gnn_a_src, L3_gnn_a_dst, L3_gnn_bias):
    import jax
    import jax.numpy as jnp

    def _L0_gnn_ref(feat, Wf, Wb, loop_weight, forward_bias, backward_bias, self_bias, src, dst, etypes, use_dis_weight, drop_out):
        import jax, jax.numpy as jnp
        import numpy as np
        from jax.ops import segment_sum
        N_NODES = 10000
        N_EDGES = 5000
        IN_FEAT = 256
        OUT_FEAT = 256
        NUM_RELS = 16

        def _inv_degree(idx, n):
            deg = segment_sum(jnp.ones(idx.shape[0], dtype=jnp.float32), idx, num_segments=n)
            return jnp.where(deg > 0, 1.0 / deg, 0.0)

        def _typed_pass(feat, W, bias, src_idx, dst_idx, etypes, norm_per_edge, n):
            proj = jnp.einsum('ni,rio->rno', feat, W)
            m = proj[etypes, src_idx] + bias
            m = m * norm_per_edge[:, None]
            return segment_sum(m, dst_idx, num_segments=n)
        n = feat.shape[0]
        norm_f = _inv_degree(dst, n)[dst]
        m_forward = _typed_pass(feat, Wf, forward_bias, src, dst, etypes, norm_f, n)
        norm_b = _inv_degree(src, n)[src]
        m_backward = _typed_pass(feat, Wb, backward_bias, dst, src, etypes, norm_b, n)
        s = feat @ loop_weight
        s = s + s + self_bias
        return s + m_forward + m_backward

    def _L1_gnn_ref(x, W, a_src, a_dst, edge_W, edge_b, bias, edge_attr, edge_index):
        import jax, jax.numpy as jnp
        import numpy as np
        N = 50000
        E = 12500
        IN = 256
        H = 8
        D = 32
        EF = 3
        n = x.shape[0]
        h = (x @ W.T).reshape(n, H, D)
        src, dst = (edge_index[0], edge_index[1])
        h_src = h[src]
        h_dst = h[dst]
        alpha = jnp.einsum('ehd,hd->eh', h_src, a_src) + jnp.einsum('ehd,hd->eh', h_dst, a_dst)
        enc = jax.nn.relu(edge_attr @ edge_W.T + edge_b).reshape(-1, H, D)
        alpha = alpha + jnp.sum(enc * h_dst, axis=-1)
        alpha = jnp.where(alpha >= 0, alpha, 0.2 * alpha)
        amax = jax.ops.segment_max(alpha, dst, num_segments=n)
        ex = jnp.exp(alpha - amax[dst])
        denom = jax.ops.segment_sum(ex, dst, num_segments=n)
        attn = ex / jnp.maximum(denom[dst], 1e-10)
        out = jax.ops.segment_sum(h_src * attn[..., None], dst, num_segments=n)
        return out.reshape(n, H * D) + bias

    def _L2_gnn_ref(x, edge_index, W1, att_src1, att_dst1, b1, W2, att_src2, att_dst2, b2):
        import jax, jax.numpy as jnp
        import numpy as np
        N_NODES = 50000
        N_EDGES = 25000
        HEADS = 4
        OUT_CH = 64
        NEG_SLOPE = 0.2

        def gat_conv(x, edge_index, W, att_src, att_dst, bias):
            n = x.shape[0]
            loops = jnp.arange(n, dtype=edge_index.dtype)
            src = jnp.concatenate([edge_index[0], loops])
            dst = jnp.concatenate([edge_index[1], loops])
            h = (x @ W).reshape(n, HEADS, OUT_CH)
            a_src = jnp.sum(h * att_src, axis=-1)
            a_dst = jnp.sum(h * att_dst, axis=-1)
            e = a_src[src] + a_dst[dst]
            e = jax.nn.leaky_relu(e, NEG_SLOPE)
            e_max = jax.ops.segment_max(e, dst, num_segments=n)
            e_exp = jnp.exp(e - e_max[dst])
            denom = jax.ops.segment_sum(e_exp, dst, num_segments=n)
            alpha = e_exp / (denom[dst] + 1e-16)
            msg = h[src] * alpha[:, :, None]
            out = jax.ops.segment_sum(msg, dst, num_segments=n)
            return out.reshape(n, HEADS * OUT_CH) + bias
        h = gat_conv(x, edge_index, W1, att_src1, att_dst1, b1)
        h = jax.nn.elu(h)
        h = gat_conv(h, edge_index, W2, att_src2, att_dst2, b2)
        h = jax.nn.elu(h)
        return h

    def _L3_gnn_ref(x, edge_index, W, a_src, a_dst, bias):
        import jax, jax.numpy as jnp
        import numpy as np
        N_NODES = 50000
        N_EDGES = 25000
        IN_FEAT = 256
        HEADS = 8
        OUT_FEAT = 32
        N = x.shape[0]
        H, F = a_src.shape
        h = (x @ W.T).reshape(N, H, F)
        src, dst = (edge_index[0], edge_index[1])
        h_src = h[src]
        h_dst = h[dst]
        alpha = jnp.einsum('ehf,hf->eh', h_src, a_src) + jnp.einsum('ehf,hf->eh', h_dst, a_dst)
        alpha = jnp.where(alpha >= 0, alpha, 0.2 * alpha)
        seg_max = jax.ops.segment_max(alpha, dst, num_segments=N)
        exp_a = jnp.exp(alpha - seg_max[dst])
        seg_sum = jax.ops.segment_sum(exp_a, dst, num_segments=N)
        alpha = exp_a / jnp.maximum(seg_sum[dst], 1e-10)
        msgs = h_src * alpha[:, :, None]
        agg = jax.ops.segment_sum(msgs, dst, num_segments=N)
        return agg.reshape(N, H * F) + bias
    edge_index = jnp.stack([src, dst])
    x = _layernorm(x + _L0_gnn_ref(x, L0_gnn_Wf, L0_gnn_Wb, L0_gnn_loop_weight, L0_gnn_forward_bias, L0_gnn_backward_bias, L0_gnn_self_bias, src, dst, edge_type_16, 0, 0), axis=-1)
    x = _layernorm(x + _L1_gnn_ref(x, L1_gnn_W, L1_gnn_a_src, L1_gnn_a_dst, L1_gnn_edge_W, L1_gnn_edge_b, L1_gnn_bias, edge_attr_3, edge_index), axis=-1)
    x = _layernorm(x + _L2_gnn_ref(x, edge_index, L2_gnn_W1, L2_gnn_att_src1, L2_gnn_att_dst1, L2_gnn_b1, L2_gnn_W2, L2_gnn_att_src2, L2_gnn_att_dst2, L2_gnn_b2), axis=-1)
    x = _layernorm(x + _L3_gnn_ref(x, edge_index, L3_gnn_W, L3_gnn_a_src, L3_gnn_a_dst, L3_gnn_bias), axis=-1)
    return x

_drawn_inputs = setup_inputs


def setup_inputs(seed=0):
    import zlib

    import numpy as np

    out = dict(_drawn_inputs(seed))
    spreads = {'L0_gnn_forward_bias': (0.0, 0.8),
     'L0_gnn_backward_bias': (0.0, 0.8),
     'L0_gnn_self_bias': (0.0, 0.8),
     'L1_gnn_edge_b': (0.0, 0.1),
     'L1_gnn_bias': (0.0, 0.1),
     'L2_gnn_b1': (0.0, 0.1),
     'L2_gnn_b2': (0.0, 0.1)}
    factors = {'L2_gnn_att_dst1': 27.547,
     'L2_gnn_att_src2': 8.0,
     'L2_gnn_att_dst2': 23.145,
     'L3_gnn_bias': 3.612}
    for name, (base, spread) in spreads.items():
        noise = np.random.default_rng([zlib.crc32(name.encode()), seed]).standard_normal(out[name].shape)
        drawn = base * np.exp(spread * noise) if base else spread * noise
        out[name] = jnp.asarray(drawn.astype(out[name].dtype))
    for name, factor in factors.items():
        out[name] = (out[name] * factor).astype(out[name].dtype)
    return out
```

```python
from contextlib import ExitStack

import concourse.bass as bass
from concourse import mybir

ALU = mybir.AluOpType
ACT = mybir.ActivationFunctionType
AX = mybir.AxisListType
F32 = mybir.dt.float32
BF16 = mybir.dt.bfloat16
I32 = mybir.dt.int32

P = 128
NODES = 3125
EDGES = 53125
FEAT = 256
RELS = 16
WINDOWS = -(-NODES // P)
NODES_PAD = WINDOWS * P
CHUNK = 44
CHUNKS = 10
TILES = CHUNK * CHUNKS
assert EDGES // P + WINDOWS <= TILES
SCAN_ROWS = 11
SCAN_TILES = CHUNK // SCAN_ROWS
SCAN_LEN = SCAN_TILES * P
EP, EJ = 125, 425
assert EP * EJ == EDGES
PARTS = EP // WINDOWS
PART_LEN = EDGES // PARTS
QUARTERS = 4
QT = TILES // QUARTERS
SEG_ROWS = CHUNKS * SCAN_ROWS
ROW = 264
COLS = 266
NTC = 272
STEP = 4
TURNS = CHUNK // STEP
BIG = 1e30
EPS = 1e-5
FAR = float(1 << 20)

C_IDENT, C_IOTA, C_ONES, C_BEFORE, C_WINOH, C_PART, C_WIN, C_TILE = 0, 128, 256, 384, 509, 534, 539, 540
C_COLS = 544


class Steps:

    def __init__(self, sem, base=0):
        self.sem, self.base, self.n = sem, base, 0

    def done(self, instruction):
        instruction.then_inc(self.sem, 1)
        self.n += 1

    def settled(self, engine):
        if self.n or not isinstance(self.base, int):
            engine.wait_ge(self.sem, self.base + self.n)


def phase_semaphores(nc, tag, ctx):
    sems = []

    def sem(name):
        sems.append(nc.alloc_semaphore(f"{tag}_{name}"))
        return sems[-1]

    ctx.callback(nc.all_engine_barrier)
    ctx.callback(nc.clear_and_free_semaphores, sems)
    return sem


def each_window(engine, body):
    with engine.Fori(0, WINDOWS // 2) as i:
        body(i * 2, 0)
        body(i * 2 + 1, 1)
    body(WINDOWS - 1, 0)


def group_edges(nc, tag, cst, d, dram, g):
    with ExitStack() as ctx:
        def sb(name, shape, dt=F32):
            return ctx.enter_context(nc.sbuf_tensor(f"{tag}_{name}", shape, dt))

        sem = phase_semaphores(nc, tag, ctx)

        rows_ps = ctx.enter_context(nc.psum_tensor(f"{tag}_rows_ps", [P, 512], F32))
        parts_ps = ctx.enter_context(nc.psum_tensor(f"{tag}_parts_ps", [P, 512], F32))
        pos_ps = [ctx.enter_context(nc.psum_tensor(f"{tag}_pos_ps{i}", [P, 512], F32)) for i in range(2)]
        lane_ps = [ctx.enter_context(nc.psum_tensor(f"{tag}_lane_ps{i}", [P, 512], F32)) for i in range(2)]

        src_e = sb("src_e", [EP, EJ], I32)
        dst_e = sb("dst_e", [EP, EJ], I32)
        typ_e = sb("typ_e", [EP, EJ], I32)
        flt_e = sb("flt_e", [EP, EJ])
        cmp_e = sb("cmp_e", [EP, EJ])
        win_i = sb("win_i", [EP, EJ], I32)
        win_f = sb("win_f", [EP, EJ])
        record = sb("record", [EP, EJ, 2], I32)
        pos_i = sb("pos_i", [EP, EJ], I32)
        below = sb("below", [EP, WINDOWS + 1])
        hit = sb("hit", [EP, PART_LEN])
        rank = sb("rank", [EP, PART_LEN])
        place = sb("place", [PARTS, PART_LEN], I32)
        total = sb("total", [EP, 1])
        total_b = sb("total_b", [EP, P])
        base = sb("base", [EP, 1])
        pick = sb("pick", [EP, WINDOWS])
        zeros = sb("zeros", [P, WINDOWS])
        start = sb("start", [P, 2, WINDOWS + 1])
        n_i = sb("n_i", [P, 2, WINDOWS], I32)
        n_t = sb("n_t", [P, 2, WINDOWS])
        last_t = sb("last_t", [P, 2, WINDOWS])
        first_t = sb("first_t", [P, 2, WINDOWS])
        shift = sb("shift", [P, WINDOWS])
        jump = sb("jump", [P, WINDOWS])
        ge = sb("ge", [P, WINDOWS])
        gej = sb("gej", [P, WINDOWS])
        win_t = sb("win_t", [QT, 2, QUARTERS])
        win128 = sb("win128", [QT, 2, QUARTERS])
        off_f = sb("off_f", [QT, QUARTERS])
        off_i = sb("off_i", [QT, QUARTERS], I32)
        pad = sb("pad", [P, TILES, 2], I32)
        r_dst = sb("r_dst", [QT, QUARTERS, P], I32)
        r_src = sb("r_src", [QT, QUARTERS, P], I32)
        r_typ = sb("r_typ", [QT, QUARTERS, P], I32)
        r_att = sb("r_att", [QT, 3, QUARTERS, P])
        r_one = sb("r_one", [QT, P])
        f_dst = sb("f_dst", [QT, QUARTERS, P])
        f_src = sb("f_src", [QT, QUARTERS, P])
        f_idx = sb("f_idx", [QT, QUARTERS, P])
        f_loc = sb("f_loc", [QT, QUARTERS, P])
        f_val = sb("f_val", [QT, QUARTERS, P])
        f_key = sb("f_key", [QT, QUARTERS, P])
        edge_key = sb("edge_key", [1, P])

        loaded = sem("loaded")
        windows_out = sem("windows_out")
        windows_in = sem("windows_in")
        pad_out = sem("pad_out")
        places_out = sem("places_out")
        places_in = sem("places_in")
        blocks_in, records_out = g["landed"][tag]
        keys_out = sem("keys_out")
        records_in = sem("records_in")
        rows_in = sem("rows_in")
        vec = sem("vec")
        src_windows = sem("src_windows")
        records_made = sem("records_made")
        pad_made = sem("pad_made")
        below_made = sem("below_made")
        total_made = sem("total_made")
        counts_done = sem("counts_done")
        parts_done = sem("parts_done")
        rank_made = sem("rank_made")
        sums_done = sem("sums_done")
        sums_taken = sem("sums_taken")
        offsets_made = sem("offsets_made")
        keys_made = sem("keys_made")
        lanes_ready = sem("lanes_ready")
        lanes_done = sem("lanes_done")
        lanes_taken = sem("lanes_taken")
        pieces = [(a, min(512, PART_LEN - a)) for a in range(0, PART_LEN, 512)]

        block = ctx.enter_context(nc.Block())

        @block.sync
        def _(sp):
            sp.dma_start(cst[:, :], d["consts"]).then_inc(loaded, 16)
            sp.dma_start(src_e[:, :], d["src"].rearrange("(p j) -> p j", p=EP)).then_inc(loaded, 16)
            sp.dma_start(dst_e[:, :], d["dst"].rearrange("(p j) -> p j", p=EP)).then_inc(loaded, 16)
            sp.dma_start(typ_e[:, :], d["edge_type_16"].rearrange("(p j) -> p j", p=EP)).then_inc(loaded, 16)
            sp.wait_ge(src_windows, 1)
            sp.dma_start(dram["src_win"].rearrange("(p j) -> p j", p=EP), win_f[:, :]).then_inc(windows_out, 16)
            sp.wait_ge(windows_out, 16)
            for w in range(WINDOWS):
                sp.dma_start(hit[w * PARTS:(w + 1) * PARTS, :],
                             dram["src_win"].rearrange("(c j) -> c j", c=PARTS)).then_inc(windows_in, 16)
            sp.wait_ge(pad_made, 2)
            sp.dma_start(dram["records"].rearrange("(p t) c -> p t c", p=P), pad[:, :, :]).then_inc(pad_out, 16)
            sp.wait_ge(keys_made, 1)
            for q in range(QUARTERS):
                sp.dma_start(dram["keys"][1 + q * QT:1 + (q + 1) * QT, :], f_key[:, q, :]).then_inc(keys_out, 16)
            for row in (0, TILES + 1):
                sp.dma_start(dram["keys"][row:row + 1, :], edge_key[:, :]).then_inc(keys_out, 16)
            sp.wait_ge(blocks_in, 16 * 6 * QUARTERS)
            for a in range(4):
                for q in range(QUARTERS):
                    sp.dma_start(dram["attrs"][a, q * QT:(q + 1) * QT, :],
                                 r_att[:, a, q, :] if a < 3 else r_one[:, :]).then_inc(keys_out, 16)
            sp.wait_ge(sums_taken, len(pieces))
            sp.dma_start(dram["places"].rearrange("(c j) -> c j", c=PARTS), place[:, :]).then_inc(places_out, 16)
            sp.wait_ge(places_out, 16)
            sp.dma_start(pos_i[:, :], dram["places"].rearrange("(p j) -> p j", p=EP)).then_inc(places_in, 16)
            sp.wait_ge(lanes_taken, 4)
            for way in range(2):
                sp.dma_start(dram["tile_win"][way].rearrange("(q p) -> q p", q=QUARTERS),
                             g["tile_win4"][:, way, :]).then_inc(rows_in, 16)
            sp.wait_ge(rows_in, 32)
            sp.dma_start(g["tile_win"][:, :, :], dram["tile_win"].rearrange("(a w) t -> a w t", a=1)).then_inc(rows_in, 16)
            sp.wait_ge(records_out, 16 * EJ)
            recs = dram["records"].rearrange("(q p e) c -> q p e c", q=QUARTERS, p=QT)
            for q in range(QUARTERS):
                sp.dma_start(pad[0:QT, q * P:(q + 1) * P, :] if q < 3 else record[0:QT, 0:P, :],
                             recs[q]).then_inc(records_in, 16)
            sp.wait_ge(keys_out, 16 * (QUARTERS + 2 + 4 * QUARTERS))
            sp.wait_ge(rows_in, 48)

        @block.gpsimd
        def _(gp):
            gp.wait_ge(offsets_made, 1)
            for q in range(QUARTERS):
                at = bass.IndirectOffsetOnAxis(ap=off_i[:, q:q + 1], axis=1)
                for flat, to in ((d["dst_pad"], r_dst[:, q, :]), (d["src_pad"], r_src[:, q, :]),
                                 (d["type_pad"], r_typ[:, q, :]), (d["attr0"], r_att[:, 0, q, :]),
                                 (d["attr1"], r_att[:, 1, q, :]), (d["attr2"], r_att[:, 2, q, :])):
                    gp.indirect_dma_start(out=to, out_offset=None, in_=flat.rearrange("(a b) -> a b", a=1),
                                          in_offset=at).then_inc(blocks_in, 16)
            gp.wait_ge(pad_out, 16)
            gp.wait_ge(places_in, 16)
            gp.wait_ge(records_made, 2)
            for j in range(EJ):
                gp.indirect_dma_start(out=dram["records"], out_offset=bass.IndirectOffsetOnAxis(ap=pos_i[:, j:j + 1], axis=0),
                                      in_=record[:, j, :], in_offset=None).then_inc(records_out, 16)
            gp.wait_ge(records_out, 16 * EJ)

        @block.tensor
        def _(pe):
            ones = cst[0:EP, C_ONES:C_ONES + P]
            pe.wait_ge(below_made, 1)
            pe.matmul(rows_ps[:, 0:WINDOWS + 1], ones, below[:, :], start=True, stop=True).then_inc(counts_done, 1)
            pe.wait_ge(total_made, 1)
            pe.matmul(rows_ps[:, 64:64 + WINDOWS], total_b[:, :], cst[0:EP, C_WINOH:C_WINOH + WINDOWS],
                      start=True, stop=True)
            pe.matmul(rows_ps[0:EP, 128:129], cst[0:EP, C_BEFORE:C_BEFORE + EP], total[:, :],
                      start=True, stop=True).then_inc(parts_done, 1)

            def lanes(n, views):
                pe.wait_ge(lanes_ready, n + 1)
                if n >= 2:
                    pe.wait_ge(lanes_taken, n - 1)
                for q, v in enumerate(views):
                    k, m = v.shape[0], v.shape[1]
                    mm = pe.transpose(lane_ps[n % 2][0:m, q * QT:q * QT + k], v, cst[0:k, C_IDENT:C_IDENT + k])
                mm.then_inc(lanes_done, 1)

            lanes(0, [win_t[:, 0, :]])
            lanes(1, [f_loc[:, q, :] for q in range(QUARTERS)])
            lanes(2, [f_src[:, q, :] for q in range(QUARTERS)])
            lanes(3, [win_t[:, 1, :]])
            lanes(4, [f_idx[:, q, :] for q in range(QUARTERS)])
            pe.wait_ge(rank_made, 1)
            for n, (a, m) in enumerate(pieces):
                if n >= 2:
                    pe.wait_ge(sums_taken, n - 1)
                pe.matmul(pos_ps[n % 2][0:PARTS, 0:m], cst[0:EP, C_PART:C_PART + PARTS], rank[:, a:a + m],
                          start=True, stop=True).then_inc(sums_done, 1)
            lanes(5, [f_loc[:, q, :] for q in range(QUARTERS)])
            lanes(6, [f_idx[:, q, :] for q in range(QUARTERS)])

        @block.scalar
        def _(act):
            for n, (a, m) in enumerate(pieces):
                act.wait_ge(sums_done, n + 1)
                act.copy(place[:, a:a + m], pos_ps[n % 2][0:PARTS, 0:m]).then_inc(sums_taken, 1)

        @block.vector
        def _(v):
            s = Steps(vec)
            v.memset(zeros[:, :], 0.0).then_inc(vec, 1)
            s.n += 1
            s.done(v.memset(below[:, 0:1], 0.0))
            s.done(v.memset(below[:, WINDOWS:WINDOWS + 1], float(EJ)))
            s.done(v.memset(edge_key[:, :], -2.0))
            s.done(v.memset(g["dst_slot"][:, TILES:], -1.0))
            s.done(v.memset(g["src_slot"][:, TILES:], -1.0))
            s.done(v.memset(r_one[:, :], 1.0))
            v.memset(pad[:, :, 0], -1).then_inc(pad_made, 1)
            v.memset(pad[:, :, 1], 0).then_inc(pad_made, 1)
            v.wait_ge(loaded, 64)
            s.done(v.tensor_scalar(win_i[:, :], src_e[:, :], 7, None, ALU.logical_shift_right))
            s.settled(v)
            v.tensor_copy(win_f[:, :], win_i[:, :]).then_inc(src_windows, 1)
            v.tensor_copy(record[:, :, 0], src_e[:, :]).then_inc(records_made, 1)
            v.scalar_tensor_tensor(out=record[:, :, 1], in0=dst_e[:, :], scalar=float(RELS), in1=typ_e[:, :],
                                   op0=ALU.mult, op1=ALU.add).then_inc(records_made, 1)
            s.done(v.tensor_copy(flt_e[:, :], dst_e[:, :]))
            s.settled(v)
            for w in range(1, WINDOWS):
                s.done(v.tensor_scalar(cmp_e[:, :], flt_e[:, :], float(w * P), None, ALU.is_lt))
                s.settled(v)
                s.done(v.tensor_reduce(below[:, w:w + 1], cmp_e[:, :], AX.X, ALU.add))
                s.settled(v)
            v.sem_inc(below_made, 1)

            def tiles_of(way):
                n = start[:, way, 1:] if way == 0 else start[:, way, 0:WINDOWS]
                if way == 0:
                    s.done(v.tensor_tensor(n_t[:, way, :], n, start[:, way, 0:WINDOWS], ALU.subtract))
                    s.settled(v)
                    n = n_t[:, way, :]
                s.done(v.tensor_scalar(n_i[:, way, :], n, float(P - 1), None, ALU.add))
                s.settled(v)
                s.done(v.tensor_scalar(n_i[:, way, :], n_i[:, way, :], 7, None, ALU.logical_shift_right))
                s.settled(v)
                s.done(v.tensor_scalar(n_t[:, way, :], n_i[:, way, :], 1.0, None, ALU.max))
                s.settled(v)
                s.done(v.tensor_tensor_scan(last_t[:, way, :], zeros[:, :], n_t[:, way, :], 0.0, ALU.add, ALU.add))
                s.settled(v)
                s.done(v.tensor_tensor(first_t[:, way, :], last_t[:, way, :], n_t[:, way, :], ALU.subtract))
                s.settled(v)

            def window_of_tiles(way):
                for q in range(QUARTERS):
                    tile = cst[0:QT, C_TILE + q:C_TILE + q + 1]
                    s.done(v.tensor_scalar(ge[0:QT, :], first_t[0:QT, way, :], tile, None, ALU.is_le))
                    s.settled(v)
                    s.done(v.tensor_reduce(win_t[:, way, q:q + 1], ge[0:QT, :], AX.X, ALU.add))
                    if way == 0:
                        s.done(v.tensor_tensor(gej[0:QT, :], ge[0:QT, :], jump[0:QT, :], ALU.mult))
                        s.settled(v)
                        s.done(v.tensor_reduce(off_f[:, q:q + 1], gej[0:QT, :], AX.X, ALU.add))
                    s.settled(v)
                s.done(v.tensor_scalar(win_t[:, way, :], win_t[:, way, :], -1.0, None, ALU.add))
                s.settled(v)
                s.done(v.tensor_scalar(win128[:, way, :], win_t[:, way, :], float(P), None, ALU.mult))
                s.settled(v)

            v.wait_ge(counts_done, 1)
            s.done(v.tensor_copy(start[:, 0, :], rows_ps[:, 0:WINDOWS + 1]))
            s.settled(v)
            tiles_of(0)
            s.done(v.scalar_tensor_tensor(out=shift[:, :], in0=first_t[:, 0, :], scalar=-float(P),
                                          in1=start[:, 0, 0:WINDOWS], op0=ALU.mult, op1=ALU.add))
            s.settled(v)
            s.done(v.tensor_copy(jump[:, 0:1], shift[:, 0:1]))
            s.done(v.tensor_tensor(jump[:, 1:], shift[:, 1:], shift[:, 0:WINDOWS - 1], ALU.subtract))
            s.settled(v)
            window_of_tiles(0)
            v.sem_inc(lanes_ready, 1)
            s.done(v.scalar_tensor_tensor(out=off_f[:, :], in0=cst[0:QT, C_TILE:C_TILE + QUARTERS], scalar=float(P),
                                          in1=off_f[:, :], op0=ALU.mult, op1=ALU.add))
            s.settled(v)
            v.tensor_scalar(off_i[:, :], off_f[:, :], float(EDGES), None, ALU.min).then_inc(offsets_made, 1)

            v.wait_ge(windows_in, 16 * WINDOWS)
            s.done(v.tensor_scalar(hit[:, :], hit[:, :], cst[0:EP, C_WIN:C_WIN + 1], None, ALU.is_equal))
            s.settled(v)
            s.done(v.tensor_tensor_scan(rank[:, :], hit[:, :], hit[:, :], 0.0, ALU.add, ALU.bypass))
            s.settled(v)
            s.done(v.tensor_copy(total[:, :], rank[:, PART_LEN - 1:PART_LEN]))
            s.settled(v)
            s.done(v.tensor_scalar(total_b[:, :], cst[0:EP, C_ONES:C_ONES + P], total[:, :], None, ALU.mult))
            s.settled(v)
            v.sem_inc(total_made, 1)

            v.wait_ge(lanes_done, 1)
            s.done(v.tensor_copy(g["tile_win4"][:, 0, :], lane_ps[0][0:QUARTERS, 0:QT]))
            s.settled(v)
            v.sem_inc(lanes_taken, 1)
            v.wait_ge(blocks_in, 16 * 6 * QUARTERS)
            s.done(v.tensor_copy(f_dst[:, :, :], r_dst[:, :, :]))
            s.done(v.tensor_copy(f_src[:, :, :], r_src[:, :, :]))
            s.settled(v)
            for q in range(QUARTERS):
                s.done(v.tensor_scalar(f_loc[:, q, :], f_dst[:, q, :], win128[:, 0, q:q + 1], None, ALU.subtract))
            s.settled(v)
            v.sem_inc(lanes_ready, 2)
            s.done(v.tensor_scalar(f_val[:, :, :], f_loc[:, :, :], 0.0, None, ALU.is_ge))
            s.settled(v)
            s.done(v.scalar_tensor_tensor(out=f_val[:, :, :], in0=f_loc[:, :, :], scalar=float(P), in1=f_val[:, :, :],
                                          op0=ALU.is_lt, op1=ALU.mult))
            s.settled(v)
            s.done(v.scalar_tensor_tensor(out=f_key[:, :, :], in0=f_dst[:, :, :], scalar=1.0, in1=f_val[:, :, :],
                                          op0=ALU.add, op1=ALU.mult))
            s.settled(v)
            v.tensor_scalar(f_key[:, :, :], f_key[:, :, :], -1.0, None, ALU.add).then_inc(keys_made, 1)
            s.done(v.scalar_tensor_tensor(out=f_idx[:, :, :], in0=f_src[:, :, :], scalar=float(RELS), in1=r_typ[:, :, :],
                                          op0=ALU.mult, op1=ALU.add))
            s.settled(v)

            v.wait_ge(parts_done, 1)
            s.done(v.tensor_copy(start[:, 1, 0:WINDOWS], rows_ps[:, 64:64 + WINDOWS]))
            s.done(v.tensor_copy(base[:, :], rows_ps[0:EP, 128:129]))
            s.settled(v)
            tiles_of(1)
            window_of_tiles(1)
            s.done(v.tensor_tensor(pick[:, :], cst[0:EP, C_WINOH:C_WINOH + WINDOWS], first_t[0:EP, 1, :], ALU.mult))
            s.settled(v)
            s.done(v.tensor_reduce(total[:, :], pick[:, :], AX.X, ALU.add))
            s.settled(v)
            s.done(v.scalar_tensor_tensor(out=base[:, :], in0=total[:, :], scalar=float(P), in1=base[:, :],
                                          op0=ALU.mult, op1=ALU.add))
            s.settled(v)
            s.done(v.tensor_scalar(base[:, :], base[:, :], -1.0, None, ALU.add))
            s.settled(v)
            v.scalar_tensor_tensor(out=rank[:, :], in0=rank[:, :], scalar=base[:, 0:1], in1=hit[:, :],
                                   op0=ALU.add, op1=ALU.mult).then_inc(rank_made, 1)

            def take(n, out):
                v.wait_ge(lanes_done, n + 1)
                k = out.shape[0]
                v.tensor_copy(out, lane_ps[n % 2][0:k, 0:out.shape[1]]).then_inc(lanes_taken, 1)

            take(1, g["dst_slot"][:, 0:TILES])
            take(2, g["src_idx"][:, :])
            v.sem_inc(lanes_ready, 2)
            take(3, g["tile_win4"][:, 1, :])
            take(4, g["fwd_idx"][:, :])
            v.wait_ge(records_in, 16 * QUARTERS)
            for q in range(QUARTERS):
                rec = pad[0:QT, q * P:(q + 1) * P, :] if q < 3 else record[0:QT, 0:P, :]
                s.done(v.tensor_scalar(f_loc[:, q, :], rec[:, :, 0], win128[:, 1, q:q + 1], None, ALU.subtract))
                s.done(v.tensor_copy(f_idx[:, q, :], rec[:, :, 1]))
            s.settled(v)
            v.sem_inc(lanes_ready, 2)
            take(5, g["src_slot"][:, 0:TILES])
            take(6, g["bwd_idx"][:, :])


def project_relations(nc, tag, cst, d, dram):
    with ExitStack() as ctx:
        def sb(name, shape, dt=F32):
            return ctx.enter_context(nc.sbuf_tensor(f"{tag}_{name}", shape, dt))

        sem = phase_semaphores(nc, tag, ctx)

        w_sb = sb("w_sb", [P, 2, 2, RELS, FEAT])
        xw = sb("xw", [P, 2, FEAT])
        xt = sb("xt", [P, 2, 2, P])
        stage = sb("stage", [P, 4, RELS // 2, FEAT])
        xt_ps = [ctx.enter_context(nc.psum_tensor(f"{tag}_xt_ps{i}", [P, 512], F32)) for i in range(2)]
        out_ps = [ctx.enter_context(nc.psum_tensor(f"{tag}_out_ps{i}", [P, 512], F32)) for i in range(4)]
        w_in = sem("w_in")
        x_in = [sem(f"x_in{i}") for i in range(2)]
        x_used = sem("x_used")
        xt_done = sem("xt_done")
        xt_taken = sem("xt_taken")
        xt_used = sem("xt_used")
        out_done = sem("out_done")
        out_taken = [sem("taken_vector"), sem("taken_scalar")]
        stored = [sem(f"stored{i}") for i in range(4)]
        stage_free = [sem(f"stage_free{i}") for i in range(4)]
        PAIRS = RELS
        AHEAD = 2
        block = ctx.enter_context(nc.Block())

        @block.sync
        def _(sp):
            for st in range(4):
                sp.sem_inc(stage_free[st], 1)
            for way, name in enumerate(("L0_gnn_Wf", "L0_gnn_Wb")):
                for r in range(RELS):
                    sp.dma_start(w_sb[:, way, :, r, :], d[name][r].rearrange("(k p) n -> p k n", p=P)).then_inc(w_in, 16)

            def load(w, par):
                sp.wait_ge(xt_done, w + AHEAD - 1)
                sp.dma_start(xw[:, par, :], d["x_pad"][bass.ds(w * P, P), :]).then_inc(x_in[par], 16)

            def store(w, par):
                for st in range(4):
                    way, half = st // 2, st % 2
                    for s in out_taken:
                        sp.wait_ge(s, w * (PAIRS // 2) + 2 * (st + 1) + AHEAD)
                    sp.dma_start(dram[("rel_table_f", "rel_table_b")[way]].rearrange("(n r) f -> n r f", r=RELS)
                                 [bass.ds(w * P, P), half * 8:half * 8 + 8, :],
                                 stage[:, st, :, :]).then_inc(stored[st], 16)
                for st in range(4):
                    sp.wait_ge(stored[st], (w + 1) * 16)
                    sp.sem_inc(stage_free[st], 1)

            load(0, 0)
            with sp.Fori(0, WINDOWS // 2) as i:
                load(i * 2 + 1, 1)
                store(i * 2, 0)
                load(i * 2 + 2, 0)
                store(i * 2 + 1, 1)
            store(WINDOWS - 1, 0)

        @block.tensor
        def _(pe):
            pe.sem_inc(xt_done, AHEAD)
            pe.sem_inc(out_done, AHEAD * PAIRS)
            pe.wait_ge(w_in, 16 * 2 * RELS)

            def body(w, par):
                pe.wait_ge(x_in[par], (w + (2 - par)) * 8)
                pe.wait_ge(xt_taken, w + 1)
                for k in range(2):
                    mm = pe.transpose(xt_ps[par][:, k * P:(k + 1) * P], xw[:, par, k * P:(k + 1) * P],
                                      cst[:, C_IDENT:C_IDENT + P])
                mm.then_inc(xt_done, 1)
                pe.wait_ge(xt_taken, w + 1 + AHEAD)
                for n in range(PAIRS):
                    way, r = n // 8, 2 * (n % 8)
                    pe.wait_ge(out_taken[n % 2], w * (PAIRS // 2) + n // 2 - 1 + AHEAD)
                    for k in range(2):
                        mm = pe.matmul(out_ps[n % 4][:, :], xt[:, par, k, :],
                                       w_sb[:, way, k, r:r + 2, :].rearrange("p r f -> p (r f)"),
                                       start=(k == 0), stop=(k == 1))
                    mm.then_inc(out_done, 1)

            each_window(pe, body)

        def take(eng, copy, lane):
            def body(w, par):
                for n in range(lane, PAIRS, 2):
                    st = n // 4
                    eng.wait_ge(out_done, (w + AHEAD) * PAIRS + n + 1)
                    if n % 4 < 2:
                        eng.wait_ge(stage_free[st], w + 1)
                    copy(stage[:, st, 2 * (n % 4):2 * (n % 4) + 2, :].rearrange("p r f -> p (r f)"),
                         out_ps[n % 4][:, :]).then_inc(out_taken[lane], 1)
            return body

        @block.vector
        def _(v):
            v.sem_inc(out_taken[0], AHEAD)
            each_window(v, take(v, v.tensor_copy, 0))

        @block.scalar
        def _(act):
            act.sem_inc(out_taken[1], AHEAD)
            act.sem_inc(xt_taken, AHEAD)
            odd_banks = take(act, act.copy, 1)

            def body(w, par):
                act.wait_ge(xt_done, w + 1 + AHEAD)
                act.wait_ge(out_done, (w + AHEAD - 1) * PAIRS)
                act.copy(xt[:, par, :, :].rearrange("p k e -> p (k e)"), xt_ps[par][:, 0:2 * P]).then_inc(xt_taken, 1)
                odd_banks(w, par)

            each_window(act, body)


def scan_tables(nc, tag, cst, dram, g):
    with ExitStack() as ctx:
        def sb(name, shape, dt=F32):
            return ctx.enter_context(nc.sbuf_tensor(f"{tag}_{name}", shape, dt))

        sem = phase_semaphores(nc, tag, ctx)

        key = sb("key", [SEG_ROWS, 3, SCAN_LEN])
        brk = sb("brk", [SEG_ROWS, 2, SCAN_LEN])
        brk_h = sb("brk_h", [SEG_ROWS, 2, SCAN_LEN], BF16)
        last = sb("last", [SEG_ROWS, SCAN_LEN])
        col = sb("col", [SEG_ROWS, 3])
        rows_ps = ctx.enter_context(nc.psum_tensor(f"{tag}_rows_ps", [P, 512], F32))
        last_ps = ctx.enter_context(nc.psum_tensor(f"{tag}_last_ps", [P, 512], F32))
        keys_in = sem("keys_in")
        vec = sem("vec")
        made = sem("made")
        turned = sem("turned")
        breaks_out = sem("breaks_out")
        breaks_in = sem("breaks_in")
        block = ctx.enter_context(nc.Block())

        @block.sync
        def _(sp):
            line = dram["keys"].rearrange("t e -> (t e)")
            for i, by in enumerate((0, -1, 1)):
                sp.dma_start(key[:, i, :], line[P + by:P + by + TILES * P].rearrange("(r e) -> r e", r=SEG_ROWS))\
                    .then_inc(keys_in, 16)
            sp.wait_ge(made, 1)
            sp.wait_ge(made, 2)
            for way in range(2):
                sp.dma_start(dram["breaks"][way], brk_h[:, way, :]).then_inc(breaks_out, 16)
            sp.wait_ge(breaks_out, 32)
            for way, to in enumerate((g["break_f"], g["break_b"])):
                for h in range(8):
                    sp.dma_start(to[h * SCAN_ROWS:(h + 1) * SCAN_ROWS, :, :],
                                 dram["breaks"][way].rearrange("(k c) e -> c k e", c=SCAN_ROWS)).then_inc(breaks_in, 16)
            sp.wait_ge(breaks_in, 16 * 16)

        @block.tensor
        def _(pe):
            pe.wait_ge(made, 2)
            ident = cst[0:SEG_ROWS, C_IDENT:C_IDENT + SEG_ROWS]
            for i in range(3):
                pe.matmul(rows_ps[0:1, i * P:i * P + SEG_ROWS], col[:, i:i + 1], ident, start=True, stop=True)
            for b in range(SCAN_TILES):
                mm = pe.transpose(last_ps[:, b * P:b * P + SEG_ROWS], last[:, b * P:(b + 1) * P], ident)
            mm.then_inc(turned, 1)

        @block.vector
        def _(v):
            s = Steps(vec)
            s.done(v.memset(g["chain_f"][:, :, :, :], -BIG))
            s.done(v.memset(g["chain_b"][:, :, :, :], -BIG))
            v.wait_ge(keys_in, 48)
            for i in range(2):
                s.done(v.tensor_tensor(brk[:, i, :], key[:, 0, :], key[:, 1 + i, :], ALU.is_equal))
            s.settled(v)
            s.done(v.tensor_scalar(brk[:, :, :], brk[:, :, :], -1.0, BIG, ALU.add, ALU.mult))
            s.settled(v)
            s.done(v.tensor_copy(brk_h[:, 0, :], brk[:, 0, :]))
            v.tensor_copy(brk_h[:, 1, ::-1], brk[:, 1, :]).then_inc(made, 1)
            s.done(v.tensor_scalar(last[:, :], brk[:, 1, :], -1.0, None, ALU.is_lt))
            s.done(v.tensor_reduce(col[:, 0:2], brk[:, :, :], AX.X, ALU.min))
            s.done(v.tensor_scalar(col[:, 2:3], brk[:, 0, 0:1], -1.0, None, ALU.is_ge))
            s.settled(v)
            v.wait_ge(made, 1)
            v.sem_inc(made, 1)
            v.wait_ge(turned, 1)
            for h in range(8):
                row = [rows_ps[0:1, i * P:i * P + SEG_ROWS].rearrange("a (k c) -> a k c", c=SCAN_ROWS) for i in range(3)]
                s.done(v.tensor_copy(g["chain_f"][:, :, h, 1:], row[0]))
                s.done(v.tensor_copy(g["chain_b"][:, :, h, 1:], row[1][:, :, ::-1]))
            s.done(v.tensor_copy(g["goes_on"][:, :], row[2][:, :, 0]))
            for b in range(SCAN_TILES):
                s.done(v.tensor_copy(
                    g["last"][:, :].rearrange("p (k c b) -> p (k c) b", c=SCAN_ROWS, b=SCAN_TILES)[:, :, b],
                    last_ps[:, b * P:b * P + SEG_ROWS]))
            s.settled(v)


def take_rows(gp, table, rows, cur, idx, free, ahead, landed, copied, width):
    def chunk(k, turn, half):
        gp.wait_ge(free, (k - 1) * CHUNK + ahead)
        gp.sem_inc(copied, 1)
        gp.tensor_copy(cur[:, half, :], idx[:, bass.ds(k * CHUNK, CHUNK)]).then_inc(copied, 1)
        gp.wait_ge(copied, (k + 1) * 3 - 1)
        gp.sem_inc(copied, 1)
        for j in range(CHUNK):
            gp.indirect_dma_start(out=rows[:, half, j, 0:width], out_offset=None, in_=table,
                                  in_offset=bass.IndirectOffsetOnAxis(ap=cur[:, half, j:j + 1], axis=0))\
                .then_inc(landed[half], 16)

    with gp.Fori(0, CHUNKS // 2) as i:
        for half in range(2):
            chunk(i * 2 + half, i, half)


def each_chunk(engine, body):
    with engine.Fori(0, CHUNKS // 2) as i:
        for half in range(2):
            body(i * 2 + half, i, half)


def tile_windows(engine, regs, tile_win, way, tile):
    engine.reg_load(regs, tile_win[0:1, way, bass.ds(tile, STEP)])
    return [engine.snap(r, min_val=0, max_val=WINDOWS - 1) for r in regs]


def relation_edges(nc, tag, cst, dram, g, rows, way, acc):
    with ExitStack() as ctx:
        sem = phase_semaphores(nc, tag, ctx)

        cur = ctx.enter_context(nc.sbuf_tensor(f"{tag}_cur", [P, 2, CHUNK], I32))
        onehot = ctx.enter_context(nc.sbuf_tensor(f"{tag}_onehot", [P, 2, 2, P], F32))
        sum_ps = [ctx.enter_context(nc.psum_tensor(f"{tag}_sum_ps{i}", [P, 512], F32)) for i in range(STEP)]
        slot, idx = (g["dst_slot"], g["fwd_idx"]) if way == 0 else (g["src_slot"], g["bwd_idx"])
        landed = g["landed"][tag]
        copied = sem("copied")
        cleared = sem("cleared")
        onehot_made = sem("onehot_made")
        sum_made = sem("sum_made")
        sum_taken = sem("sum_taken")
        chunks_begun = sem("chunks_begun")
        AHEAD = 2 * CHUNK
        block = ctx.enter_context(nc.Block())

        @block.gpsimd
        def _(gp):
            take_rows(gp, dram[("rel_table_f", "rel_table_b")[way]], rows, cur, idx, sum_made, AHEAD, landed, copied, FEAT)

        @block.tensor
        def _(pe):
            pe.sem_inc(sum_made, AHEAD)
            pe.wait_ge(cleared, 2)

            def chunk(k, i, half):
                pe.wait_ge(landed[half], (i + 1) * (16 * CHUNK))
                pe.sem_inc(chunks_begun, 1)
                with pe.Fori(0, TURNS) as turn:
                    for j in range(STEP):
                        if j % 2 == 0:
                            pe.wait_ge(onehot_made, k * (2 * TURNS + 2) + turn * 2 + (j // 2 + 1))
                        pe.wait_ge(sum_taken, k * CHUNK + turn * STEP + (j + 1))
                        pe.matmul(sum_ps[j][:, 0:FEAT + 1], onehot[:, j // 2, j % 2, :],
                                  rows[:, half, bass.ds(turn * STEP + j, 1), 0:FEAT + 1].rearrange("p a f -> p (a f)"),
                                  start=True, stop=True).then_inc(sum_made, 1)

            each_chunk(pe, chunk)

        @block.vector
        def _(v):
            v.sem_inc(sum_taken, STEP)
            v.memset(acc[:, :, :], 0.0).then_inc(cleared, 1)
            v.memset(rows[:, :, :, FEAT:FEAT + 1], 1.0).then_inc(cleared, 1)
            v.wait_ge(cleared, 2)
            regs = [v.alloc_register(f"{tag}_v_window{j}") for j in range(STEP)]

            def make(tile, sub):
                for jj in range(2):
                    i = v.tensor_scalar(onehot[:, sub, jj, :], cst[:, C_IOTA:C_IOTA + P],
                                        slot[:, bass.ds(tile + (2 * sub + jj), 1)], None, ALU.is_equal)
                i.then_inc(onehot_made, 1)

            def chunk(k, i, half):
                v.wait_ge(sum_made, k * CHUNK + AHEAD)
                for sub in range(2):
                    make(k * CHUNK, sub)
                with v.Fori(0, TURNS) as turn:
                    windows = tile_windows(v, regs, g["tile_win"], way, k * CHUNK + turn * STEP)
                    for sub in range(2):
                        v.wait_ge(sum_made, k * CHUNK + turn * STEP + (2 * sub + 2 + AHEAD))
                        make(k * CHUNK + turn * STEP + STEP, sub)
                        for j in (2 * sub, 2 * sub + 1):
                            v.wait_ge(sum_taken, k * CHUNK + turn * STEP + (j + STEP))
                            a = acc[:, bass.ds(windows[j], 1), 0:FEAT + 1].rearrange("p a f -> p (a f)")
                            v.tensor_tensor(a, a, sum_ps[j][:, 0:FEAT + 1], ALU.add).then_inc(sum_taken, 1)

            each_chunk(v, chunk)


def load_rows(sp, rows_sb, dram_rows, done):
    sp.dma_start(rows_sb, dram_rows.rearrange("(w p) f -> p w f", p=P)).then_inc(done, 16)


def finish(nc, tag, cst, kind, heads, d, dram, g, rows, acc, acc_b, nt, x_from, x_to, bias_name, out):
    D = FEAT // heads
    with ExitStack() as ctx:
        def sb(name, shape, dt=F32):
            return ctx.enter_context(nc.sbuf_tensor(f"{tag}_{name}", shape, dt))

        sem = phase_semaphores(nc, tag, ctx)

        flat = rows.rearrange("p a t f -> p (a t f)")
        x = flat[:, 0:WINDOWS * FEAT].rearrange("p (w f) -> p w f", f=FEAT)
        t = flat[:, WINDOWS * FEAT:2 * WINDOWS * FEAT].rearrange("p (w f) -> p w f", f=FEAT)
        bias = sb("bias", [P, 3, FEAT])
        loop_w = sb("loop_w", [P, 2, FEAT]) if kind == "relations" else None
        xt = sb("xt", [P, 2, 2, P]) if kind == "relations" else None
        den = sb("den", [P, 2, WINDOWS * 8])
        m = sb("m", [P, WINDOWS * 4])
        mean = sb("mean", [P, WINDOWS])
        var = sb("var", [P, WINDOWS])
        ps = [ctx.enter_context(nc.psum_tensor(f"{tag}_fin_ps{i}", [P, 512], F32)) for i in range(4)]
        x_in = sem("x_in")
        vec = sem("vec")
        to_scalar = sem("to_scalar")
        from_scalar = sem("from_scalar")
        turned = sem("turned")
        turned_out = sem("turned_out")
        looped = sem("looped")
        loop_taken = sem("loop_taken")
        y_ready = sem("y_ready")
        stored = sem("stored")
        block = ctx.enter_context(nc.Block())
        y = acc[:, :, 0:FEAT]
        y4 = lambda a: a.rearrange("p w (h d) -> p w h d", h=heads)
        norm = kind != "elu"

        @block.sync
        def _(sp):
            load_rows(sp, x, x_from, x_in)
            names = bias_name if isinstance(bias_name, tuple) else (bias_name,)
            for i in range(3):
                name = names[i] if i < len(names) else names[0]
                sp.dma_start(bias[:, i, :], d[name].rearrange("(a f) -> a f", a=1).to_broadcast([P, FEAT]))\
                    .then_inc(x_in, 16)
            if kind == "relations":
                sp.dma_start(loop_w[:, :, :], d["L0_gnn_loop_weight"].rearrange("(k p) n -> p k n", p=P)).then_inc(x_in, 16)
            sp.wait_ge(y_ready, 1)
            if out is None:
                sp.dma_start(x_to.rearrange("(w p) f -> p w f", p=P), y).then_inc(stored, 16)
                sp.wait_ge(stored, 16)
            else:
                whole = NODES // P
                sp.dma_start(out[0:whole * P, :].rearrange("(w p) f -> p w f", p=P), y[:, 0:whole, :]).then_inc(stored, 16)
                sp.dma_start(out[whole * P:NODES, :], y[0:NODES - whole * P, whole, :]).then_inc(stored, 16)
                sp.wait_ge(stored, 32)

        loads = 16 * (5 if kind == "relations" else 4)

        if kind == "relations":
            @block.tensor
            def _(pe):
                pe.wait_ge(x_in, loads)
                for w in range(WINDOWS):
                    if w >= 2:
                        pe.wait_ge(turned_out, w - 1)
                    for k in range(2):
                        mm = pe.transpose(ps[w % 2][:, k * P:(k + 1) * P], x[:, w, k * P:(k + 1) * P],
                                          cst[:, C_IDENT:C_IDENT + P])
                    mm.then_inc(turned, 1)
                    pe.wait_ge(turned_out, w + 1)
                    if w >= 2:
                        pe.wait_ge(loop_taken, w - 1)
                    for k in range(2):
                        mm = pe.matmul(ps[2 + w % 2][:, 0:FEAT], xt[:, w % 2, k, :], loop_w[:, k, :],
                                       start=(k == 0), stop=(k == 1))
                    mm.then_inc(looped, 1)

        @block.scalar
        def _(act):
            if kind == "relations":
                for w in range(WINDOWS):
                    act.wait_ge(turned, w + 1)
                    if w >= 2:
                        act.wait_ge(looped, w - 1)
                    act.copy(xt[:, w % 2, :, :].rearrange("p k e -> p (k e)"), ps[w % 2][:, 0:2 * P]).then_inc(turned_out, 1)
            n = 0
            if kind in ("self", "elu"):
                act.wait_ge(to_scalar, 1)
                act.activation(m[:, :], m[:, :], ACT.Exp).then_inc(from_scalar, 1)
                act.wait_ge(to_scalar, 2)
                act.activation(t, t, ACT.Exp).then_inc(from_scalar, 1)
                n = 2
            if norm:
                act.wait_ge(to_scalar, n + 1)
                act.activation(t, y, ACT.Square).then_inc(from_scalar, 1)
                act.wait_ge(to_scalar, n + 2)
                act.activation(var[:, :], var[:, :], ACT.Sqrt).then_inc(from_scalar, 1)

        @block.vector
        def _(v):
            s = Steps(vec)
            over_f = lambda a: a.unsqueeze(2).to_broadcast([P, WINDOWS, FEAT])
            over_w = lambda a: a.unsqueeze(1).to_broadcast([P, WINDOWS, FEAT])
            over_d = lambda a: a.rearrange("p (w h) -> p w h", h=heads).unsqueeze(3).to_broadcast([P, WINDOWS, heads, D])
            v.wait_ge(x_in, loads)
            if kind == "relations":
                for way, a in enumerate((acc, acc_b)):
                    c = den[:, way, 0:WINDOWS]
                    s.done(v.tensor_scalar(den[:, way, WINDOWS:2 * WINDOWS], a[:, :, FEAT], 1.0, None, ALU.min))
                    s.done(v.tensor_scalar(c, a[:, :, FEAT], 1.0, None, ALU.max))
                    s.settled(v)
                    s.done(v.reciprocal(c, c))
                    s.settled(v)
                    s.done(v.tensor_tensor(a[:, :, 0:FEAT], a[:, :, 0:FEAT], over_f(c), ALU.mult))
                    s.done(v.tensor_tensor(t, over_w(bias[:, way, :]), over_f(den[:, way, WINDOWS:2 * WINDOWS]), ALU.mult))
                    s.settled(v)
                    s.done(v.tensor_tensor(a[:, :, 0:FEAT], a[:, :, 0:FEAT], t, ALU.add))
                    s.settled(v)
                s.done(v.tensor_tensor(y, y, acc_b[:, :, 0:FEAT], ALU.add))
                s.settled(v)
                s.done(v.tensor_tensor(y, y, over_w(bias[:, 2, :]), ALU.add))
                s.settled(v)
                for w in range(WINDOWS):
                    v.wait_ge(looped, w + 1)
                    v.scalar_tensor_tensor(out=acc[:, w, 0:FEAT], in0=ps[2 + w % 2][:, 0:FEAT], scalar=2.0,
                                           in1=acc[:, w, 0:FEAT], op0=ALU.mult, op1=ALU.add).then_inc(loop_taken, 1)
                v.wait_ge(loop_taken, WINDOWS)
            else:
                c = den[:, 0, 0:WINDOWS * heads]
                c3 = c.rearrange("p (w h) -> p w h", h=heads)
                if kind in ("self", "elu"):
                    m3 = m[:, :].rearrange("p (w h) -> p w h", h=heads)
                    c1 = den[:, 1, 0:WINDOWS * heads].rearrange("p (w h) -> p w h", h=heads)
                    zs = nt[:, :, 268:272]
                    has = acc[:, :, 264:265].to_broadcast([P, WINDOWS, heads])
                    s.done(v.tensor_tensor(c1, has, zs, ALU.mult))
                    s.settled(v)
                    s.done(v.tensor_tensor(m3, c1, acc[:, :, 260:264], ALU.subtract))
                    s.settled(v)
                    v.sem_inc(to_scalar, 1)
                    v.wait_ge(from_scalar, 1)
                    s.done(v.tensor_tensor(c3, acc[:, :, 256:260], m3, ALU.add))
                    s.done(v.tensor_tensor(y4(t), y4(nt[:, :, 0:FEAT]), over_d(m[:, :]), ALU.mult))
                    s.settled(v)
                    s.done(v.tensor_tensor(y, y, t, ALU.add))
                    s.done(v.tensor_scalar(c, c, 1e-16, None, ALU.add))
                else:
                    s.done(v.tensor_scalar(c3, acc[:, :, 256:256 + heads], 1e-10, None, ALU.max))
                s.settled(v)
                s.done(v.reciprocal(c, c))
                s.settled(v)
                s.done(v.tensor_tensor(y4(y), y4(y), over_d(c), ALU.mult))
                s.settled(v)
                s.done(v.tensor_tensor(y, y, over_w(bias[:, 0, :]), ALU.add))
                s.settled(v)
            n = 0
            if kind in ("self", "elu"):
                s.done(v.tensor_scalar(t, y, 0.0, None, ALU.min))
                s.settled(v)
                v.sem_inc(to_scalar, 1)
                s.done(v.tensor_scalar(y, y, 0.0, -1.0, ALU.max, ALU.add))
                s.settled(v)
                v.wait_ge(from_scalar, 2)
                s.done(v.tensor_tensor(y, y, t, ALU.add))
                s.settled(v)
                n = 2
            if norm:
                s.done(v.tensor_tensor(y, y, x, ALU.add))
                s.settled(v)
                s.done(v.tensor_reduce(mean[:, :], y, AX.X, ALU.add))
                s.settled(v)
                s.done(v.tensor_scalar(mean[:, :], mean[:, :], 1.0 / FEAT, None, ALU.mult))
                s.settled(v)
                s.done(v.tensor_tensor(y, y, over_f(mean[:, :]), ALU.subtract))
                s.settled(v)
                v.sem_inc(to_scalar, 1)
                v.wait_ge(from_scalar, n + 1)
                s.done(v.tensor_reduce(var[:, :], t, AX.X, ALU.add))
                s.settled(v)
                s.done(v.tensor_scalar(var[:, :], var[:, :], 1.0 / FEAT, EPS, ALU.mult, ALU.add))
                s.settled(v)
                v.sem_inc(to_scalar, 1)
                v.wait_ge(from_scalar, n + 2)
                s.done(v.reciprocal(var[:, :], var[:, :]))
                s.settled(v)
                s.done(v.tensor_tensor(y, y, over_f(var[:, :]), ALU.mult))
                s.settled(v)
            v.sem_inc(y_ready, 1)


def project_nodes(nc, tag, cst, heads, self_edge, d, dram, nt, x_from, w_name, a_src_name, a_dst_name):
    D = FEAT // heads
    with ExitStack() as ctx:
        def sb(name, shape, dt=F32):
            return ctx.enter_context(nc.sbuf_tensor(f"{tag}_{name}", shape, dt))

        sem = phase_semaphores(nc, tag, ctx)

        w_sb = sb("w_sb", [P, 2, NTC])
        att = sb("att", [P, 2, FEAT])
        prod = sb("prod", [P, 2, 2, FEAT])
        xw = sb("xw", [P, 2, FEAT])
        xt = sb("xt", [P, 2, 2, P])
        own = sb("own", [P, WINDOWS, 4])
        xt_ps = [ctx.enter_context(nc.psum_tensor(f"{tag}_xt_ps{i}", [P, 512], F32)) for i in range(2)]
        h_ps = [ctx.enter_context(nc.psum_tensor(f"{tag}_h_ps{i}", [P, 512], F32)) for i in range(2)]
        w_in = sem("w_in")
        vec = sem("vec")
        w_ready = sem("w_ready")
        x_in = [sem(f"x_in{i}") for i in range(2)]
        xt_done = sem("xt_done")
        xt_taken = sem("xt_taken")
        h_done = sem("h_done")
        h_taken = sem("h_taken")
        stored = sem("stored")
        AHEAD = 2
        block = ctx.enter_context(nc.Block())

        @block.sync
        def _(sp):
            sp.dma_start(w_sb[:, :, 0:FEAT], d[w_name].rearrange("(k p) n -> p k n", p=P)).then_inc(w_in, 16)
            for i, name in enumerate((a_src_name, a_dst_name)):
                sp.dma_start(att[:, i, :], d[name].rearrange("(a f) -> a f", a=1).to_broadcast([P, FEAT])).then_inc(w_in, 16)

            def load(w, par):
                sp.wait_ge(xt_done, w + AHEAD - 1)
                sp.dma_start(xw[:, par, :], x_from[bass.ds(w * P, P), :]).then_inc(x_in[par], 16)

            def store(w, par):
                sp.wait_ge(h_taken, w + 1 + AHEAD)
                sp.dma_start(dram["nodes"][bass.ds(w * P, P), :],
                             nt[:, bass.ds(w, 1), 0:ROW].rearrange("p a f -> p (a f)")).then_inc(stored, 16)

            load(0, 0)
            with sp.Fori(0, WINDOWS // 2) as i:
                load(i * 2 + 1, 1)
                store(i * 2, 0)
                load(i * 2 + 2, 0)
                store(i * 2 + 1, 1)
            store(WINDOWS - 1, 0)
            sp.wait_ge(stored, 16 * WINDOWS)

        @block.tensor
        def _(pe):
            pe.sem_inc(xt_done, AHEAD)
            pe.sem_inc(h_done, AHEAD)
            pe.wait_ge(w_ready, 1)

            def body(w, par):
                pe.wait_ge(x_in[par], (w + (2 - par)) * 8)
                pe.wait_ge(xt_taken, w + 1)
                for k in range(2):
                    mm = pe.transpose(xt_ps[par][:, k * P:(k + 1) * P], xw[:, par, k * P:(k + 1) * P],
                                      cst[:, C_IDENT:C_IDENT + P])
                mm.then_inc(xt_done, 1)
                pe.wait_ge(xt_taken, w + 1 + AHEAD)
                pe.wait_ge(h_taken, w + 1)
                for k in range(2):
                    mm = pe.matmul(h_ps[par][:, 0:NTC], xt[:, par, k, :], w_sb[:, k, :], start=(k == 0), stop=(k == 1))
                mm.then_inc(h_done, 1)

            each_window(pe, body)

        @block.scalar
        def _(act):
            act.sem_inc(xt_taken, AHEAD)

            def body(w, par):
                act.wait_ge(xt_done, w + 1 + AHEAD)
                act.wait_ge(h_done, w + 1)
                act.copy(xt[:, par, :, :].rearrange("p k e -> p (k e)"), xt_ps[par][:, 0:2 * P]).then_inc(xt_taken, 1)

            each_window(act, body)

        @block.vector
        def _(v):
            s = Steps(vec)
            v.sem_inc(h_taken, AHEAD)
            s.done(v.memset(w_sb[:, :, FEAT:NTC], 0.0))
            v.wait_ge(w_in, 48)
            for i in range(2):
                for k in range(2):
                    s.done(v.tensor_tensor(prod[:, i, k, :], w_sb[:, k, 0:FEAT], att[:, i, :], ALU.mult))
            s.settled(v)
            for i in range(2):
                for k in range(2):
                    s.done(v.tensor_reduce(w_sb[:, k, FEAT + 8 * i:FEAT + 8 * i + heads],
                                           prod[:, i, k, :].rearrange("p (h d) -> p h d", h=heads), AX.X, ALU.add))
            s.settled(v)
            v.sem_inc(w_ready, 1)

            def body(w, par):
                v.wait_ge(h_done, w + 1 + AHEAD)
                v.tensor_scalar(nt[:, bass.ds(w, 1), :].rearrange("p a f -> p (a f)"), h_ps[par][:, 0:NTC],
                                1.0, None, ALU.mult).then_inc(h_taken, 1)

            each_window(v, body)
            if self_edge:
                v.wait_ge(h_taken, WINDOWS + AHEAD)
                s.done(v.tensor_tensor(own[:, :, :], nt[:, :, 256:260], nt[:, :, 264:268], ALU.add))
                s.settled(v)
                s.done(v.scalar_tensor_tensor(out=nt[:, :, 268:272], in0=own[:, :, :], scalar=0.2, in1=own[:, :, :],
                                              op0=ALU.mult, op1=ALU.max))
                s.settled(v)


def attention_edges(nc, tag, cst, kind, heads, d, dram, g, rows, acc, nt):
    D = FEAT // heads
    Q = heads * SCAN_ROWS
    own_edge = kind in ("self", "elu")
    with_attr = kind == "edge"
    width = ROW + 1 if own_edge else FEAT + heads
    CHAIN = 22 + (3 if own_edge else 0)
    with ExitStack() as ctx:
        def sb(name, shape, dt=F32):
            return ctx.enter_context(nc.sbuf_tensor(f"{tag}_{name}", shape, dt))

        sem = phase_semaphores(nc, tag, ctx)

        def bank(name):
            return ctx.enter_context(nc.psum_tensor(f"{tag}_{name}", [P, 512], F32))

        cur = sb("cur", [P, 2, CHUNK], I32)
        onehot = sb("onehot", [P, 2, 2, P])
        turned_sb = sb("turned_sb", [P, 2, 2, P])
        z = sb("z", [P, heads * CHUNK])
        top = sb("top", [P, heads * CHUNK])
        scan_a = sb("scan_a", [Q, SCAN_LEN])
        scan_b = sb("scan_b", [Q, SCAN_LEN])
        entry = sb("entry", [Q, 1])
        chain_in = sb("chain_in", [1, 2, heads, SCAN_ROWS + 1])
        chain = sb("chain", [1, 2, heads, SCAN_ROWS + 1])
        chain_row = sb("chain_row", [1, 2, Q])
        carried = sb("carried", [1, 2, heads])
        fall = sb("fall", [1, heads])
        first_hot = sb("first_hot", [P, P])
        first_col = sb("first_col", [P, 1])
        factor = sb("factor", [P, heads])
        turn_ps = [bank("turn_ps0"), bank("turn_ps1")]
        dst_ps = [bank("dst_ps0"), bank("dst_ps1")]
        attr_ps = [bank("attr_ps0"), bank("attr_ps1")]
        scan_ps = bank("scan_ps")
        small_ps = bank("small_ps")
        sum_ps = [turn_ps[0], turn_ps[1], attr_ps[0], attr_ps[1]]
        ROW_AT, COL_AT, FALL_AT, FIRST_AT = 352, 448, 456, 472
        if with_attr:
            attr = sb("attr", [4, 2, 2 * P])
            attr_w = sb("attr_w", [4, FEAT])
            encoded = sb("encoded", [P, 2, 2 * FEAT])
            prod = sb("prod", [P, 2, FEAT])
            part = sb("part", [P, 2, 8])
            dst_part = sb("dst_part", [P, CHUNK, 8])

        landed = g["landed"][tag]
        copied = sem("copied")
        cleared = sem("cleared")
        onehot_made = sem("onehot_made")
        turned = sem("turned")
        turned_out = sem("turned_out")
        dst_done = sem("dst_done")
        dst_taken = sem("dst_taken")
        weights_in = sem("weights_in")
        attr_in = [sem(f"attr_in{i}") for i in range(2)]
        enc_done = sem("enc_done")
        enc_out = sem("enc_out")
        enc_used = sem("enc_used")
        vec = sem("vec")
        z_ready = sem("z_ready")
        z_turned = sem("z_turned")
        ends_ready = sem("ends_ready")
        ends_row = sem("ends_row")
        entry_ready = sem("entry_ready")
        entry_col = sem("entry_col")
        first_ready = sem("first_ready")
        first_done = sem("first_done")
        first_out = sem("first_out")
        factor_ready = sem("factor_ready")
        top_ready = sem("top_ready")
        top_turned = sem("top_turned")
        less_top = sem("less_top")
        weights_made = sem("weights_made")
        hot_made = sem("hot_made")
        part_made = sem("part_made")
        weighted = sem("weighted")
        sum_made = sem("sum_made")
        sum_taken = sem("sum_taken")
        chunks_begun = sem("chunks_begun")
        AHEAD = 2 * CHUNK
        HOTS = 2 * TURNS + 2
        block = ctx.enter_context(nc.Block())

        if with_attr:
            @block.sync
            def _(sp):
                sp.dma_start(attr_w[0:3, :], d["L1_gnn_edge_W"]).then_inc(weights_in, 16)
                sp.dma_start(attr_w[3:4, :], d["L1_gnn_edge_b"].rearrange("(a f) -> a f", a=1)).then_inc(weights_in, 16)
                with sp.Fori(0, CHUNKS * TURNS) as turn:
                    for sub in range(2):
                        sp.wait_ge(enc_done, turn * 2 + (sub + 1))
                        sp.dma_start(attr[:, sub, :].rearrange("a (t e) -> a t e", e=P),
                                     dram["attrs"][:, bass.ds(turn * STEP + 2 * sub, 2), :]).then_inc(attr_in[sub], 16)

        @block.gpsimd
        def _(gp):
            take_rows(gp, dram["nodes"], rows, cur, g["src_idx"], sum_made, AHEAD, landed, copied, ROW)

        @block.tensor
        def _(pe):
            ident = cst[:, C_IDENT:C_IDENT + P]
            pe.sem_inc(sum_made, AHEAD)
            pe.sem_inc(turned, 2)
            pe.sem_inc(dst_done, STEP)
            if with_attr:
                pe.sem_inc(enc_done, 2)
                pe.wait_ge(weights_in, 32)
            pe.wait_ge(cleared, 1)
            regs = [pe.alloc_register(f"{tag}_pe_window{j}") for j in range(STEP)]

            def chunk(k, i, half):
                pe.wait_ge(sum_taken, k * CHUNK + STEP)
                if not with_attr:
                    pe.wait_ge(z_ready, k + 1)
                pe.sem_inc(chunks_begun, 1)
                with pe.Fori(0, TURNS) as turn:
                    windows = tile_windows(pe, regs, g["tile_win"], 0, k * CHUNK + turn * STEP)
                    tile = k * CHUNK + turn * STEP
                    pair = k * (2 * TURNS) + turn * 2
                    for sub in range(2):
                        pe.wait_ge(onehot_made, k * HOTS + turn * 2 + (sub + 1))
                        pe.wait_ge(turned_out, pair + (sub + 1))
                        for jj in range(2):
                            mm = pe.transpose(turn_ps[sub][:, jj * P:(jj + 1) * P], onehot[:, sub, jj, :], ident)
                        mm.then_inc(turned, 1)
                        if with_attr:
                            pe.wait_ge(attr_in[sub], (k * TURNS + turn + 1) * 16)
                            pe.wait_ge(enc_out, pair + (sub + 1))
                            for jj in range(2):
                                mm = pe.matmul(attr_ps[sub][:, jj * FEAT:(jj + 1) * FEAT],
                                               attr[:, sub, jj * P:(jj + 1) * P], attr_w[:, :], start=True, stop=True)
                            mm.then_inc(enc_done, 1)
                    for sub in range(2):
                        pe.wait_ge(turned_out, pair + (sub + 3))
                        for jj in range(2):
                            j = 2 * sub + jj
                            if with_attr:
                                pe.wait_ge(dst_taken, tile + (j + 3))
                                pe.matmul(dst_ps[jj][:, 0:NTC], turned_sb[:, sub, jj, :],
                                          nt[:, bass.ds(windows[j], 1), :].rearrange("p a f -> p (a f)"),
                                          start=True, stop=True).then_inc(dst_done, 1)
                            else:
                                pe.matmul(dst_ps[0][:, bass.ds((turn * STEP + j) * 8, 8)], turned_sb[:, sub, jj, :],
                                          nt[:, bass.ds(windows[j], 1), ROW:NTC].rearrange("p a f -> p (a f)"),
                                          start=True, stop=True).then_inc(dst_done, 1)
                pe.wait_ge(z_ready, k + 2)
                pe.sem_inc(chunks_begun, 1)
                for b in range(SCAN_TILES):
                    mm = pe.transpose(scan_ps[0:Q, b * P:(b + 1) * P], (top if own_edge else z)[:, b::SCAN_TILES], ident)
                mm.then_inc(z_turned, 1)
                pe.wait_ge(ends_ready, k * 2 + 1)
                pe.sem_inc(chunks_begun, 1)
                pe.matmul(small_ps[0:1, ROW_AT:ROW_AT + Q], scan_a[:, SCAN_LEN - 1:SCAN_LEN], ident[0:Q, 0:Q],
                          start=True, stop=True).then_inc(ends_row, 1)
                pe.wait_ge(entry_ready, k * 2 + 1)
                pe.sem_inc(chunks_begun, 1)
                pe.matmul(small_ps[0:Q, COL_AT:COL_AT + 1], chain_row[:, 0, :], cst[0:1, C_ONES:C_ONES + 1],
                          start=True, stop=True).then_inc(entry_col, 1)
                pe.wait_ge(first_ready, k + 1)
                pe.matmul(dst_ps[1][:, FIRST_AT:FIRST_AT + 1], first_hot[:, :], ident[:, 0:1],
                          start=True, stop=True).then_inc(first_done, 1)
                pe.wait_ge(ends_ready, k * 2 + 2)
                pe.sem_inc(chunks_begun, 1)
                pe.matmul(small_ps[0:1, ROW_AT:ROW_AT + Q], scan_b[:, 0:1], ident[0:Q, 0:Q],
                          start=True, stop=True).then_inc(ends_row, 1)
                pe.wait_ge(entry_ready, k * 2 + 2)
                pe.wait_ge(first_out, k + 1)
                pe.sem_inc(chunks_begun, 1)
                pe.matmul(dst_ps[1][:, FALL_AT:FALL_AT + heads], cst[0:1, C_ONES:C_ONES + P], fall[:, :],
                          start=True, stop=True)
                pe.matmul(small_ps[0:Q, COL_AT:COL_AT + 1], chain_row[:, 1, :], cst[0:1, C_ONES:C_ONES + 1],
                          start=True, stop=True).then_inc(entry_col, 1)
                pe.wait_ge(top_ready, k + 1)
                pe.sem_inc(chunks_begun, 1)
                for b in range(SCAN_TILES):
                    mm = pe.transpose(small_ps[:, b * Q:(b + 1) * Q], scan_b[:, b * P:(b + 1) * P], ident[0:Q, 0:Q])
                mm.then_inc(top_turned, 1)
                with pe.Fori(0, TURNS) as turn:
                    pe.wait_ge(weighted, k * TURNS + turn + 1)
                    for j in range(STEP):
                        if j % 2 == 0:
                            pe.wait_ge(hot_made, k * HOTS + turn * 2 + (j // 2 + 1))
                        pe.wait_ge(sum_taken, k * CHUNK + turn * STEP + (j + 1))
                        pe.matmul(sum_ps[j][:, 0:width], onehot[:, j // 2, j % 2, :],
                                  rows[:, half, bass.ds(turn * STEP + j, 1), 0:width].rearrange("p a f -> p (a f)"),
                                  start=True, stop=True).then_inc(sum_made, 1)

            each_chunk(pe, chunk)

        @block.scalar
        def _(act):
            act.sem_inc(turned_out, 2)
            if with_attr:
                act.sem_inc(enc_out, 2)

            def chunk(k, i, half):
                with act.Fori(0, TURNS) as turn:
                    pair = k * (2 * TURNS) + turn * 2
                    tile = k * CHUNK + turn * STEP
                    for sub in range(2):
                        act.wait_ge(turned, pair + (sub + 3))
                        act.wait_ge(dst_done, tile + (2 * sub + 2))
                        act.copy(turned_sb[:, sub, :, :].rearrange("p a n -> p (a n)"), turn_ps[sub][:, 0:2 * P])\
                            .then_inc(turned_out, 1)
                        if with_attr:
                            act.wait_ge(enc_done, pair + (sub + 3))
                            act.wait_ge(enc_used, tile + (2 * sub + 2))
                            act.activation(encoded[:, sub, :], attr_ps[sub][:, :], ACT.Relu).then_inc(enc_out, 1)
                act.wait_ge(first_done, k + 1)
                act.copy(first_col[:, :], dst_ps[1][:, FIRST_AT:FIRST_AT + 1]).then_inc(first_out, 1)
                act.wait_ge(first_out, k + 1)
                act.wait_ge(entry_col, k * 2 + 2)
                act.activation(factor[:, :], dst_ps[1][:, FALL_AT:FALL_AT + heads], ACT.Exp,
                               scale=first_col[:, 0:1]).then_inc(factor_ready, 1)
                act.wait_ge(less_top, k + 1)
                act.activation(rows[:, half, :, FEAT:FEAT + heads].rearrange("p t h -> p h t"),
                               z[:, :].rearrange("p (h t) -> p h t", h=heads), ACT.Exp).then_inc(weights_made, 1)

            each_chunk(act, chunk)

        @block.vector
        def _(v):
            v.sem_inc(sum_taken, STEP)
            v.sem_inc(z_ready, 1)
            if with_attr:
                v.sem_inc(dst_taken, STEP)
                v.sem_inc(enc_used, STEP)
            v.memset(acc[:, :, :], 0.0).then_inc(cleared, 1)
            v.memset(chain_in[:, :, :, :], -BIG).then_inc(cleared, 1)
            v.memset(carried[:, :, :], -BIG).then_inc(cleared, 1)
            v.wait_ge(cleared, 3)
            regs = [v.alloc_register(f"{tag}_v_window{j}") for j in range(STEP)]
            slot = g["dst_slot"]

            def hot(out, tile):
                return v.tensor_scalar(out, cst[:, C_IOTA:C_IOTA + P], slot[:, bass.ds(tile, 1)], None, ALU.is_equal)

            def make(tile, sub, made):
                for jj in range(2):
                    i = hot(onehot[:, sub, jj, :], tile + (2 * sub + jj))
                i.then_inc(made, 1)

            def chunk(k, i, half):
                s = Steps(vec, k * CHAIN)
                zh = z[:, :].rearrange("p (h t) -> p h t", h=heads)
                hr = lambda a: a.rearrange("p t h -> p h t")
                v.wait_ge(sum_made, k * CHUNK + AHEAD)
                for sub in range(2):
                    make(k * CHUNK, sub, onehot_made)
                with v.Fori(0, TURNS) as turn:
                    tile = k * CHUNK + turn * STEP
                    for sub in range(2):
                        v.wait_ge(turned, k * (2 * TURNS) + turn * 2 + (sub + 3))
                        make(tile + STEP, sub, onehot_made)
                    if with_attr:
                        for j in range(STEP):
                            v.wait_ge(dst_done, tile + (j + 1 + STEP))
                            v.wait_ge(enc_out, k * (2 * TURNS) + turn * 2 + (j // 2 + 3))
                            v.tensor_tensor(prod[:, j % 2, :], dst_ps[j % 2][:, 0:FEAT],
                                            encoded[:, j // 2, (j % 2) * FEAT:(j % 2 + 1) * FEAT], ALU.mult).then_inc(enc_used, 1)
                            v.wait_ge(enc_used, tile + (j + 1 + STEP))
                            v.tensor_reduce(part[:, j % 2, :], prod[:, j % 2, :].rearrange("p (h d) -> p h d", h=8),
                                            AX.X, ALU.add).then_inc(part_made, 1)
                            v.wait_ge(part_made, tile + (j + 1))
                            v.tensor_tensor(dst_part[:, bass.ds(turn * STEP + j, 1), :].rearrange("p a h -> p (a h)"),
                                            dst_ps[j % 2][:, ROW:NTC], part[:, j % 2, :], ALU.add).then_inc(dst_taken, 1)
                hot(first_hot[:, :], k * CHUNK).then_inc(first_ready, 1)
                v.wait_ge(landed[half], (i + 1) * (16 * CHUNK))
                if with_attr:
                    v.wait_ge(dst_taken, (k + 1) * CHUNK + STEP)
                    terms = dst_part[:, :, :]
                else:
                    v.wait_ge(dst_done, (k + 1) * CHUNK + STEP)
                    terms = dst_ps[0][:, 0:CHUNK * 8].rearrange("p (t h) -> p t h", h=8)
                s.done(v.tensor_tensor(zh, hr(rows[:, half, :, FEAT:FEAT + heads]), hr(terms[:, :, 0:heads]), ALU.add))
                s.settled(v)
                s.done(v.scalar_tensor_tensor(out=z[:, :], in0=z[:, :], scalar=0.2, in1=z[:, :], op0=ALU.mult, op1=ALU.max))
                s.settled(v)
                if own_edge:
                    s.done(v.tensor_tensor(top[:, :].rearrange("p (h t) -> p h t", h=heads), zh, hr(terms[:, :, 4:8]), ALU.max))
                    s.settled(v)
                v.sem_inc(z_ready, 1)
                breaks = g["break_f"][0:Q, bass.ds(k, 1), :].rearrange("q a e -> q (a e)")
                v.wait_ge(z_turned, k + 1)
                s.done(v.tensor_tensor_scan(scan_a[:, :], breaks, scan_ps[0:Q, :], -BIG, ALU.add, ALU.max))
                s.settled(v)
                v.sem_inc(ends_ready, 1)
                v.wait_ge(ends_row, k * 2 + 1)
                ends = small_ps[0:1, ROW_AT:ROW_AT + Q].rearrange("a (h c) -> a h c", h=heads)
                s.done(v.tensor_copy(chain_in[:, 0, :, 1:], ends))
                s.done(v.tensor_copy(chain_in[:, 0, :, 0], carried[:, half, :]))
                s.settled(v)
                s.done(v.tensor_tensor_scan(chain[:, 0, :, :].rearrange("a h c -> a (h c)"),
                                            g["chain_f"][:, bass.ds(k, 1), 0:heads, :].rearrange("a b h c -> a (b h c)"),
                                            chain_in[:, 0, :, :].rearrange("a h c -> a (h c)"), -BIG, ALU.add, ALU.max))
                s.settled(v)
                s.done(v.tensor_copy(chain_row[:, 0, :].rearrange("a (h c) -> a h c", h=heads), chain[:, 0, :, 0:SCAN_ROWS]))
                s.done(v.tensor_copy(carried[:, 1 - half, :], chain[:, 0, :, SCAN_ROWS]))
                s.settled(v)
                v.sem_inc(entry_ready, 1)
                v.wait_ge(entry_col, k * 2 + 1)
                s.done(v.tensor_copy(entry[:, :], small_ps[0:Q, COL_AT:COL_AT + 1]))
                s.settled(v)
                s.done(v.tensor_tensor_scan(scan_a[:, :], breaks, scan_ps[0:Q, :], entry[:, :], ALU.add, ALU.max))
                s.settled(v)
                breaks = g["break_b"][0:Q, bass.ds(k, 1), :].rearrange("q a e -> q (a e)")
                s.done(v.tensor_tensor_scan(scan_b[:, ::-1], breaks, scan_a[:, ::-1], -BIG, ALU.add, ALU.max))
                s.settled(v)
                v.sem_inc(ends_ready, 1)
                v.wait_ge(ends_row, k * 2 + 2)
                s.done(v.tensor_copy(chain_in[:, 1, :, 0:SCAN_ROWS], ends))
                s.settled(v)
                s.done(v.tensor_tensor_scan(chain[:, 1, :, :].rearrange("a h c -> a (h c)")[:, ::-1],
                                            g["chain_b"][:, bass.ds(k, 1), 0:heads, :].rearrange("a b h c -> a (b h c)"),
                                            chain_in[:, 1, :, :].rearrange("a h c -> a (h c)")[:, ::-1], -BIG, ALU.add, ALU.max))
                s.settled(v)
                s.done(v.tensor_copy(chain_row[:, 1, :].rearrange("a (h c) -> a h c", h=heads), chain[:, 1, :, 1:]))
                s.done(v.tensor_tensor(fall[:, :], carried[:, half, :], chain[:, 1, :, 0], ALU.subtract))
                s.settled(v)
                s.done(v.tensor_scalar(fall[:, :], fall[:, :], g["goes_on"][:, bass.ds(k, 1)], None, ALU.mult))
                s.settled(v)
                v.sem_inc(entry_ready, 1)
                v.wait_ge(entry_col, k * 2 + 2)
                s.done(v.tensor_copy(entry[:, :], small_ps[0:Q, COL_AT:COL_AT + 1]))
                s.settled(v)
                s.done(v.tensor_tensor_scan(scan_b[:, ::-1], breaks, scan_a[:, ::-1], entry[:, :], ALU.add, ALU.max))
                s.settled(v)
                v.sem_inc(top_ready, 1)
                v.reg_load(regs[0], g["tile_win"][0:1, 0, bass.ds(k * CHUNK, 1)])
                window = v.snap(regs[0], min_val=0, max_val=WINDOWS - 1)
                v.wait_ge(factor_ready, k + 1)
                v.wait_ge(sum_taken, k * CHUNK + STEP)
                a = acc[:, bass.ds(window, 1), :].rearrange("p a f -> p (a f)")
                s.done(v.tensor_tensor(a[:, 0:FEAT].rearrange("p (h d) -> p h d", h=heads),
                                       a[:, 0:FEAT].rearrange("p (h d) -> p h d", h=heads),
                                       factor[:, :].unsqueeze(2).to_broadcast([P, heads, D]), ALU.mult))
                s.done(v.tensor_tensor(a[:, FEAT:FEAT + heads], a[:, FEAT:FEAT + heads], factor[:, :], ALU.mult))
                s.settled(v)
                v.wait_ge(top_turned, k + 1)
                s.done(v.tensor_copy(top[:, :].rearrange("p (q b) -> p b q", b=SCAN_TILES),
                                     small_ps[:, 0:SCAN_TILES * Q].rearrange("p (b q) -> p b q", b=SCAN_TILES)))
                s.settled(v)
                s.done(v.tensor_tensor(z[:, :], z[:, :], top[:, :], ALU.subtract))
                s.settled(v)
                v.sem_inc(less_top, 1)
                if own_edge:
                    lasts = g["last"][:, bass.ds(k * CHUNK, CHUNK)]
                    s.done(v.tensor_tensor(hr(rows[:, half, :, 260:264]), top[:, :].rearrange("p (h t) -> p h t", h=heads),
                                           lasts.unsqueeze(1).to_broadcast([P, heads, CHUNK]), ALU.mult))
                    s.done(v.tensor_scalar(rows[:, half, :, ROW:ROW + 1].rearrange("p t a -> p (t a)"), lasts, 1.0, None, ALU.mult))
                    s.settled(v)
                assert s.n == CHAIN, s.n
                v.wait_ge(weights_made, k + 1)
                for sub in range(2):
                    make(k * CHUNK, sub, hot_made)
                with v.Fori(0, TURNS) as turn:
                    windows = tile_windows(v, regs, g["tile_win"], 0, k * CHUNK + turn * STEP)
                    tile = k * CHUNK + turn * STEP
                    r = rows[:, half, bass.ds(turn * STEP, STEP), :]
                    v.tensor_tensor(r[:, :, 0:FEAT].rearrange("p t (h d) -> p t h d", h=heads),
                                    r[:, :, 0:FEAT].rearrange("p t (h d) -> p t h d", h=heads),
                                    r[:, :, FEAT:FEAT + heads].unsqueeze(3).to_broadcast([P, STEP, heads, D]),
                                    ALU.mult).then_inc(weighted, 1)
                    for sub in range(2):
                        v.wait_ge(sum_made, tile + (2 * sub + 2 + AHEAD))
                        make(tile + STEP, sub, hot_made)
                        for j in (2 * sub, 2 * sub + 1):
                            v.wait_ge(sum_taken, tile + (j + STEP))
                            a = acc[:, bass.ds(windows[j], 1), 0:width].rearrange("p a f -> p (a f)")
                            v.tensor_tensor(a, a, sum_ps[j][:, 0:width], ALU.add).then_inc(sum_taken, 1)

            each_chunk(v, chunk)


def build(nc, d, out, layers=5):
    dram = {}
    for name, shape, dt in (("src_win", [EDGES], F32), ("places", [EDGES], I32), ("records", [TILES * P, 2], I32),
                            ("keys", [TILES + 2, P], F32), ("attrs", [4, TILES, P], F32), ("tile_win", [2, TILES], I32),
                            ("breaks", [2, SEG_ROWS, SCAN_LEN], BF16), ("rel_table_f", [NODES_PAD * RELS, FEAT], F32),
                            ("rel_table_b", [NODES_PAD * RELS, FEAT], F32),
                            ("nodes", [NODES_PAD, ROW], F32), ("x1", [NODES_PAD, FEAT], F32),
                            ("x2", [NODES_PAD, FEAT], F32)):
        dram[name] = nc.dram_tensor(f"dram_{name}", shape, dt, kind="Internal").ap()
    with ExitStack() as ctx:
        def sb(name, shape, dt=F32):
            return ctx.enter_context(nc.sbuf_tensor(name, shape, dt))

        cst = sb("cst", [P, C_COLS])
        g = {}
        g["landed"] = {tag: [ctx.enter_context(nc.semaphore(f"{tag}_landed{i}")) for i in range(2)]
                       for tag in ("group", "fwd", "bwd", "att0", "att1", "att2", "att3")}
        g["src_idx"] = sb("src_idx", [P, TILES], I32)
        g["dst_slot"] = sb("dst_slot", [P, TILES + STEP])
        g["tile_win"] = sb("tile_win", [1, 2, TILES], I32)
        with ExitStack() as relations:
            for name, shape, dt in (("fwd_idx", [P, TILES], I32), ("bwd_idx", [P, TILES], I32),
                                    ("src_slot", [P, TILES + STEP], F32), ("tile_win4", [QUARTERS, 2, QT], I32)):
                g[name] = relations.enter_context(nc.sbuf_tensor(name, shape, dt))
            group_edges(nc, "group", cst, d, dram, g)
            project_relations(nc, "rel", cst, d, dram)
            rows = relations.enter_context(nc.sbuf_tensor("rel_rows", [P, 2, CHUNK, COLS], F32))
            acc = relations.enter_context(nc.sbuf_tensor("acc_f", [P, WINDOWS, COLS], F32))
            acc_b = relations.enter_context(nc.sbuf_tensor("acc_b", [P, WINDOWS, COLS], F32))
            relation_edges(nc, 'fwd', cst, dram, g, rows, 0, acc)
            relation_edges(nc, 'bwd', cst, dram, g, rows, 1, acc_b)
            finish(nc, "fin0", cst, "relations", 1, d, dram, g, rows, acc, acc_b, None, d["x_pad"], dram["x1"],
                   ("L0_gnn_forward_bias", "L0_gnn_backward_bias", "L0_gnn_self_bias"), out if layers == 1 else None)
        g["break_f"] = sb("break_f", [8 * SCAN_ROWS, CHUNKS, SCAN_LEN], BF16)
        g["break_b"] = sb("break_b", [8 * SCAN_ROWS, CHUNKS, SCAN_LEN], BF16)
        g["chain_f"] = sb("chain_f", [1, CHUNKS, 8, SCAN_ROWS + 1])
        g["chain_b"] = sb("chain_b", [1, CHUNKS, 8, SCAN_ROWS + 1])
        g["goes_on"] = sb("goes_on", [1, CHUNKS])
        g["last"] = sb("last", [P, TILES])
        if layers > 1:
            scan_tables(nc, 'scan', cst, dram, g)
        for n, (kind, heads, x_from, rest, x_to, w, a, b, bias) in enumerate((
                ("edge", 8, "x1", "x1", "x2", "L1_gnn_W", "L1_gnn_a_src", "L1_gnn_a_dst", "L1_gnn_bias"),
                ("elu", 4, "x2", "x2", "x1", "L2_gnn_W1", "L2_gnn_att_src1", "L2_gnn_att_dst1", "L2_gnn_b1"),
                ("self", 4, "x1", "x2", "x1", "L2_gnn_W2", "L2_gnn_att_src2", "L2_gnn_att_dst2", "L2_gnn_b2"),
                ("plain", 8, "x1", "x1", "x2", "L3_gnn_W", "L3_gnn_a_src", "L3_gnn_a_dst", "L3_gnn_bias"))):
            if n + 2 > layers:
                break
            with ExitStack() as layer:
                nt = layer.enter_context(nc.sbuf_tensor(f"nt{n}", [P, WINDOWS, NTC], F32))
                project_nodes(nc, f'nodes{n}', cst, heads, kind in ("self", "elu"), d, dram, nt, dram[x_from], w, a, b)
                acc = layer.enter_context(nc.sbuf_tensor(f"acc{n}", [P, WINDOWS, COLS], F32))
                rows = layer.enter_context(nc.sbuf_tensor(f"rows{n}", [P, 2, CHUNK, COLS], F32))
                attention_edges(nc, f'att{n}', cst, kind, heads, d, dram, g, rows, acc, nt)
                finish(nc, f'fin{n + 1}', cst, kind, heads, d, dram, g, rows, acc, None, nt, dram[rest], dram[x_to], bias,
                       out if n + 2 == layers else None)


LAYERS = 5


def constants():
    import numpy as np
    c = np.zeros((P, C_COLS), np.float32)
    p = np.arange(EP)
    c[:, C_IDENT:C_IDENT + P] = np.eye(P)
    c[:, C_IOTA:C_IOTA + P] = np.arange(P)
    c[:, C_ONES:C_ONES + P] = 1
    c[:EP, C_BEFORE:C_BEFORE + EP] = (p[:, None] // PARTS == p // PARTS) & (p[:, None] < p)
    c[:EP, C_WINOH:C_WINOH + WINDOWS] = p[:, None] // PARTS == np.arange(WINDOWS)
    c[:EP, C_PART:C_PART + PARTS] = p[:, None] % PARTS == np.arange(PARTS)
    c[:EP, C_WIN] = p // PARTS
    c[:QT, C_TILE:C_TILE + QUARTERS] = np.arange(QT)[:, None] + QT * np.arange(QUARTERS)
    return c


def kernel(**inputs):
    import numpy as _np
    import concourse.bacc as _bacc
    from concourse import mybir as _mybir
    from concourse.bass_utils import run_bass_kernel_spmd as _run

    def padded(a, value):
        return _np.concatenate([a, _np.full((P,) + a.shape[1:], value, a.dtype)])

    inputs = {name: _np.asarray(a) for name, a in inputs.items()}
    given = {name: inputs[name] for name in (
        "src", "dst", "edge_type_16", "L0_gnn_Wf", "L0_gnn_Wb", "L0_gnn_loop_weight", "L0_gnn_forward_bias",
        "L0_gnn_backward_bias", "L0_gnn_self_bias", "L1_gnn_edge_b", "L1_gnn_bias", "L2_gnn_W1", "L2_gnn_b1",
        "L2_gnn_W2", "L2_gnn_b2", "L3_gnn_bias")}
    for name in ("L1_gnn_a_src", "L1_gnn_a_dst", "L2_gnn_att_src1", "L2_gnn_att_dst1", "L2_gnn_att_src2",
                 "L2_gnn_att_dst2", "L3_gnn_a_src", "L3_gnn_a_dst"):
        given[name] = inputs[name].reshape(-1)
    for name in ("L1_gnn_W", "L1_gnn_edge_W", "L3_gnn_W"):
        given[name] = inputs[name].T
    x = inputs["x"]
    given["x_pad"] = _np.concatenate([x, _np.zeros((NODES_PAD - NODES, FEAT), x.dtype)])
    given["src_pad"] = padded(inputs["src"], 0)
    given["dst_pad"] = padded(inputs["dst"], int(FAR))
    given["type_pad"] = padded(inputs["edge_type_16"], 0)
    for i in range(3):
        given[f"attr{i}"] = padded(inputs["edge_attr_3"][:, i], 0)
    given["consts"] = constants()

    nc = _bacc.Bacc("TRN2", target_bir_lowering=False, num_devices=1)
    arrays, d = {}, {}
    for name, a in given.items():
        a = _np.ascontiguousarray(a)
        arrays[f"in_{name}"] = a
        d[name] = nc.dram_tensor(f"in_{name}", a.shape, _mybir.dt.from_np(a.dtype), kind="ExternalInput").ap()
    out = nc.dram_tensor("out", (NODES, FEAT), F32, kind="ExternalOutput").ap()
    build(nc, d, out, LAYERS)
    r = _run(nc, [arrays], core_ids=[0])
    return r.results[0]["out"]
```

```python
from contextlib import ExitStack

import concourse.bass as bass
from concourse import mybir

ALU = mybir.AluOpType
ACT = mybir.ActivationFunctionType
AX = mybir.AxisListType
F32 = mybir.dt.float32
BF16 = mybir.dt.bfloat16
I32 = mybir.dt.int32

P = 128
NODES = 3125
EDGES = 53125
FEAT = 256
RELS = 16
WINDOWS = -(-NODES // P)
NODES_PAD = WINDOWS * P
CHUNK = 44
CHUNKS = 10
TILES = CHUNK * CHUNKS
assert EDGES // P + WINDOWS <= TILES
SCAN_ROWS = 11
SCAN_TILES = CHUNK // SCAN_ROWS
SCAN_LEN = SCAN_TILES * P
EP, EJ = 125, 425
assert EP * EJ == EDGES
PARTS = EP // WINDOWS
PART_LEN = EDGES // PARTS
QUARTERS = 4
QT = TILES // QUARTERS
SEG_ROWS = CHUNKS * SCAN_ROWS
ROW = 264
COLS = 266
NTC = 272
STEP = 4
TURNS = CHUNK // STEP
BIG = 1e30
EPS = 1e-5
FAR = float(1 << 20)

C_IDENT, C_IOTA, C_ONES, C_BEFORE, C_WINOH, C_PART, C_WIN, C_TILE, C_ROW = 0, 128, 256, 384, 509, 534, 539, 540, 544
C_COLS = 545


class Steps:

    def __init__(self, sem, base=0):
        self.sem, self.base, self.n = sem, base, 0

    def done(self, instruction):
        instruction.then_inc(self.sem, 1)
        self.n += 1

    def settled(self, engine):
        if self.n or not isinstance(self.base, int):
            engine.wait_ge(self.sem, self.base + self.n)


def phase_semaphores(nc, tag, ctx):
    sems = []

    def sem(name):
        sems.append(nc.alloc_semaphore(f"{tag}_{name}"))
        return sems[-1]

    ctx.callback(nc.all_engine_barrier)
    ctx.callback(nc.clear_and_free_semaphores, sems)
    return sem


def each_window(engine, body):
    with engine.Fori(0, WINDOWS // 2) as i:
        body(i * 2, 0)
        body(i * 2 + 1, 1)
    body(WINDOWS - 1, 0)


def group_edges(nc, tag, cst, d, dram, g):
    with ExitStack() as ctx:
        def sb(name, shape, dt=F32):
            return ctx.enter_context(nc.sbuf_tensor(f"{tag}_{name}", shape, dt))

        sem = phase_semaphores(nc, tag, ctx)

        rows_ps = ctx.enter_context(nc.psum_tensor(f"{tag}_rows_ps", [P, 512], F32))
        parts_ps = ctx.enter_context(nc.psum_tensor(f"{tag}_parts_ps", [P, 512], F32))
        pos_ps = [ctx.enter_context(nc.psum_tensor(f"{tag}_pos_ps{i}", [P, 512], F32)) for i in range(2)]
        lane_ps = [ctx.enter_context(nc.psum_tensor(f"{tag}_lane_ps{i}", [P, 512], F32)) for i in range(2)]

        src_e = sb("src_e", [EP, EJ], I32)
        dst_e = sb("dst_e", [EP, EJ], I32)
        typ_e = sb("typ_e", [EP, EJ], I32)
        flt_e = sb("flt_e", [EP, EJ])
        cmp_e = sb("cmp_e", [EP, EJ])
        win_i = sb("win_i", [EP, EJ], I32)
        win_f = sb("win_f", [EP, EJ])
        below = sb("below", [EP, WINDOWS + 1])
        hit = sb("hit", [EP, PART_LEN])
        rank = sb("rank", [EP, PART_LEN])
        place = sb("place", [PARTS, PART_LEN], I32)
        total = sb("total", [EP, 1])
        total_b = sb("total_b", [EP, P])
        base = sb("base", [EP, 1])
        pick = sb("pick", [EP, WINDOWS])
        zeros = sb("zeros", [P, WINDOWS])
        start = sb("start", [P, 2, WINDOWS + 1])
        n_i = sb("n_i", [P, 2, WINDOWS], I32)
        n_t = sb("n_t", [P, 2, WINDOWS])
        last_t = sb("last_t", [P, 2, WINDOWS])
        first_t = sb("first_t", [P, 2, WINDOWS])
        shift = sb("shift", [P, WINDOWS])
        jump = sb("jump", [P, WINDOWS])
        ge = sb("ge", [P, WINDOWS])
        gej = sb("gej", [P, WINDOWS])
        win_t = sb("win_t", [QT, 2, QUARTERS])
        win128, record, pos_i = g["win128"], g["record"], g["pos_i"]
        off_f = sb("off_f", [QT, QUARTERS])
        off_i = sb("off_i", [QT, QUARTERS], I32)
        pad = sb("pad", [P, TILES, 2], I32)
        r_dst = sb("r_dst", [QT, QUARTERS, P], I32)
        r_src = sb("r_src", [QT, QUARTERS, P], I32)
        r_typ = sb("r_typ", [QT, QUARTERS, P], I32)
        r_att = sb("r_att", [QT, 3, QUARTERS, P])
        r_one = sb("r_one", [QT, P])
        f_dst = sb("f_dst", [QT, QUARTERS, P])
        f_src = sb("f_src", [QT, QUARTERS, P])
        f_idx = sb("f_idx", [QT, QUARTERS, P])
        f_loc = sb("f_loc", [QT, QUARTERS, P])
        f_val = sb("f_val", [QT, QUARTERS, P])
        f_key = sb("f_key", [QT, QUARTERS, P])
        edge_key = sb("edge_key", [1, P])

        loaded = sem("loaded")
        windows_out = sem("windows_out")
        windows_in = sem("windows_in")
        pad_out = sem("pad_out")
        places_out = sem("places_out")
        places_in = sem("places_in")
        blocks_in = g["landed"][tag][0]
        keys_out = sem("keys_out")
        rows_in = sem("rows_in")
        vec = sem("vec")
        src_windows = sem("src_windows")
        records_made = sem("records_made")
        pad_made = sem("pad_made")
        below_made = sem("below_made")
        total_made = sem("total_made")
        counts_done = sem("counts_done")
        parts_done = sem("parts_done")
        rank_made = sem("rank_made")
        sums_done = sem("sums_done")
        sums_taken = sem("sums_taken")
        offsets_made = sem("offsets_made")
        keys_made = sem("keys_made")
        lanes_ready = sem("lanes_ready")
        lanes_done = sem("lanes_done")
        lanes_taken = sem("lanes_taken")
        pieces = [(a, min(512, PART_LEN - a)) for a in range(0, PART_LEN, 512)]

        block = ctx.enter_context(nc.Block())

        @block.sync
        def _(sp):
            sp.dma_start(cst[:, :], d["consts"]).then_inc(loaded, 16)
            sp.dma_start(src_e[:, :], d["src"].rearrange("(p j) -> p j", p=EP)).then_inc(loaded, 16)
            sp.dma_start(dst_e[:, :], d["dst"].rearrange("(p j) -> p j", p=EP)).then_inc(loaded, 16)
            sp.dma_start(typ_e[:, :], d["edge_type_16"].rearrange("(p j) -> p j", p=EP)).then_inc(loaded, 16)
            sp.wait_ge(src_windows, 1)
            sp.dma_start(dram["src_win"].rearrange("(p j) -> p j", p=EP), win_f[:, :]).then_inc(windows_out, 16)
            sp.wait_ge(windows_out, 16)
            for w in range(WINDOWS):
                sp.dma_start(hit[w * PARTS:(w + 1) * PARTS, :],
                             dram["src_win"].rearrange("(c j) -> c j", c=PARTS)).then_inc(windows_in, 16)
            sp.wait_ge(pad_made, 2)
            sp.dma_start(dram["records"].rearrange("(p t) c -> p t c", p=P), pad[:, :, :]).then_inc(pad_out, 16)
            sp.wait_ge(keys_made, 1)
            for q in range(QUARTERS):
                sp.dma_start(dram["keys"][1 + q * QT:1 + (q + 1) * QT, :], f_key[:, q, :]).then_inc(keys_out, 16)
                sp.dma_start(dram["slots"][q * QT:(q + 1) * QT, :], f_loc[:, q, :]).then_inc(keys_out, 16)
            for row in (0, TILES + 1):
                sp.dma_start(dram["keys"][row:row + 1, :], edge_key[:, :]).then_inc(keys_out, 16)
            sp.wait_ge(blocks_in, 16 * 6 * QUARTERS)
            for a in range(4):
                for q in range(QUARTERS):
                    sp.dma_start(dram["attrs"][a, q * QT:(q + 1) * QT, :],
                                 r_att[:, a, q, :] if a < 3 else r_one[:, :]).then_inc(keys_out, 16)
            sp.wait_ge(sums_taken, len(pieces))
            sp.dma_start(dram["places"].rearrange("(c j) -> c j", c=PARTS), place[:, :]).then_inc(places_out, 16)
            sp.wait_ge(places_out, 16)
            sp.dma_start(pos_i[:, :], dram["places"].rearrange("(p j) -> p j", p=EP)).then_inc(places_in, 16)
            sp.wait_ge(lanes_taken, 4)
            for way in range(2):
                sp.dma_start(dram["tile_win"][way].rearrange("(q p) -> q p", q=QUARTERS),
                             g["tile_win4"][:, way, :]).then_inc(rows_in, 16)
            sp.wait_ge(rows_in, 32)
            sp.dma_start(g["tile_win"][:, :, :], dram["tile_win"].rearrange("(a w) t -> a w t", a=1)).then_inc(rows_in, 16)
            sp.wait_ge(keys_out, 16 * (2 * QUARTERS + 2 + 4 * QUARTERS))
            sp.wait_ge(rows_in, 48)
            sp.wait_ge(pad_out, 16)
            sp.wait_ge(places_in, 16)

        @block.gpsimd
        def _(gp):
            gp.wait_ge(offsets_made, 1)
            for q in range(QUARTERS):
                at = bass.IndirectOffsetOnAxis(ap=off_i[:, q:q + 1], axis=1)
                for flat, to in ((d["dst_pad"], r_dst[:, q, :]), (d["src_pad"], r_src[:, q, :]),
                                 (d["type_pad"], r_typ[:, q, :]), (d["attr0"], r_att[:, 0, q, :]),
                                 (d["attr1"], r_att[:, 1, q, :]), (d["attr2"], r_att[:, 2, q, :])):
                    gp.indirect_dma_start(out=to, out_offset=None, in_=flat.rearrange("(a b) -> a b", a=1),
                                          in_offset=at).then_inc(blocks_in, 16)

        @block.tensor
        def _(pe):
            ones = cst[0:EP, C_ONES:C_ONES + P]
            pe.wait_ge(below_made, 1)
            pe.matmul(rows_ps[:, 0:WINDOWS + 1], ones, below[:, :], start=True, stop=True).then_inc(counts_done, 1)
            pe.wait_ge(total_made, 1)
            pe.matmul(rows_ps[:, 64:64 + WINDOWS], total_b[:, :], cst[0:EP, C_WINOH:C_WINOH + WINDOWS],
                      start=True, stop=True)
            pe.matmul(rows_ps[0:EP, 128:129], cst[0:EP, C_BEFORE:C_BEFORE + EP], total[:, :],
                      start=True, stop=True).then_inc(parts_done, 1)

            def lanes(n, views):
                pe.wait_ge(lanes_ready, n + 1)
                if n >= 2:
                    pe.wait_ge(lanes_taken, n - 1)
                for q, v in enumerate(views):
                    k, m = v.shape[0], v.shape[1]
                    mm = pe.transpose(lane_ps[n % 2][0:m, q * QT:q * QT + k], v, cst[0:k, C_IDENT:C_IDENT + k])
                mm.then_inc(lanes_done, 1)

            lanes(0, [win_t[:, 0, :]])
            lanes(1, [f_loc[:, q, :] for q in range(QUARTERS)])
            lanes(2, [f_src[:, q, :] for q in range(QUARTERS)])
            lanes(3, [win_t[:, 1, :]])
            lanes(4, [f_idx[:, q, :] for q in range(QUARTERS)])
            pe.wait_ge(rank_made, 1)
            for n, (a, m) in enumerate(pieces):
                if n >= 2:
                    pe.wait_ge(sums_taken, n - 1)
                pe.matmul(pos_ps[n % 2][0:PARTS, 0:m], cst[0:EP, C_PART:C_PART + PARTS], rank[:, a:a + m],
                          start=True, stop=True).then_inc(sums_done, 1)

        @block.scalar
        def _(act):
            for n, (a, m) in enumerate(pieces):
                act.wait_ge(sums_done, n + 1)
                act.copy(place[:, a:a + m], pos_ps[n % 2][0:PARTS, 0:m]).then_inc(sums_taken, 1)

        @block.vector
        def _(v):
            s = Steps(vec)
            v.memset(zeros[:, :], 0.0).then_inc(vec, 1)
            s.n += 1
            s.done(v.memset(below[:, 0:1], 0.0))
            s.done(v.memset(below[:, WINDOWS:WINDOWS + 1], float(EJ)))
            s.done(v.memset(edge_key[:, :], -2.0))
            s.done(v.memset(g["dst_slot"][:, TILES:], -1.0))
            s.done(v.memset(g["src_slot"][:, TILES:], -1.0))
            s.done(v.memset(r_one[:, :], 1.0))
            v.memset(pad[:, :, 0], -1).then_inc(pad_made, 1)
            v.memset(pad[:, :, 1], 0).then_inc(pad_made, 1)
            v.wait_ge(loaded, 64)
            s.done(v.tensor_scalar(win_i[:, :], src_e[:, :], 7, None, ALU.logical_shift_right))
            s.settled(v)
            v.tensor_copy(win_f[:, :], win_i[:, :]).then_inc(src_windows, 1)
            v.tensor_copy(record[:, :, 0], src_e[:, :]).then_inc(records_made, 1)
            v.scalar_tensor_tensor(out=record[:, :, 1], in0=dst_e[:, :], scalar=float(RELS), in1=typ_e[:, :],
                                   op0=ALU.mult, op1=ALU.add).then_inc(records_made, 1)
            s.done(v.tensor_copy(flt_e[:, :], dst_e[:, :]))
            s.settled(v)
            for w in range(1, WINDOWS):
                s.done(v.tensor_scalar(cmp_e[:, :], flt_e[:, :], float(w * P), None, ALU.is_lt))
                s.settled(v)
                s.done(v.tensor_reduce(below[:, w:w + 1], cmp_e[:, :], AX.X, ALU.add))
                s.settled(v)
            v.sem_inc(below_made, 1)

            def tiles_of(way):
                n = start[:, way, 1:] if way == 0 else start[:, way, 0:WINDOWS]
                if way == 0:
                    s.done(v.tensor_tensor(n_t[:, way, :], n, start[:, way, 0:WINDOWS], ALU.subtract))
                    s.settled(v)
                    n = n_t[:, way, :]
                s.done(v.tensor_scalar(n_i[:, way, :], n, float(P - 1), None, ALU.add))
                s.settled(v)
                s.done(v.tensor_scalar(n_i[:, way, :], n_i[:, way, :], 7, None, ALU.logical_shift_right))
                s.settled(v)
                s.done(v.tensor_scalar(n_t[:, way, :], n_i[:, way, :], 1.0, None, ALU.max))
                s.settled(v)
                s.done(v.tensor_tensor_scan(last_t[:, way, :], zeros[:, :], n_t[:, way, :], 0.0, ALU.add, ALU.add))
                s.settled(v)
                s.done(v.tensor_tensor(first_t[:, way, :], last_t[:, way, :], n_t[:, way, :], ALU.subtract))
                s.settled(v)

            def window_of_tiles(way):
                for q in range(QUARTERS):
                    tile = cst[0:QT, C_TILE + q:C_TILE + q + 1]
                    s.done(v.tensor_scalar(ge[0:QT, :], first_t[0:QT, way, :], tile, None, ALU.is_le))
                    s.settled(v)
                    s.done(v.tensor_reduce(win_t[:, way, q:q + 1], ge[0:QT, :], AX.X, ALU.add))
                    if way == 0:
                        s.done(v.tensor_tensor(gej[0:QT, :], ge[0:QT, :], jump[0:QT, :], ALU.mult))
                        s.settled(v)
                        s.done(v.tensor_reduce(off_f[:, q:q + 1], gej[0:QT, :], AX.X, ALU.add))
                    s.settled(v)
                s.done(v.tensor_scalar(win_t[:, way, :], win_t[:, way, :], -1.0, None, ALU.add))
                s.settled(v)
                s.done(v.tensor_scalar(win128[:, way, :], win_t[:, way, :], float(P), None, ALU.mult))
                s.settled(v)

            v.wait_ge(counts_done, 1)
            s.done(v.tensor_copy(start[:, 0, :], rows_ps[:, 0:WINDOWS + 1]))
            s.settled(v)
            tiles_of(0)
            s.done(v.scalar_tensor_tensor(out=shift[:, :], in0=first_t[:, 0, :], scalar=-float(P),
                                          in1=start[:, 0, 0:WINDOWS], op0=ALU.mult, op1=ALU.add))
            s.settled(v)
            s.done(v.tensor_copy(jump[:, 0:1], shift[:, 0:1]))
            s.done(v.tensor_tensor(jump[:, 1:], shift[:, 1:], shift[:, 0:WINDOWS - 1], ALU.subtract))
            s.settled(v)
            window_of_tiles(0)
            v.sem_inc(lanes_ready, 1)
            s.done(v.scalar_tensor_tensor(out=off_f[:, :], in0=cst[0:QT, C_TILE:C_TILE + QUARTERS], scalar=float(P),
                                          in1=off_f[:, :], op0=ALU.mult, op1=ALU.add))
            s.settled(v)
            v.tensor_scalar(off_i[:, :], off_f[:, :], float(EDGES), None, ALU.min).then_inc(offsets_made, 1)

            v.wait_ge(windows_in, 16 * WINDOWS)
            s.done(v.tensor_scalar(hit[:, :], hit[:, :], cst[0:EP, C_WIN:C_WIN + 1], None, ALU.is_equal))
            s.settled(v)
            s.done(v.tensor_tensor_scan(rank[:, :], hit[:, :], hit[:, :], 0.0, ALU.add, ALU.bypass))
            s.settled(v)
            s.done(v.tensor_copy(total[:, :], rank[:, PART_LEN - 1:PART_LEN]))
            s.settled(v)
            s.done(v.tensor_scalar(total_b[:, :], cst[0:EP, C_ONES:C_ONES + P], total[:, :], None, ALU.mult))
            s.settled(v)
            v.sem_inc(total_made, 1)

            v.wait_ge(lanes_done, 1)
            s.done(v.tensor_copy(g["tile_win4"][:, 0, :], lane_ps[0][0:QUARTERS, 0:QT]))
            s.settled(v)
            v.sem_inc(lanes_taken, 1)
            v.wait_ge(blocks_in, 16 * 6 * QUARTERS)
            s.done(v.tensor_copy(f_dst[:, :, :], r_dst[:, :, :]))
            s.done(v.tensor_copy(f_src[:, :, :], r_src[:, :, :]))
            s.settled(v)
            for q in range(QUARTERS):
                s.done(v.tensor_scalar(f_loc[:, q, :], f_dst[:, q, :], win128[:, 0, q:q + 1], None, ALU.subtract))
            s.settled(v)
            v.sem_inc(lanes_ready, 2)
            s.done(v.tensor_scalar(f_val[:, :, :], f_loc[:, :, :], 0.0, None, ALU.is_ge))
            s.settled(v)
            s.done(v.scalar_tensor_tensor(out=f_val[:, :, :], in0=f_loc[:, :, :], scalar=float(P), in1=f_val[:, :, :],
                                          op0=ALU.is_lt, op1=ALU.mult))
            s.settled(v)
            s.done(v.scalar_tensor_tensor(out=f_key[:, :, :], in0=f_dst[:, :, :], scalar=1.0, in1=f_val[:, :, :],
                                          op0=ALU.add, op1=ALU.mult))
            s.settled(v)
            v.tensor_scalar(f_key[:, :, :], f_key[:, :, :], -1.0, None, ALU.add).then_inc(keys_made, 1)
            s.done(v.scalar_tensor_tensor(out=f_idx[:, :, :], in0=f_src[:, :, :], scalar=float(RELS), in1=r_typ[:, :, :],
                                          op0=ALU.mult, op1=ALU.add))
            s.settled(v)

            v.wait_ge(parts_done, 1)
            s.done(v.tensor_copy(start[:, 1, 0:WINDOWS], rows_ps[:, 64:64 + WINDOWS]))
            s.done(v.tensor_copy(base[:, :], rows_ps[0:EP, 128:129]))
            s.settled(v)
            tiles_of(1)
            window_of_tiles(1)
            s.done(v.tensor_tensor(pick[:, :], cst[0:EP, C_WINOH:C_WINOH + WINDOWS], first_t[0:EP, 1, :], ALU.mult))
            s.settled(v)
            s.done(v.tensor_reduce(total[:, :], pick[:, :], AX.X, ALU.add))
            s.settled(v)
            s.done(v.scalar_tensor_tensor(out=base[:, :], in0=total[:, :], scalar=float(P), in1=base[:, :],
                                          op0=ALU.mult, op1=ALU.add))
            s.settled(v)
            s.done(v.tensor_scalar(base[:, :], base[:, :], -1.0, None, ALU.add))
            s.settled(v)
            v.scalar_tensor_tensor(out=rank[:, :], in0=rank[:, :], scalar=base[:, 0:1], in1=hit[:, :],
                                   op0=ALU.add, op1=ALU.mult).then_inc(rank_made, 1)

            def take(n, out):
                v.wait_ge(lanes_done, n + 1)
                k = out.shape[0]
                v.tensor_copy(out, lane_ps[n % 2][0:k, 0:out.shape[1]]).then_inc(lanes_taken, 1)

            take(1, g["dst_slot"][:, 0:TILES])
            take(2, g["src_idx"][:, :])
            v.sem_inc(lanes_ready, 2)
            take(3, g["tile_win4"][:, 1, :])
            take(4, g["fwd_idx"][:, :])


def project_relations(nc, tag, cst, d, dram, g):
    with ExitStack() as ctx:
        def sb(name, shape, dt=F32):
            return ctx.enter_context(nc.sbuf_tensor(f"{tag}_{name}", shape, dt))

        sem = phase_semaphores(nc, tag, ctx)

        w_sb = sb("w_sb", [P, 2, 2, RELS, FEAT])
        xw = sb("xw", [P, 2, FEAT])
        xt = sb("xt", [P, 2, 2, P])
        stage = sb("stage", [P, 4, RELS // 2, FEAT])
        xt_ps = [ctx.enter_context(nc.psum_tensor(f"{tag}_xt_ps{i}", [P, 512], F32)) for i in range(2)]
        out_ps = [ctx.enter_context(nc.psum_tensor(f"{tag}_out_ps{i}", [P, 512], F32)) for i in range(4)]
        w_in = sem("w_in")
        x_in = [sem(f"x_in{i}") for i in range(2)]
        x_used = sem("x_used")
        xt_done = sem("xt_done")
        xt_taken = sem("xt_taken")
        xt_used = sem("xt_used")
        out_done = sem("out_done")
        out_taken = [sem("taken_vector"), sem("taken_scalar")]
        stored = [sem(f"stored{i}") for i in range(4)]
        stage_free = [sem(f"stage_free{i}") for i in range(4)]
        PAIRS = RELS
        AHEAD = 2
        block = ctx.enter_context(nc.Block())

        @block.sync
        def _(sp):
            for st in range(4):
                sp.sem_inc(stage_free[st], 1)
            for way, name in enumerate(("L0_gnn_Wf", "L0_gnn_Wb")):
                for r in range(RELS):
                    sp.dma_start(w_sb[:, way, :, r, :], d[name][r].rearrange("(k p) n -> p k n", p=P)).then_inc(w_in, 16)

            def load(w, par):
                sp.wait_ge(xt_done, w + AHEAD - 1)
                sp.dma_start(xw[:, par, :], d["x_pad"][bass.ds(w * P, P), :]).then_inc(x_in[par], 16)

            def store(w, par):
                for st in range(4):
                    way, half = st // 2, st % 2
                    for s in out_taken:
                        sp.wait_ge(s, w * (PAIRS // 2) + 2 * (st + 1) + AHEAD)
                    sp.dma_start(dram[("rel_table_f", "rel_table_b")[way]].rearrange("(n r) f -> n r f", r=RELS)
                                 [bass.ds(w * P, P), half * 8:half * 8 + 8, :],
                                 stage[:, st, :, :]).then_inc(stored[st], 16)
                for st in range(4):
                    sp.wait_ge(stored[st], (w + 1) * 16)
                    sp.sem_inc(stage_free[st], 1)

            load(0, 0)
            with sp.Fori(0, WINDOWS // 2) as i:
                load(i * 2 + 1, 1)
                store(i * 2, 0)
                load(i * 2 + 2, 0)
                store(i * 2 + 1, 1)
            store(WINDOWS - 1, 0)

        @block.gpsimd
        def _(gp):
            for j in range(EJ):
                gp.indirect_dma_start(out=dram["records"],
                                      out_offset=bass.IndirectOffsetOnAxis(ap=g["pos_i"][:, j:j + 1], axis=0),
                                      in_=g["record"][:, j, :], in_offset=None).then_inc(g["landed"][tag][0], 16)
            gp.wait_ge(g["landed"][tag][0], 16 * EJ)

        @block.tensor
        def _(pe):
            pe.sem_inc(xt_done, AHEAD)
            pe.sem_inc(out_done, AHEAD * PAIRS)
            pe.wait_ge(w_in, 16 * 2 * RELS)

            def body(w, par):
                pe.wait_ge(x_in[par], (w + (2 - par)) * 8)
                pe.wait_ge(xt_taken, w + 1)
                for k in range(2):
                    mm = pe.transpose(xt_ps[par][:, k * P:(k + 1) * P], xw[:, par, k * P:(k + 1) * P],
                                      cst[:, C_IDENT:C_IDENT + P])
                mm.then_inc(xt_done, 1)
                pe.wait_ge(xt_taken, w + 1 + AHEAD)
                for n in range(PAIRS):
                    way, r = n // 8, 2 * (n % 8)
                    pe.wait_ge(out_taken[n % 2], w * (PAIRS // 2) + n // 2 - 1 + AHEAD)
                    for k in range(2):
                        mm = pe.matmul(out_ps[n % 4][:, :], xt[:, par, k, :],
                                       w_sb[:, way, k, r:r + 2, :].rearrange("p r f -> p (r f)"),
                                       start=(k == 0), stop=(k == 1))
                    mm.then_inc(out_done, 1)

            each_window(pe, body)

        def take(eng, copy, lane):
            def body(w, par):
                for n in range(lane, PAIRS, 2):
                    st = n // 4
                    eng.wait_ge(out_done, (w + AHEAD) * PAIRS + n + 1)
                    if n % 4 < 2:
                        eng.wait_ge(stage_free[st], w + 1)
                    copy(stage[:, st, 2 * (n % 4):2 * (n % 4) + 2, :].rearrange("p r f -> p (r f)"),
                         out_ps[n % 4][:, :]).then_inc(out_taken[lane], 1)
            return body

        @block.vector
        def _(v):
            v.sem_inc(out_taken[0], AHEAD)
            each_window(v, take(v, v.tensor_copy, 0))

        @block.scalar
        def _(act):
            act.sem_inc(out_taken[1], AHEAD)
            act.sem_inc(xt_taken, AHEAD)
            odd_banks = take(act, act.copy, 1)

            def body(w, par):
                act.wait_ge(xt_done, w + 1 + AHEAD)
                act.wait_ge(out_done, (w + AHEAD - 1) * PAIRS)
                act.copy(xt[:, par, :, :].rearrange("p k e -> p (k e)"), xt_ps[par][:, 0:2 * P]).then_inc(xt_taken, 1)
                odd_banks(w, par)

            each_window(act, body)


def grouped_slots(nc, tag, cst, dram, g):
    with ExitStack() as ctx:
        def sb(name, shape, dt=F32):
            return ctx.enter_context(nc.sbuf_tensor(f"{tag}_{name}", shape, dt))

        sem = phase_semaphores(nc, tag, ctx)
        rec = sb("rec", [QT, QUARTERS, P, 2], I32)
        field = sb("field", [QT, 2, QUARTERS, P])
        lane_ps = [ctx.enter_context(nc.psum_tensor(f"{tag}_lane_ps{i}", [P, 512], F32)) for i in range(2)]
        records_in = sem("records_in")
        fields_made = sem("fields_made")
        lanes_done = sem("lanes_done")
        lanes_taken = sem("lanes_taken")
        block = ctx.enter_context(nc.Block())

        @block.sync
        def _(sp):
            sp.dma_start(rec[:, :, :, :], dram["records"].rearrange("(q p e) c -> p q e c", q=QUARTERS, p=QT))\
                .then_inc(records_in, 16)

        @block.tensor
        def _(pe):
            pe.wait_ge(fields_made, 2 * QUARTERS)
            for i in range(2):
                for q in range(QUARTERS):
                    mm = pe.transpose(lane_ps[i][:, q * QT:(q + 1) * QT], field[:, i, q, :], cst[0:QT, C_IDENT:C_IDENT + QT])
                mm.then_inc(lanes_done, 1)

        @block.vector
        def _(v):
            v.wait_ge(records_in, 16)
            for q in range(QUARTERS):
                v.tensor_scalar(field[:, 0, q, :], rec[:, q, :, 0], g["win128"][:, 1, q:q + 1], None, ALU.subtract)\
                    .then_inc(fields_made, 1)
                v.tensor_copy(field[:, 1, q, :], rec[:, q, :, 1]).then_inc(fields_made, 1)
            for i, out in enumerate((g["src_slot"][:, 0:TILES], g["bwd_idx"][:, :])):
                v.wait_ge(lanes_done, i + 1)
                v.tensor_copy(out, lane_ps[i][:, 0:TILES]).then_inc(lanes_taken, 1)
            v.wait_ge(lanes_taken, 2)


def scan_tables(nc, tag, cst, dram, g):
    with ExitStack() as ctx:
        def sb(name, shape, dt=F32):
            return ctx.enter_context(nc.sbuf_tensor(f"{tag}_{name}", shape, dt))

        sem = phase_semaphores(nc, tag, ctx)

        key = sb("key", [SEG_ROWS, 3, SCAN_LEN])
        slots = sb("slots", [SEG_ROWS, SCAN_LEN])
        brk = sb("brk", [SEG_ROWS, 2, SCAN_LEN])
        brk_h = sb("brk_h", [SEG_ROWS, 2, SCAN_LEN], BF16)
        last = sb("last", [SEG_ROWS, SCAN_LEN])
        col = sb("col", [SEG_ROWS, 3])
        rows_ps = ctx.enter_context(nc.psum_tensor(f"{tag}_rows_ps", [P, 512], F32))
        last_ps = ctx.enter_context(nc.psum_tensor(f"{tag}_last_ps", [P, 512], F32))
        keys_in = sem("keys_in")
        vec = sem("vec")
        made = sem("made")
        turned = sem("turned")
        breaks_out = sem("breaks_out")
        breaks_in = sem("breaks_in")
        block = ctx.enter_context(nc.Block())

        @block.sync
        def _(sp):
            line = dram["keys"].rearrange("t e -> (t e)")
            for i, by in enumerate((0, -1, 1)):
                sp.dma_start(key[:, i, :], line[P + by:P + by + TILES * P].rearrange("(r e) -> r e", r=SEG_ROWS))\
                    .then_inc(keys_in, 16)
            sp.dma_start(slots[:, :], dram["slots"].rearrange("(r b) e -> r (b e)", b=SCAN_TILES)).then_inc(keys_in, 16)
            sp.wait_ge(made, 1)
            sp.wait_ge(made, 2)
            for way in range(2):
                sp.dma_start(dram["breaks"][way], brk_h[:, way, :]).then_inc(breaks_out, 16)
            sp.wait_ge(breaks_out, 32)
            for way, to in enumerate((g["break_f"], g["break_b"])):
                for h in range(8):
                    sp.dma_start(to[h * SCAN_ROWS:(h + 1) * SCAN_ROWS, :, :],
                                 dram["breaks"][way].rearrange("(k c) e -> c k e", c=SCAN_ROWS)).then_inc(breaks_in, 16)
            sp.wait_ge(breaks_in, 16 * 16)

        @block.tensor
        def _(pe):
            pe.wait_ge(made, 2)
            ident = cst[0:SEG_ROWS, C_IDENT:C_IDENT + SEG_ROWS]
            for i in range(3):
                pe.matmul(rows_ps[0:1, i * P:i * P + SEG_ROWS], col[:, i:i + 1], ident, start=True, stop=True)
            for b in range(SCAN_TILES):
                mm = pe.transpose(last_ps[:, b * P:b * P + SEG_ROWS], last[:, b * P:(b + 1) * P], ident)
            mm.then_inc(turned, 1)

        @block.vector
        def _(v):
            s = Steps(vec)
            s.done(v.memset(g["chain_f"][:, :, :, :], -BIG))
            s.done(v.memset(g["chain_b"][:, :, :, :], -BIG))
            v.wait_ge(keys_in, 64)
            s.done(v.tensor_copy(g["slot_rows"][:, :], slots[:, :]))
            s.done(v.tensor_copy(g["pick_row"][:, :], cst[0:SEG_ROWS, C_IDENT:C_IDENT + SEG_ROWS]))
            for i in range(2):
                s.done(v.tensor_tensor(brk[:, i, :], key[:, 0, :], key[:, 1 + i, :], ALU.is_equal))
            s.settled(v)
            s.done(v.tensor_scalar(brk[:, :, :], brk[:, :, :], -1.0, BIG, ALU.add, ALU.mult))
            s.settled(v)
            s.done(v.tensor_copy(brk_h[:, 0, :], brk[:, 0, :]))
            v.tensor_copy(brk_h[:, 1, ::-1], brk[:, 1, :]).then_inc(made, 1)
            s.done(v.tensor_scalar(last[:, :], brk[:, 1, :], -1.0, None, ALU.is_lt))
            s.done(v.tensor_reduce(col[:, 0:2], brk[:, :, :], AX.X, ALU.min))
            s.done(v.tensor_scalar(col[:, 2:3], brk[:, 0, 0:1], -1.0, None, ALU.is_ge))
            s.settled(v)
            v.wait_ge(made, 1)
            v.sem_inc(made, 1)
            v.wait_ge(turned, 1)
            for h in range(8):
                row = [rows_ps[0:1, i * P:i * P + SEG_ROWS].rearrange("a (k c) -> a k c", c=SCAN_ROWS) for i in range(3)]
                s.done(v.tensor_copy(g["chain_f"][:, :, h, 1:], row[0]))
                s.done(v.tensor_copy(g["chain_b"][:, :, h, 1:], row[1][:, :, ::-1]))
            s.done(v.tensor_copy(g["goes_on"][:, :], row[2][:, :, 0]))
            for b in range(SCAN_TILES):
                s.done(v.tensor_copy(
                    g["last"][:, :].rearrange("p (k c b) -> p (k c) b", c=SCAN_ROWS, b=SCAN_TILES)[:, :, b],
                    last_ps[:, b * P:b * P + SEG_ROWS]))
            s.settled(v)


def take_rows(gp, table, rows, cur, idx, free, ahead, landed, copied, width):
    def chunk(k, turn, half):
        gp.wait_ge(free, (k - 1) * CHUNK + ahead)
        gp.sem_inc(copied, 1)
        gp.tensor_copy(cur[:, half, :], idx[:, bass.ds(k * CHUNK, CHUNK)]).then_inc(copied, 1)
        gp.wait_ge(copied, (k + 1) * 3 - 1)
        gp.sem_inc(copied, 1)
        for j in range(CHUNK):
            gp.indirect_dma_start(out=rows[:, half, j, 0:width], out_offset=None, in_=table,
                                  in_offset=bass.IndirectOffsetOnAxis(ap=cur[:, half, j:j + 1], axis=0))\
                .then_inc(landed[half], 16)

    with gp.Fori(0, CHUNKS // 2) as i:
        for half in range(2):
            chunk(i * 2 + half, i, half)


def each_chunk(engine, body):
    with engine.Fori(0, CHUNKS // 2) as i:
        for half in range(2):
            body(i * 2 + half, i, half)


def tile_windows(engine, regs, tile_win, way, tile):
    engine.reg_load(regs, tile_win[0:1, way, bass.ds(tile, len(regs))])
    return [engine.snap(r, min_val=0, max_val=WINDOWS - 1) for r in regs]


def each_turn(engine, k, regs, tile_win, body):
    with engine.Fori(0, TURNS // 2) as i:
        windows = tile_windows(engine, regs, tile_win, 0, k * CHUNK + i * (2 * STEP))
        for parity in range(2):
            body(i * 2 + parity, parity, windows[parity * STEP:(parity + 1) * STEP], True)
    body(TURNS - 1, 0, tile_windows(engine, regs[0:STEP], tile_win, 0, k * CHUNK + (TURNS - 1) * STEP), False)


def relation_edges(nc, tag, cst, dram, g, rows, way, acc):
    with ExitStack() as ctx:
        sem = phase_semaphores(nc, tag, ctx)

        cur = ctx.enter_context(nc.sbuf_tensor(f"{tag}_cur", [P, 2, CHUNK], I32))
        onehot = ctx.enter_context(nc.sbuf_tensor(f"{tag}_onehot", [P, 2, 2, P], F32))
        sum_ps = [ctx.enter_context(nc.psum_tensor(f"{tag}_sum_ps{i}", [P, 512], F32)) for i in range(STEP)]
        slot, idx = (g["dst_slot"], g["fwd_idx"]) if way == 0 else (g["src_slot"], g["bwd_idx"])
        landed = g["landed"][tag]
        copied = sem("copied")
        cleared = sem("cleared")
        onehot_made = sem("onehot_made")
        sum_made = sem("sum_made")
        sum_taken = sem("sum_taken")
        chunks_begun = sem("chunks_begun")
        AHEAD = 2 * CHUNK
        block = ctx.enter_context(nc.Block())

        @block.gpsimd
        def _(gp):
            take_rows(gp, dram[("rel_table_f", "rel_table_b")[way]], rows, cur, idx, sum_made, AHEAD, landed, copied, FEAT)

        @block.tensor
        def _(pe):
            pe.sem_inc(sum_made, AHEAD)
            pe.wait_ge(cleared, 2)

            def chunk(k, i, half):
                pe.wait_ge(landed[half], (i + 1) * (16 * CHUNK))
                pe.sem_inc(chunks_begun, 1)
                with pe.Fori(0, TURNS) as turn:
                    for j in range(STEP):
                        if j % 2 == 0:
                            pe.wait_ge(onehot_made, k * (2 * TURNS + 2) + turn * 2 + (j // 2 + 1))
                        pe.wait_ge(sum_taken, k * CHUNK + turn * STEP + (j + 1))
                        pe.matmul(sum_ps[j][:, 0:FEAT + 1], onehot[:, j // 2, j % 2, :],
                                  rows[:, half, bass.ds(turn * STEP + j, 1), 0:FEAT + 1].rearrange("p a f -> p (a f)"),
                                  start=True, stop=True).then_inc(sum_made, 1)

            each_chunk(pe, chunk)

        @block.vector
        def _(v):
            v.sem_inc(sum_taken, STEP)
            v.memset(acc[:, :, :], 0.0).then_inc(cleared, 1)
            v.memset(rows[:, :, :, FEAT:FEAT + 1], 1.0).then_inc(cleared, 1)
            v.wait_ge(cleared, 2)
            regs = [v.alloc_register(f"{tag}_v_window{j}") for j in range(STEP)]

            def make(tile, sub):
                for jj in range(2):
                    i = v.tensor_scalar(onehot[:, sub, jj, :], cst[:, C_IOTA:C_IOTA + P],
                                        slot[:, bass.ds(tile + (2 * sub + jj), 1)], None, ALU.is_equal)
                i.then_inc(onehot_made, 1)

            def chunk(k, i, half):
                v.wait_ge(sum_made, k * CHUNK + AHEAD)
                for sub in range(2):
                    make(k * CHUNK, sub)
                with v.Fori(0, TURNS) as turn:
                    windows = tile_windows(v, regs, g["tile_win"], way, k * CHUNK + turn * STEP)
                    for sub in range(2):
                        v.wait_ge(sum_made, k * CHUNK + turn * STEP + (2 * sub + 2 + AHEAD))
                        make(k * CHUNK + turn * STEP + STEP, sub)
                        for j in (2 * sub, 2 * sub + 1):
                            v.wait_ge(sum_taken, k * CHUNK + turn * STEP + (j + STEP))
                            a = acc[:, bass.ds(windows[j], 1), 0:FEAT + 1].rearrange("p a f -> p (a f)")
                            v.tensor_tensor(a, a, sum_ps[j][:, 0:FEAT + 1], ALU.add).then_inc(sum_taken, 1)

            each_chunk(v, chunk)


def load_rows(sp, rows_sb, dram_rows, done):
    sp.dma_start(rows_sb, dram_rows.rearrange("(w p) f -> p w f", p=P)).then_inc(done, 16)


def finish(nc, tag, cst, kind, heads, d, dram, g, rows, acc, acc_b, nt, x_from, x_to, bias_name, out):
    D = FEAT // heads
    with ExitStack() as ctx:
        def sb(name, shape, dt=F32):
            return ctx.enter_context(nc.sbuf_tensor(f"{tag}_{name}", shape, dt))

        sem = phase_semaphores(nc, tag, ctx)

        flat = rows.rearrange("p a t f -> p (a t f)")
        x = flat[:, 0:WINDOWS * FEAT].rearrange("p (w f) -> p w f", f=FEAT)
        t = flat[:, WINDOWS * FEAT:2 * WINDOWS * FEAT].rearrange("p (w f) -> p w f", f=FEAT)
        bias = sb("bias", [P, 3, FEAT])
        loop_w = sb("loop_w", [P, 2, FEAT]) if kind == "relations" else None
        xt = sb("xt", [P, 2, 2, P]) if kind == "relations" else None
        den = sb("den", [P, 2, WINDOWS * 8])
        m = sb("m", [P, WINDOWS * 4])
        mean = sb("mean", [P, WINDOWS])
        var = sb("var", [P, WINDOWS])
        ps = [ctx.enter_context(nc.psum_tensor(f"{tag}_fin_ps{i}", [P, 512], F32)) for i in range(4)]
        x_in = sem("x_in")
        vec = sem("vec")
        to_scalar = sem("to_scalar")
        from_scalar = sem("from_scalar")
        turned = sem("turned")
        turned_out = sem("turned_out")
        looped = sem("looped")
        loop_taken = sem("loop_taken")
        y_ready = sem("y_ready")
        stored = sem("stored")
        block = ctx.enter_context(nc.Block())
        y = acc[:, :, 0:FEAT]
        y4 = lambda a: a.rearrange("p w (h d) -> p w h d", h=heads)
        norm = kind != "elu"

        @block.sync
        def _(sp):
            load_rows(sp, x, x_from, x_in)
            names = bias_name if isinstance(bias_name, tuple) else (bias_name,)
            for i in range(3):
                name = names[i] if i < len(names) else names[0]
                sp.dma_start(bias[:, i, :], d[name].rearrange("(a f) -> a f", a=1).to_broadcast([P, FEAT]))\
                    .then_inc(x_in, 16)
            if kind == "relations":
                sp.dma_start(loop_w[:, :, :], d["L0_gnn_loop_weight"].rearrange("(k p) n -> p k n", p=P)).then_inc(x_in, 16)
            sp.wait_ge(y_ready, 1)
            if out is None:
                sp.dma_start(x_to.rearrange("(w p) f -> p w f", p=P), y).then_inc(stored, 16)
                sp.wait_ge(stored, 16)
            else:
                whole = NODES // P
                sp.dma_start(out[0:whole * P, :].rearrange("(w p) f -> p w f", p=P), y[:, 0:whole, :]).then_inc(stored, 16)
                sp.dma_start(out[whole * P:NODES, :], y[0:NODES - whole * P, whole, :]).then_inc(stored, 16)
                sp.wait_ge(stored, 32)

        loads = 16 * (5 if kind == "relations" else 4)

        if kind == "relations":
            @block.tensor
            def _(pe):
                pe.wait_ge(x_in, loads)
                for w in range(WINDOWS):
                    if w >= 2:
                        pe.wait_ge(turned_out, w - 1)
                    for k in range(2):
                        mm = pe.transpose(ps[w % 2][:, k * P:(k + 1) * P], x[:, w, k * P:(k + 1) * P],
                                          cst[:, C_IDENT:C_IDENT + P])
                    mm.then_inc(turned, 1)
                    pe.wait_ge(turned_out, w + 1)
                    if w >= 2:
                        pe.wait_ge(loop_taken, w - 1)
                    for k in range(2):
                        mm = pe.matmul(ps[2 + w % 2][:, 0:FEAT], xt[:, w % 2, k, :], loop_w[:, k, :],
                                       start=(k == 0), stop=(k == 1))
                    mm.then_inc(looped, 1)

        @block.scalar
        def _(act):
            if kind == "relations":
                for w in range(WINDOWS):
                    act.wait_ge(turned, w + 1)
                    if w >= 2:
                        act.wait_ge(looped, w - 1)
                    act.copy(xt[:, w % 2, :, :].rearrange("p k e -> p (k e)"), ps[w % 2][:, 0:2 * P]).then_inc(turned_out, 1)
            n = 0
            if kind in ("self", "elu"):
                act.wait_ge(to_scalar, 1)
                act.activation(m[:, :], m[:, :], ACT.Exp).then_inc(from_scalar, 1)
                act.wait_ge(to_scalar, 2)
                act.activation(t, t, ACT.Exp).then_inc(from_scalar, 1)
                n = 2
            if norm:
                act.wait_ge(to_scalar, n + 1)
                act.activation(t, y, ACT.Square).then_inc(from_scalar, 1)
                act.wait_ge(to_scalar, n + 2)
                act.activation(var[:, :], var[:, :], ACT.Sqrt).then_inc(from_scalar, 1)

        @block.vector
        def _(v):
            s = Steps(vec)
            over_f = lambda a: a.unsqueeze(2).to_broadcast([P, WINDOWS, FEAT])
            over_w = lambda a: a.unsqueeze(1).to_broadcast([P, WINDOWS, FEAT])
            over_d = lambda a: a.rearrange("p (w h) -> p w h", h=heads).unsqueeze(3).to_broadcast([P, WINDOWS, heads, D])
            v.wait_ge(x_in, loads)
            if kind == "relations":
                for way, a in enumerate((acc, acc_b)):
                    c = den[:, way, 0:WINDOWS]
                    s.done(v.tensor_scalar(den[:, way, WINDOWS:2 * WINDOWS], a[:, :, FEAT], 1.0, None, ALU.min))
                    s.done(v.tensor_scalar(c, a[:, :, FEAT], 1.0, None, ALU.max))
                    s.settled(v)
                    s.done(v.reciprocal(c, c))
                    s.settled(v)
                    s.done(v.tensor_tensor(a[:, :, 0:FEAT], a[:, :, 0:FEAT], over_f(c), ALU.mult))
                    s.done(v.tensor_tensor(t, over_w(bias[:, way, :]), over_f(den[:, way, WINDOWS:2 * WINDOWS]), ALU.mult))
                    s.settled(v)
                    s.done(v.tensor_tensor(a[:, :, 0:FEAT], a[:, :, 0:FEAT], t, ALU.add))
                    s.settled(v)
                s.done(v.tensor_tensor(y, y, acc_b[:, :, 0:FEAT], ALU.add))
                s.settled(v)
                s.done(v.tensor_tensor(y, y, over_w(bias[:, 2, :]), ALU.add))
                s.settled(v)
                for w in range(WINDOWS):
                    v.wait_ge(looped, w + 1)
                    v.scalar_tensor_tensor(out=acc[:, w, 0:FEAT], in0=ps[2 + w % 2][:, 0:FEAT], scalar=2.0,
                                           in1=acc[:, w, 0:FEAT], op0=ALU.mult, op1=ALU.add).then_inc(loop_taken, 1)
                v.wait_ge(loop_taken, WINDOWS)
            else:
                c = den[:, 0, 0:WINDOWS * heads]
                c3 = c.rearrange("p (w h) -> p w h", h=heads)
                if kind in ("self", "elu"):
                    m3 = m[:, :].rearrange("p (w h) -> p w h", h=heads)
                    c1 = den[:, 1, 0:WINDOWS * heads].rearrange("p (w h) -> p w h", h=heads)
                    zs = nt[:, :, 268:272]
                    has = acc[:, :, 264:265].to_broadcast([P, WINDOWS, heads])
                    s.done(v.tensor_tensor(c1, has, zs, ALU.mult))
                    s.settled(v)
                    s.done(v.tensor_tensor(m3, c1, acc[:, :, 260:264], ALU.subtract))
                    s.settled(v)
                    v.sem_inc(to_scalar, 1)
                    v.wait_ge(from_scalar, 1)
                    s.done(v.tensor_tensor(c3, acc[:, :, 256:260], m3, ALU.add))
                    s.done(v.tensor_tensor(y4(t), y4(nt[:, :, 0:FEAT]), over_d(m[:, :]), ALU.mult))
                    s.settled(v)
                    s.done(v.tensor_tensor(y, y, t, ALU.add))
                    s.done(v.tensor_scalar(c, c, 1e-16, None, ALU.add))
                else:
                    s.done(v.tensor_scalar(c3, acc[:, :, 256:256 + heads], 1e-10, None, ALU.max))
                s.settled(v)
                s.done(v.reciprocal(c, c))
                s.settled(v)
                s.done(v.tensor_tensor(y4(y), y4(y), over_d(c), ALU.mult))
                s.settled(v)
                s.done(v.tensor_tensor(y, y, over_w(bias[:, 0, :]), ALU.add))
                s.settled(v)
            n = 0
            if kind in ("self", "elu"):
                s.done(v.tensor_scalar(t, y, 0.0, None, ALU.min))
                s.settled(v)
                v.sem_inc(to_scalar, 1)
                s.done(v.tensor_scalar(y, y, 0.0, -1.0, ALU.max, ALU.add))
                s.settled(v)
                v.wait_ge(from_scalar, 2)
                s.done(v.tensor_tensor(y, y, t, ALU.add))
                s.settled(v)
                n = 2
            if norm:
                s.done(v.tensor_tensor(y, y, x, ALU.add))
                s.settled(v)
                s.done(v.tensor_reduce(mean[:, :], y, AX.X, ALU.add))
                s.settled(v)
                s.done(v.tensor_scalar(mean[:, :], mean[:, :], 1.0 / FEAT, None, ALU.mult))
                s.settled(v)
                s.done(v.tensor_tensor(y, y, over_f(mean[:, :]), ALU.subtract))
                s.settled(v)
                v.sem_inc(to_scalar, 1)
                v.wait_ge(from_scalar, n + 1)
                s.done(v.tensor_reduce(var[:, :], t, AX.X, ALU.add))
                s.settled(v)
                s.done(v.tensor_scalar(var[:, :], var[:, :], 1.0 / FEAT, EPS, ALU.mult, ALU.add))
                s.settled(v)
                v.sem_inc(to_scalar, 1)
                v.wait_ge(from_scalar, n + 2)
                s.done(v.reciprocal(var[:, :], var[:, :]))
                s.settled(v)
                s.done(v.tensor_tensor(y, y, over_f(var[:, :]), ALU.mult))
                s.settled(v)
            v.sem_inc(y_ready, 1)


def project_nodes(nc, tag, cst, heads, self_edge, d, dram, nt, x_from, w_name, a_src_name, a_dst_name):
    D = FEAT // heads
    with ExitStack() as ctx:
        def sb(name, shape, dt=F32):
            return ctx.enter_context(nc.sbuf_tensor(f"{tag}_{name}", shape, dt))

        sem = phase_semaphores(nc, tag, ctx)

        w_sb = sb("w_sb", [P, 2, NTC])
        att = sb("att", [P, 2, FEAT])
        prod = sb("prod", [P, 2, 2, FEAT])
        xw = sb("xw", [P, 2, FEAT])
        xt = sb("xt", [P, 2, 2, P])
        own = sb("own", [P, WINDOWS, 4])
        xt_ps = [ctx.enter_context(nc.psum_tensor(f"{tag}_xt_ps{i}", [P, 512], F32)) for i in range(2)]
        h_ps = [ctx.enter_context(nc.psum_tensor(f"{tag}_h_ps{i}", [P, 512], F32)) for i in range(2)]
        w_in = sem("w_in")
        vec = sem("vec")
        w_ready = sem("w_ready")
        x_in = [sem(f"x_in{i}") for i in range(2)]
        xt_done = sem("xt_done")
        xt_taken = sem("xt_taken")
        h_done = sem("h_done")
        h_taken = sem("h_taken")
        stored = sem("stored")
        AHEAD = 2
        block = ctx.enter_context(nc.Block())

        @block.sync
        def _(sp):
            sp.dma_start(w_sb[:, :, 0:FEAT], d[w_name].rearrange("(k p) n -> p k n", p=P)).then_inc(w_in, 16)
            for i, name in enumerate((a_src_name, a_dst_name)):
                sp.dma_start(att[:, i, :], d[name].rearrange("(a f) -> a f", a=1).to_broadcast([P, FEAT])).then_inc(w_in, 16)

            def load(w, par):
                sp.wait_ge(xt_done, w + AHEAD - 1)
                sp.dma_start(xw[:, par, :], x_from[bass.ds(w * P, P), :]).then_inc(x_in[par], 16)

            def store(w, par):
                sp.wait_ge(h_taken, w + 1 + AHEAD)
                sp.dma_start(dram["nodes"][bass.ds(w * P, P), :],
                             nt[:, bass.ds(w, 1), 0:ROW].rearrange("p a f -> p (a f)")).then_inc(stored, 16)

            load(0, 0)
            with sp.Fori(0, WINDOWS // 2) as i:
                load(i * 2 + 1, 1)
                store(i * 2, 0)
                load(i * 2 + 2, 0)
                store(i * 2 + 1, 1)
            store(WINDOWS - 1, 0)
            sp.wait_ge(stored, 16 * WINDOWS)

        @block.tensor
        def _(pe):
            pe.sem_inc(xt_done, AHEAD)
            pe.sem_inc(h_done, AHEAD)
            pe.wait_ge(w_ready, 1)

            def body(w, par):
                pe.wait_ge(x_in[par], (w + (2 - par)) * 8)
                pe.wait_ge(xt_taken, w + 1)
                for k in range(2):
                    mm = pe.transpose(xt_ps[par][:, k * P:(k + 1) * P], xw[:, par, k * P:(k + 1) * P],
                                      cst[:, C_IDENT:C_IDENT + P])
                mm.then_inc(xt_done, 1)
                pe.wait_ge(xt_taken, w + 1 + AHEAD)
                pe.wait_ge(h_taken, w + 1)
                for k in range(2):
                    mm = pe.matmul(h_ps[par][:, 0:NTC], xt[:, par, k, :], w_sb[:, k, :], start=(k == 0), stop=(k == 1))
                mm.then_inc(h_done, 1)

            each_window(pe, body)

        @block.scalar
        def _(act):
            act.sem_inc(xt_taken, AHEAD)

            def body(w, par):
                act.wait_ge(xt_done, w + 1 + AHEAD)
                act.wait_ge(h_done, w + 1)
                act.copy(xt[:, par, :, :].rearrange("p k e -> p (k e)"), xt_ps[par][:, 0:2 * P]).then_inc(xt_taken, 1)

            each_window(act, body)

        @block.vector
        def _(v):
            s = Steps(vec)
            v.sem_inc(h_taken, AHEAD)
            s.done(v.memset(w_sb[:, :, FEAT:NTC], 0.0))
            v.wait_ge(w_in, 48)
            for i in range(2):
                for k in range(2):
                    s.done(v.tensor_tensor(prod[:, i, k, :], w_sb[:, k, 0:FEAT], att[:, i, :], ALU.mult))
            s.settled(v)
            for i in range(2):
                for k in range(2):
                    s.done(v.tensor_reduce(w_sb[:, k, FEAT + 8 * i:FEAT + 8 * i + heads],
                                           prod[:, i, k, :].rearrange("p (h d) -> p h d", h=heads), AX.X, ALU.add))
            s.settled(v)
            v.sem_inc(w_ready, 1)

            def body(w, par):
                v.wait_ge(h_done, w + 1 + AHEAD)
                v.tensor_scalar(nt[:, bass.ds(w, 1), :].rearrange("p a f -> p (a f)"), h_ps[par][:, 0:NTC],
                                1.0, None, ALU.mult).then_inc(h_taken, 1)

            each_window(v, body)
            if self_edge:
                v.wait_ge(h_taken, WINDOWS + AHEAD)
                s.done(v.tensor_tensor(own[:, :, :], nt[:, :, 256:260], nt[:, :, 264:268], ALU.add))
                s.settled(v)
                s.done(v.scalar_tensor_tensor(out=nt[:, :, 268:272], in0=own[:, :, :], scalar=0.2, in1=own[:, :, :],
                                              op0=ALU.mult, op1=ALU.max))
                s.settled(v)


def attention_edges(nc, tag, cst, kind, heads, d, dram, g, rows, acc, nt):
    D = FEAT // heads
    Q = heads * SCAN_ROWS
    own_edge = kind in ("self", "elu")
    with_attr = kind == "edge"
    width = ROW + 1 if own_edge else FEAT + heads
    CHAIN = 22 + (3 if own_edge else 0) + (0 if with_attr else 3)
    with ExitStack() as ctx:
        def sb(name, shape, dt=F32):
            return ctx.enter_context(nc.sbuf_tensor(f"{tag}_{name}", shape, dt))

        sem = phase_semaphores(nc, tag, ctx)

        def bank(name):
            return ctx.enter_context(nc.psum_tensor(f"{tag}_{name}", [P, 512], F32))

        cur = sb("cur", [P, 2, CHUNK], I32)
        onehot = sb("onehot", [P, 4, 2, P])
        hot_t = sb("hot_t", [P, 2, 2, P]) if with_attr else sb("hot_t", [P, CHUNK, P], BF16)
        distance = sb("distance", [P, 2, 2, P], BF16)
        z = sb("z", [P, heads * CHUNK])
        top = sb("top", [P, heads * CHUNK])
        scan_a = sb("scan_a", [Q, SCAN_LEN])
        scan_b = sb("scan_b", [Q, SCAN_LEN])
        entry = sb("entry", [Q, 1])
        chain_in = sb("chain_in", [1, 2, heads, SCAN_ROWS + 1])
        chain = sb("chain", [1, 2, heads, SCAN_ROWS + 1])
        chain_row = sb("chain_row", [1, 2, Q])
        carried = sb("carried", [1, 2, heads])
        fall = sb("fall", [1, heads])
        first_hot = sb("first_hot", [P, P])
        first_col = sb("first_col", [P, 1])
        factor = sb("factor", [P, heads])
        turn_ps = [bank("turn_ps0"), bank("turn_ps1")]
        dst_ps = [bank("dst_ps0"), bank("dst_ps1")]
        attr_ps = [bank("attr_ps0"), bank("attr_ps1")]
        scan_ps = bank("scan_ps")
        small_ps = bank("small_ps")
        sum_ps = [turn_ps[0], turn_ps[1], attr_ps[0], attr_ps[1]]
        term_ps, spread_ps = [dst_ps[0], attr_ps[0], attr_ps[1]], [turn_ps[0], turn_ps[1], scan_ps]
        TERM_TURNS = 4
        ROW_AT, COL_AT, FALL_AT, FIRST_AT = 352, 448, 456, 472
        if with_attr:
            attr = sb("attr", [4, 2, 2 * P])
            attr_w = sb("attr_w", [4, FEAT])
            encoded = sb("encoded", [P, 2, 2 * FEAT])
            prod = sb("prod", [P, 2, FEAT])
            part = sb("part", [P, 2, 8])
            dst_part = sb("dst_part", [P, CHUNK, 8])
        else:
            nt_part = sb("nt_part", [P, WINDOWS, 3, 8], BF16)
            terms = sb("terms", [P, CHUNK, 8]) if own_edge else top[:, :].rearrange("p (t h) -> p t h", h=8)
            nt_rest = terms[:, 0:WINDOWS, :]

        landed = g["landed"][tag]
        copied = sem("copied")
        cleared = sem("cleared")
        spread = sem("spread")
        hot_t_made = sem("hot_t_made")
        dst_done = sem("dst_done")
        dst_taken = sem("dst_taken")
        weights_in = sem("weights_in")
        attr_in = [sem(f"attr_in{i}") for i in range(2)]
        enc_done = sem("enc_done")
        enc_out = sem("enc_out")
        enc_used = sem("enc_used")
        vec = sem("vec")
        z_ready = sem("z_ready")
        z_turned = sem("z_turned")
        ends_ready = sem("ends_ready")
        ends_row = sem("ends_row")
        entry_ready = sem("entry_ready")
        entry_col = sem("entry_col")
        first_ready = sem("first_ready")
        first_done = sem("first_done")
        first_out = sem("first_out")
        factor_ready = sem("factor_ready")
        top_ready = sem("top_ready")
        top_turned = sem("top_turned")
        less_top = sem("less_top")
        weights_made = sem("weights_made")
        hot_made = sem("hot_made")
        distances = sem("distances")
        parts_split = sem("parts_split")
        part_made = sem("part_made")
        weighted = sem("weighted")
        sum_made = sem("sum_made")
        sum_taken = sem("sum_taken")
        chunks_begun = sem("chunks_begun")
        AHEAD = 2 * CHUNK
        PAIRS = 2 * TURNS
        block = ctx.enter_context(nc.Block())

        if with_attr:
            @block.sync
            def _(sp):
                sp.dma_start(attr_w[0:3, :], d["L1_gnn_edge_W"]).then_inc(weights_in, 16)
                sp.dma_start(attr_w[3:4, :], d["L1_gnn_edge_b"].rearrange("(a f) -> a f", a=1)).then_inc(weights_in, 16)
                with sp.Fori(0, CHUNKS * TURNS) as turn:
                    for sub in range(2):
                        sp.wait_ge(enc_done, turn * 2 + (sub + 1))
                        sp.dma_start(attr[:, sub, :].rearrange("a (t e) -> a t e", e=P),
                                     dram["attrs"][:, bass.ds(turn * STEP + 2 * sub, 2), :]).then_inc(attr_in[sub], 16)

        @block.gpsimd
        def _(gp):
            take_rows(gp, dram["nodes"], rows, cur, g["src_idx"], sum_made, AHEAD, landed, copied, ROW)

        @block.tensor
        def _(pe):
            ident = cst[:, C_IDENT:C_IDENT + P]
            pe.sem_inc(sum_made, AHEAD)
            pe.sem_inc(dst_done, STEP)
            if with_attr:
                pe.sem_inc(enc_done, 2)
                pe.wait_ge(weights_in, 32)
            else:
                pe.wait_ge(parts_split, 5)
            pe.wait_ge(cleared, 1)
            regs = [pe.alloc_register(f"{tag}_pe_window{j}") for j in range(3 * STEP)]

            def spread_pair(k, turn, sub):
                pe.wait_ge(hot_t_made, k * PAIRS + turn * 2 + (sub + 1))
                pe.sem_inc(chunks_begun, 1)
                pe.matmul(turn_ps[sub][:, 0:2 * P],
                          g["pick_row"][:, bass.ds(k * TURNS + turn, 1)].to_broadcast([SEG_ROWS, P]),
                          g["slot_rows"][:, sub * 2 * P:(sub + 1) * 2 * P], start=True, stop=True).then_inc(spread, 1)
                pe.wait_ge(attr_in[sub], (k * TURNS + turn + 1) * 16)
                pe.wait_ge(enc_out, k * PAIRS + turn * 2 + (sub + 1))
                for jj in range(2):
                    mm = pe.matmul(attr_ps[sub][:, jj * FEAT:(jj + 1) * FEAT],
                                   attr[:, sub, jj * P:(jj + 1) * P], attr_w[:, :], start=True, stop=True)
                mm.then_inc(enc_done, 1)

            def destination_rows(k):
                def turn_rows(turn, parity, windows, more):
                    for sub in range(2):
                        pe.wait_ge(hot_t_made, k * PAIRS + turn * 2 + (sub + 3))
                        for jj in range(2):
                            j = 2 * sub + jj
                            pe.wait_ge(dst_taken, k * CHUNK + turn * STEP + (j + 3))
                            pe.matmul(dst_ps[jj][:, 0:NTC], hot_t[:, sub, jj, :],
                                      nt[:, bass.ds(windows[j], 1), :].rearrange("p a f -> p (a f)"),
                                      start=True, stop=True).then_inc(dst_done, 1)
                        if more:
                            spread_pair(k, turn + 1, sub)

                for sub in range(2):
                    spread_pair(k, 0, sub)
                each_turn(pe, k, regs[0:2 * STEP], g["tile_win"], turn_rows)

            def spread_turn(k, turn, bank, order):
                pe.wait_ge(hot_t_made, k * TURNS + order)
                pe.sem_inc(chunks_begun, 1)
                pe.matmul(spread_ps[bank][:, :],
                          g["pick_row"][:, bass.ds(k * TURNS + turn, 1)].to_broadcast([SEG_ROWS, P]),
                          g["slot_rows"][:, :], start=True, stop=True).then_inc(spread, 1)

            def destination_terms(k):
                def one_round(i, banks, spread_next):
                    windows = [tile_windows(pe, regs[b * STEP:(b + 1) * STEP], g["tile_win"], 0,
                                            k * CHUNK + i * STEP + b * (TERM_TURNS * STEP)) for b in range(banks)]
                    for b in range(banks):
                        if b < spread_next:
                            spread_turn(k, i + (1 + b * TERM_TURNS), b, i * 3 + (b + 4))
                        pe.wait_ge(hot_t_made, k * TURNS + i * 3 + (b + 4))
                        pe.sem_inc(chunks_begun, 1)
                        for j in range(STEP):
                            pe.matmul(term_ps[b][:, bass.ds((i * STEP + j) * 24, 24)],
                                      hot_t[:, bass.ds((i + b * TERM_TURNS) * STEP + j, 1), :].rearrange("p a n -> p (a n)"),
                                      nt_part[:, bass.ds(windows[b][j], 1), :, :].rearrange("p a n f -> p (a n f)"),
                                      start=True, stop=True).then_inc(dst_done, 1)

                for b in range(3):
                    spread_turn(k, b * TERM_TURNS, b, b + 1)
                with pe.Fori(0, TERM_TURNS - 2) as i:
                    one_round(i, 3, 3)
                one_round(TERM_TURNS - 2, 3, 2)
                one_round(TERM_TURNS - 1, 2, 0)

            def chunk(k, i, half):
                pe.wait_ge(sum_taken, k * CHUNK + STEP)
                if with_attr:
                    destination_rows(k)
                else:
                    pe.wait_ge(z_ready, k + 1)
                    destination_terms(k)
                pe.wait_ge(z_ready, k + 2)
                pe.sem_inc(chunks_begun, 1)
                for b in range(SCAN_TILES):
                    mm = pe.transpose(scan_ps[0:Q, b * P:(b + 1) * P], (top if own_edge else z)[:, b::SCAN_TILES], ident)
                mm.then_inc(z_turned, 1)
                pe.wait_ge(ends_ready, k * 2 + 1)
                pe.sem_inc(chunks_begun, 1)
                pe.matmul(small_ps[0:1, ROW_AT:ROW_AT + Q], scan_a[:, SCAN_LEN - 1:SCAN_LEN], ident[0:Q, 0:Q],
                          start=True, stop=True).then_inc(ends_row, 1)
                pe.wait_ge(entry_ready, k * 2 + 1)
                pe.sem_inc(chunks_begun, 1)
                pe.matmul(small_ps[0:Q, COL_AT:COL_AT + 1], chain_row[:, 0, :], cst[0:1, C_ONES:C_ONES + 1],
                          start=True, stop=True).then_inc(entry_col, 1)
                pe.wait_ge(first_ready, k + 1)
                pe.matmul(dst_ps[1][:, FIRST_AT:FIRST_AT + 1], first_hot[:, :], ident[:, 0:1],
                          start=True, stop=True).then_inc(first_done, 1)
                pe.wait_ge(ends_ready, k * 2 + 2)
                pe.sem_inc(chunks_begun, 1)
                pe.matmul(small_ps[0:1, ROW_AT:ROW_AT + Q], scan_b[:, 0:1], ident[0:Q, 0:Q],
                          start=True, stop=True).then_inc(ends_row, 1)
                pe.wait_ge(entry_ready, k * 2 + 2)
                pe.wait_ge(first_out, k + 1)
                pe.sem_inc(chunks_begun, 1)
                pe.matmul(dst_ps[1][:, FALL_AT:FALL_AT + heads], cst[0:1, C_ONES:C_ONES + P], fall[:, :],
                          start=True, stop=True)
                pe.matmul(small_ps[0:Q, COL_AT:COL_AT + 1], chain_row[:, 1, :], cst[0:1, C_ONES:C_ONES + 1],
                          start=True, stop=True).then_inc(entry_col, 1)
                pe.wait_ge(top_ready, k + 1)
                pe.sem_inc(chunks_begun, 1)
                for b in range(SCAN_TILES):
                    mm = pe.transpose(small_ps[:, b * Q:(b + 1) * Q], scan_b[:, b * P:(b + 1) * P], ident[0:Q, 0:Q])
                mm.then_inc(top_turned, 1)
                def sums(turn, parity):
                    pe.wait_ge(weighted, k * TURNS + turn + 1)
                    for j in range(STEP):
                        if j % 2 == 0:
                            pe.wait_ge(hot_made, k * PAIRS + turn * 2 + (j // 2 + 3))
                        pe.wait_ge(sum_taken, k * CHUNK + turn * STEP + (j + 1))
                        pe.matmul(sum_ps[j][:, 0:width], onehot[:, 2 * parity + j // 2, j % 2, :],
                                  rows[:, half, bass.ds(turn * STEP + j, 1), 0:width].rearrange("p a f -> p (a f)"),
                                  start=True, stop=True).then_inc(sum_made, 1)

                with pe.Fori(0, TURNS // 2) as pair:
                    for parity in range(2):
                        sums(pair * 2 + parity, parity)
                sums(TURNS - 1, 0)

            each_chunk(pe, chunk)

        @block.scalar
        def _(act):
            act.sem_inc(hot_made, 2)
            if with_attr:
                act.sem_inc(enc_out, 2)

            def make_hot(k, turn, parity):
                for sub in range(2):
                    act.wait_ge(hot_made, k * PAIRS + turn * 2 + (sub + 1))
                    act.sem_inc(chunks_begun, 1)
                    for jj in range(2):
                        act.activation(distance[:, sub, jj, :], cst[:, C_IOTA:C_IOTA + P], ACT.Abs, scale=-1.0,
                                       bias=g["dst_slot"][:, bass.ds(k * CHUNK + turn * STEP + (2 * sub + jj), 1)])\
                            .then_inc(distances, 1)
                for sub in range(2):
                    act.wait_ge(sum_made, k * CHUNK + turn * STEP + (2 * sub + AHEAD - 6))
                    act.wait_ge(distances, k * CHUNK + turn * STEP + (2 * sub + 2))
                    act.activation(onehot[:, 2 * parity + sub, :, :].rearrange("p a n -> p (a n)"),
                                   distance[:, sub, :, :].rearrange("p a n -> p (a n)"), ACT.Relu, scale=-1.0,
                                   bias=cst[:, C_ONES:C_ONES + 1]).then_inc(hot_made, 1)

            def chunk(k, i, half):
                if with_attr:
                    with act.Fori(0, TURNS) as turn:
                        for sub in range(2):
                            act.wait_ge(enc_done, k * PAIRS + turn * 2 + (sub + 3))
                            act.wait_ge(enc_used, k * CHUNK + turn * STEP + (2 * sub + 2))
                            act.activation(encoded[:, sub, :], attr_ps[sub][:, :], ACT.Relu).then_inc(enc_out, 1)
                act.wait_ge(sum_made, k * CHUNK + AHEAD)
                make_hot(k, 0, 0)
                act.wait_ge(first_done, k + 1)
                act.copy(first_col[:, :], dst_ps[1][:, FIRST_AT:FIRST_AT + 1]).then_inc(first_out, 1)
                act.wait_ge(first_out, k + 1)
                act.wait_ge(entry_col, k * 2 + 2)
                act.activation(factor[:, :], dst_ps[1][:, FALL_AT:FALL_AT + heads], ACT.Exp,
                               scale=first_col[:, 0:1]).then_inc(factor_ready, 1)
                act.wait_ge(less_top, k + 1)
                act.activation(rows[:, half, :, FEAT:FEAT + heads].rearrange("p t h -> p h t"),
                               z[:, :].rearrange("p (h t) -> p h t", h=heads), ACT.Exp).then_inc(weights_made, 1)
                with act.Fori(0, TURNS // 2) as pair:
                    make_hot(k, pair * 2 + 1, 1)
                    make_hot(k, pair * 2 + 2, 0)

            each_chunk(act, chunk)

        @block.vector
        def _(v):
            v.sem_inc(sum_taken, STEP)
            v.sem_inc(z_ready, 1)
            v.sem_inc(hot_t_made, 2 if with_attr else 3)
            if with_attr:
                v.sem_inc(dst_taken, STEP)
                v.sem_inc(enc_used, STEP)
            v.memset(acc[:, :, :], 0.0).then_inc(cleared, 1)
            v.memset(chain_in[:, :, :, :], -BIG).then_inc(cleared, 1)
            v.memset(carried[:, :, :], -BIG).then_inc(cleared, 1)
            v.wait_ge(cleared, 3)
            if not with_attr:
                left = nt[:, :, ROW:NTC]
                for n in range(3):
                    v.tensor_copy(nt_part[:, :, n, :], left).then_inc(parts_split, 1)
                    if n < 2:
                        v.wait_ge(parts_split, 2 * n + 1)
                        v.tensor_tensor(nt_rest[:, :, :], left, nt_part[:, :, n, :], ALU.subtract).then_inc(parts_split, 1)
                        v.wait_ge(parts_split, 2 * n + 2)
                        left = nt_rest[:, :, :]
            regs = [v.alloc_register(f"{tag}_v_window{j}") for j in range(2 * STEP)]
            slot = g["dst_slot"]

            def make_hot_t(k, turn, sub):
                v.wait_ge(spread, k * PAIRS + turn * 2 + (sub + 1))
                v.wait_ge(dst_done, k * CHUNK + turn * STEP + (2 * sub + 2))
                v.tensor_scalar(hot_t[:, sub, :, :].rearrange("p a n -> p (a n)"), turn_ps[sub][:, 0:2 * P],
                                cst[:, C_ROW:C_ROW + 1], None, ALU.is_equal).then_inc(hot_t_made, 1)

            def turn_hot_t(k, i, bank):
                v.wait_ge(spread, k * TURNS + i * 3 + (bank + 1))
                v.tensor_scalar(hot_t[:, bass.ds((i + bank * TERM_TURNS) * STEP, STEP), :].rearrange("p a n -> p (a n)"),
                                spread_ps[bank][:, :], cst[:, C_ROW:C_ROW + 1], None, ALU.is_equal).then_inc(hot_t_made, 1)

            def edge_logits(k, turn, sub):
                tile = k * CHUNK + turn * STEP
                for j in (2 * sub, 2 * sub + 1):
                    v.wait_ge(dst_done, tile + (j + 1 + STEP))
                    v.wait_ge(enc_out, k * PAIRS + turn * 2 + (j // 2 + 3))
                    v.tensor_tensor(prod[:, j % 2, :], dst_ps[j % 2][:, 0:FEAT],
                                    encoded[:, j // 2, (j % 2) * FEAT:(j % 2 + 1) * FEAT], ALU.mult).then_inc(enc_used, 1)
                    v.wait_ge(enc_used, tile + (j + 1 + STEP))
                    v.tensor_reduce(part[:, j % 2, :], prod[:, j % 2, :].rearrange("p (h d) -> p h d", h=8),
                                    AX.X, ALU.add).then_inc(part_made, 1)
                    v.wait_ge(part_made, tile + (j + 1))
                    v.tensor_tensor(dst_part[:, bass.ds(turn * STEP + j, 1), :].rearrange("p a h -> p (a h)"),
                                    dst_ps[j % 2][:, ROW:NTC], part[:, j % 2, :], ALU.add).then_inc(dst_taken, 1)

            def chunk(k, i, half):
                s = Steps(vec, k * CHAIN)
                zh = z[:, :].rearrange("p (h t) -> p h t", h=heads)
                hr = lambda a: a.rearrange("p t h -> p h t")
                if with_attr:
                    for sub in range(2):
                        make_hot_t(k, 0, sub)

                    def logits(turn):
                        for sub in range(2):
                            edge_logits(k, turn, sub)
                            make_hot_t(k, turn + 1, sub)

                    with v.Fori(0, TURNS // 2) as pair:
                        for parity in range(2):
                            logits(pair * 2 + parity)
                    for sub in range(2):
                        edge_logits(k, TURNS - 1, sub)
                else:
                    v.wait_ge(dst_done, k * CHUNK + STEP)
                    v.sem_inc(chunks_begun, 1)
                    with v.Fori(0, TERM_TURNS - 1) as number:
                        for bank in range(3):
                            turn_hot_t(k, number, bank)
                    for bank in range(2):
                        turn_hot_t(k, TERM_TURNS - 1, bank)
                v.tensor_scalar(first_hot[:, :], cst[:, C_IOTA:C_IOTA + P], slot[:, bass.ds(k * CHUNK, 1)], None,
                                ALU.is_equal).then_inc(first_ready, 1)
                v.wait_ge(landed[half], (i + 1) * (16 * CHUNK))
                if with_attr:
                    v.wait_ge(dst_taken, (k + 1) * CHUNK + STEP)
                    term = dst_part[:, :, :]
                else:
                    v.wait_ge(dst_done, (k + 1) * CHUNK + STEP)
                    for bank in range(3):
                        tiles = min(TERM_TURNS * STEP, CHUNK - bank * TERM_TURNS * STEP)
                        s.done(v.tensor_reduce(terms[:, bank * TERM_TURNS * STEP:bank * TERM_TURNS * STEP + tiles, :],
                                               term_ps[bank][:, 0:tiles * 24].rearrange("p (t n h) -> p t h n", n=3, h=8),
                                               AX.X, ALU.add))
                    s.settled(v)
                    term = terms[:, :, :]
                s.done(v.tensor_tensor(zh, hr(rows[:, half, :, FEAT:FEAT + heads]), hr(term[:, :, 0:heads]), ALU.add))
                s.settled(v)
                s.done(v.scalar_tensor_tensor(out=z[:, :], in0=z[:, :], scalar=0.2, in1=z[:, :], op0=ALU.mult, op1=ALU.max))
                s.settled(v)
                if own_edge:
                    s.done(v.tensor_tensor(top[:, :].rearrange("p (h t) -> p h t", h=heads), zh, hr(term[:, :, 4:8]), ALU.max))
                    s.settled(v)
                v.sem_inc(z_ready, 1)
                breaks = g["break_f"][0:Q, bass.ds(k, 1), :].rearrange("q a e -> q (a e)")
                v.wait_ge(z_turned, k + 1)
                s.done(v.tensor_tensor_scan(scan_a[:, :], breaks, scan_ps[0:Q, :], -BIG, ALU.add, ALU.max))
                s.settled(v)
                v.sem_inc(ends_ready, 1)
                v.wait_ge(ends_row, k * 2 + 1)
                ends = small_ps[0:1, ROW_AT:ROW_AT + Q].rearrange("a (h c) -> a h c", h=heads)
                s.done(v.tensor_copy(chain_in[:, 0, :, 1:], ends))
                s.done(v.tensor_copy(chain_in[:, 0, :, 0], carried[:, half, :]))
                s.settled(v)
                s.done(v.tensor_tensor_scan(chain[:, 0, :, :].rearrange("a h c -> a (h c)"),
                                            g["chain_f"][:, bass.ds(k, 1), 0:heads, :].rearrange("a b h c -> a (b h c)"),
                                            chain_in[:, 0, :, :].rearrange("a h c -> a (h c)"), -BIG, ALU.add, ALU.max))
                s.settled(v)
                s.done(v.tensor_copy(chain_row[:, 0, :].rearrange("a (h c) -> a h c", h=heads), chain[:, 0, :, 0:SCAN_ROWS]))
                s.done(v.tensor_copy(carried[:, 1 - half, :], chain[:, 0, :, SCAN_ROWS]))
                s.settled(v)
                v.sem_inc(entry_ready, 1)
                v.wait_ge(entry_col, k * 2 + 1)
                s.done(v.tensor_copy(entry[:, :], small_ps[0:Q, COL_AT:COL_AT + 1]))
                s.settled(v)
                s.done(v.tensor_tensor_scan(scan_a[:, :], breaks, scan_ps[0:Q, :], entry[:, :], ALU.add, ALU.max))
                s.settled(v)
                breaks = g["break_b"][0:Q, bass.ds(k, 1), :].rearrange("q a e -> q (a e)")
                s.done(v.tensor_tensor_scan(scan_b[:, ::-1], breaks, scan_a[:, ::-1], -BIG, ALU.add, ALU.max))
                s.settled(v)
                v.sem_inc(ends_ready, 1)
                v.wait_ge(ends_row, k * 2 + 2)
                s.done(v.tensor_copy(chain_in[:, 1, :, 0:SCAN_ROWS], ends))
                s.settled(v)
                s.done(v.tensor_tensor_scan(chain[:, 1, :, :].rearrange("a h c -> a (h c)")[:, ::-1],
                                            g["chain_b"][:, bass.ds(k, 1), 0:heads, :].rearrange("a b h c -> a (b h c)"),
                                            chain_in[:, 1, :, :].rearrange("a h c -> a (h c)")[:, ::-1], -BIG, ALU.add, ALU.max))
                s.settled(v)
                s.done(v.tensor_copy(chain_row[:, 1, :].rearrange("a (h c) -> a h c", h=heads), chain[:, 1, :, 1:]))
                s.done(v.tensor_tensor(fall[:, :], carried[:, half, :], chain[:, 1, :, 0], ALU.subtract))
                s.settled(v)
                s.done(v.tensor_scalar(fall[:, :], fall[:, :], g["goes_on"][:, bass.ds(k, 1)], None, ALU.mult))
                s.settled(v)
                v.sem_inc(entry_ready, 1)
                v.wait_ge(entry_col, k * 2 + 2)
                s.done(v.tensor_copy(entry[:, :], small_ps[0:Q, COL_AT:COL_AT + 1]))
                s.settled(v)
                s.done(v.tensor_tensor_scan(scan_b[:, ::-1], breaks, scan_a[:, ::-1], entry[:, :], ALU.add, ALU.max))
                s.settled(v)
                v.sem_inc(top_ready, 1)
                v.reg_load(regs[0], g["tile_win"][0:1, 0, bass.ds(k * CHUNK, 1)])
                window = v.snap(regs[0], min_val=0, max_val=WINDOWS - 1)
                v.wait_ge(factor_ready, k + 1)
                v.wait_ge(sum_taken, k * CHUNK + STEP)
                a = acc[:, bass.ds(window, 1), :].rearrange("p a f -> p (a f)")
                s.done(v.tensor_tensor(a[:, 0:FEAT].rearrange("p (h d) -> p h d", h=heads),
                                       a[:, 0:FEAT].rearrange("p (h d) -> p h d", h=heads),
                                       factor[:, :].unsqueeze(2).to_broadcast([P, heads, D]), ALU.mult))
                s.done(v.tensor_tensor(a[:, FEAT:FEAT + heads], a[:, FEAT:FEAT + heads], factor[:, :], ALU.mult))
                s.settled(v)
                v.wait_ge(top_turned, k + 1)
                s.done(v.tensor_copy(top[:, :].rearrange("p (q b) -> p b q", b=SCAN_TILES),
                                     small_ps[:, 0:SCAN_TILES * Q].rearrange("p (b q) -> p b q", b=SCAN_TILES)))
                s.settled(v)
                s.done(v.tensor_tensor(z[:, :], z[:, :], top[:, :], ALU.subtract))
                s.settled(v)
                v.sem_inc(less_top, 1)
                if own_edge:
                    lasts = g["last"][:, bass.ds(k * CHUNK, CHUNK)]
                    s.done(v.tensor_tensor(hr(rows[:, half, :, 260:264]), top[:, :].rearrange("p (h t) -> p h t", h=heads),
                                           lasts.unsqueeze(1).to_broadcast([P, heads, CHUNK]), ALU.mult))
                    s.done(v.tensor_scalar(rows[:, half, :, ROW:ROW + 1].rearrange("p t a -> p (t a)"), lasts, 1.0, None, ALU.mult))
                    s.settled(v)
                assert s.n == CHAIN, s.n
                v.wait_ge(weights_made, k + 1)

                def weigh(turn):
                    r = rows[:, half, bass.ds(turn * STEP, STEP), :]
                    v.tensor_tensor(r[:, :, 0:FEAT].rearrange("p t (h d) -> p t h d", h=heads),
                                    r[:, :, 0:FEAT].rearrange("p t (h d) -> p t h d", h=heads),
                                    r[:, :, FEAT:FEAT + heads].unsqueeze(3).to_broadcast([P, STEP, heads, D]),
                                    ALU.mult).then_inc(weighted, 1)

                def turn_sums(turn, parity, windows, more):
                    tile = k * CHUNK + turn * STEP
                    if more:
                        weigh(turn + 1)
                    for j in range(STEP):
                        v.wait_ge(sum_made, tile + (j + 1 + AHEAD))
                        v.wait_ge(sum_taken, tile + (j + STEP))
                        a = acc[:, bass.ds(windows[j], 1), 0:width].rearrange("p a f -> p (a f)")
                        v.tensor_tensor(a, a, sum_ps[j][:, 0:width], ALU.add).then_inc(sum_taken, 1)

                weigh(0)
                each_turn(v, k, regs, g["tile_win"], turn_sums)

            each_chunk(v, chunk)


def build(nc, d, out, layers=5):
    dram = {}
    for name, shape, dt in (("src_win", [EDGES], F32), ("places", [EDGES], I32), ("records", [TILES * P, 2], I32),
                            ("keys", [TILES + 2, P], F32), ("slots", [TILES, P], F32), ("attrs", [4, TILES, P], F32), ("tile_win", [2, TILES], I32),
                            ("breaks", [2, SEG_ROWS, SCAN_LEN], BF16), ("rel_table_f", [NODES_PAD * RELS, FEAT], F32),
                            ("rel_table_b", [NODES_PAD * RELS, FEAT], F32),
                            ("nodes", [NODES_PAD, ROW], F32), ("x1", [NODES_PAD, FEAT], F32),
                            ("x2", [NODES_PAD, FEAT], F32)):
        dram[name] = nc.dram_tensor(f"dram_{name}", shape, dt, kind="Internal").ap()
    with ExitStack() as ctx:
        def sb(name, shape, dt=F32):
            return ctx.enter_context(nc.sbuf_tensor(name, shape, dt))

        cst = sb("cst", [P, C_COLS])
        g = {}
        g["landed"] = {tag: [ctx.enter_context(nc.semaphore(f"{tag}_landed{i}")) for i in range(2)]
                       for tag in ("group", "rel", "fwd", "bwd", "att0", "att1", "att2", "att3")}
        g["src_idx"] = sb("src_idx", [P, TILES], I32)
        g["dst_slot"] = sb("dst_slot", [P, TILES + STEP])
        g["tile_win"] = sb("tile_win", [1, 2, TILES], I32)
        with ExitStack() as relations:
            for name, shape, dt in (("fwd_idx", [P, TILES], I32), ("bwd_idx", [P, TILES], I32),
                                    ("src_slot", [P, TILES + STEP], F32), ("tile_win4", [QUARTERS, 2, QT], I32),
                                    ("win128", [QT, 2, QUARTERS], F32), ("record", [EP, EJ, 2], I32),
                                    ("pos_i", [EP, EJ], I32)):
                g[name] = relations.enter_context(nc.sbuf_tensor(name, shape, dt))
            group_edges(nc, "group", cst, d, dram, g)
            project_relations(nc, "rel", cst, d, dram, g)
            grouped_slots(nc, "slots", cst, dram, g)
            rows = relations.enter_context(nc.sbuf_tensor("rel_rows", [P, 2, CHUNK, COLS], F32))
            acc = relations.enter_context(nc.sbuf_tensor("acc_f", [P, WINDOWS, COLS], F32))
            acc_b = relations.enter_context(nc.sbuf_tensor("acc_b", [P, WINDOWS, COLS], F32))
            relation_edges(nc, 'fwd', cst, dram, g, rows, 0, acc)
            relation_edges(nc, 'bwd', cst, dram, g, rows, 1, acc_b)
            finish(nc, "fin0", cst, "relations", 1, d, dram, g, rows, acc, acc_b, None, d["x_pad"], dram["x1"],
                   ("L0_gnn_forward_bias", "L0_gnn_backward_bias", "L0_gnn_self_bias"), out if layers == 1 else None)
        g["break_f"] = sb("break_f", [8 * SCAN_ROWS, CHUNKS, SCAN_LEN], BF16)
        g["break_b"] = sb("break_b", [8 * SCAN_ROWS, CHUNKS, SCAN_LEN], BF16)
        g["chain_f"] = sb("chain_f", [1, CHUNKS, 8, SCAN_ROWS + 1], BF16)
        g["chain_b"] = sb("chain_b", [1, CHUNKS, 8, SCAN_ROWS + 1], BF16)
        g["goes_on"] = sb("goes_on", [1, CHUNKS])
        g["last"] = sb("last", [P, TILES])
        g["slot_rows"] = sb("slot_rows", [SEG_ROWS, SCAN_LEN], BF16)
        g["pick_row"] = sb("pick_row", [SEG_ROWS, SEG_ROWS], BF16)
        if layers > 1:
            scan_tables(nc, 'scan', cst, dram, g)
        for n, (kind, heads, x_from, rest, x_to, w, a, b, bias) in enumerate((
                ("edge", 8, "x1", "x1", "x2", "L1_gnn_W", "L1_gnn_a_src", "L1_gnn_a_dst", "L1_gnn_bias"),
                ("elu", 4, "x2", "x2", "x1", "L2_gnn_W1", "L2_gnn_att_src1", "L2_gnn_att_dst1", "L2_gnn_b1"),
                ("self", 4, "x1", "x2", "x1", "L2_gnn_W2", "L2_gnn_att_src2", "L2_gnn_att_dst2", "L2_gnn_b2"),
                ("plain", 8, "x1", "x1", "x2", "L3_gnn_W", "L3_gnn_a_src", "L3_gnn_a_dst", "L3_gnn_bias"))):
            if n + 2 > layers:
                break
            with ExitStack() as layer:
                nt = layer.enter_context(nc.sbuf_tensor(f"nt{n}", [P, WINDOWS, NTC], F32))
                project_nodes(nc, f'nodes{n}', cst, heads, kind in ("self", "elu"), d, dram, nt, dram[x_from], w, a, b)
                acc = layer.enter_context(nc.sbuf_tensor(f"acc{n}", [P, WINDOWS, COLS], F32))
                rows = layer.enter_context(nc.sbuf_tensor(f"rows{n}", [P, 2, CHUNK, COLS], F32))
                attention_edges(nc, f'att{n}', cst, kind, heads, d, dram, g, rows, acc, nt)
                finish(nc, f'fin{n + 1}', cst, kind, heads, d, dram, g, rows, acc, None, nt, dram[rest], dram[x_to], bias,
                       out if n + 2 == layers else None)


LAYERS = 5


def constants():
    import numpy as np
    c = np.zeros((P, C_COLS), np.float32)
    p = np.arange(EP)
    c[:, C_IDENT:C_IDENT + P] = np.eye(P)
    c[:, C_IOTA:C_IOTA + P] = np.arange(P)
    c[:, C_ONES:C_ONES + P] = 1
    c[:, C_ROW] = np.arange(P)
    c[:EP, C_BEFORE:C_BEFORE + EP] = (p[:, None] // PARTS == p // PARTS) & (p[:, None] < p)
    c[:EP, C_WINOH:C_WINOH + WINDOWS] = p[:, None] // PARTS == np.arange(WINDOWS)
    c[:EP, C_PART:C_PART + PARTS] = p[:, None] % PARTS == np.arange(PARTS)
    c[:EP, C_WIN] = p // PARTS
    c[:QT, C_TILE:C_TILE + QUARTERS] = np.arange(QT)[:, None] + QT * np.arange(QUARTERS)
    return c


def kernel(**inputs):
    import numpy as _np
    import concourse.bacc as _bacc
    from concourse import mybir as _mybir
    from concourse.bass_utils import run_bass_kernel_spmd as _run

    def padded(a, value):
        return _np.concatenate([a, _np.full((P,) + a.shape[1:], value, a.dtype)])

    inputs = {name: _np.asarray(a) for name, a in inputs.items()}
    given = {name: inputs[name] for name in (
        "src", "dst", "edge_type_16", "L0_gnn_Wf", "L0_gnn_Wb", "L0_gnn_loop_weight", "L0_gnn_forward_bias",
        "L0_gnn_backward_bias", "L0_gnn_self_bias", "L1_gnn_edge_b", "L1_gnn_bias", "L2_gnn_W1", "L2_gnn_b1",
        "L2_gnn_W2", "L2_gnn_b2", "L3_gnn_bias")}
    for name in ("L1_gnn_a_src", "L1_gnn_a_dst", "L2_gnn_att_src1", "L2_gnn_att_dst1", "L2_gnn_att_src2",
                 "L2_gnn_att_dst2", "L3_gnn_a_src", "L3_gnn_a_dst"):
        given[name] = inputs[name].reshape(-1)
    for name in ("L1_gnn_W", "L1_gnn_edge_W", "L3_gnn_W"):
        given[name] = inputs[name].T
    x = inputs["x"]
    given["x_pad"] = _np.concatenate([x, _np.zeros((NODES_PAD - NODES, FEAT), x.dtype)])
    given["src_pad"] = padded(inputs["src"], 0)
    given["dst_pad"] = padded(inputs["dst"], int(FAR))
    given["type_pad"] = padded(inputs["edge_type_16"], 0)
    for i in range(3):
        given[f"attr{i}"] = padded(inputs["edge_attr_3"][:, i], 0)
    given["consts"] = constants()

    nc = _bacc.Bacc("TRN2", target_bir_lowering=False, num_devices=1)
    arrays, d = {}, {}
    for name, a in given.items():
        a = _np.ascontiguousarray(a)
        arrays[f"in_{name}"] = a
        d[name] = nc.dram_tensor(f"in_{name}", a.shape, _mybir.dt.from_np(a.dtype), kind="ExternalInput").ap()
    out = nc.dram_tensor("out", (NODES, FEAT), F32, kind="ExternalOutput").ap()
    build(nc, d, out, LAYERS)
    r = _run(nc, [arrays], core_ids=[0])
    return r.results[0]["out"]
```

```python
from contextlib import ExitStack

import concourse.bass as bass
from concourse import mybir

ALU = mybir.AluOpType
ACT = mybir.ActivationFunctionType
AX = mybir.AxisListType
F32 = mybir.dt.float32
BF16 = mybir.dt.bfloat16
I32 = mybir.dt.int32

P = 128
NODES = 3125
EDGES = 53125
FEAT = 256
RELS = 16
WINDOWS = -(-NODES // P)
NODES_PAD = WINDOWS * P
CHUNK = 44
CHUNKS = 10
TILES = CHUNK * CHUNKS
assert EDGES // P + WINDOWS <= TILES
SCAN_ROWS = 11
SCAN_TILES = CHUNK // SCAN_ROWS
SCAN_LEN = SCAN_TILES * P
EP, EJ = 125, 425
assert EP * EJ == EDGES
PARTS = EP // WINDOWS
PART_LEN = EDGES // PARTS
QUARTERS = 4
QT = TILES // QUARTERS
SEG_ROWS = CHUNKS * SCAN_ROWS
ROW = 264
COLS = 266
NTC = 272
STEP = 4
TURNS = CHUNK // STEP
BIG = 1e30
EPS = 1e-5
FAR = float(1 << 20)

C_IDENT, C_IOTA, C_ONES, C_BEFORE, C_WINOH, C_PART, C_WIN, C_TILE, C_ROW = 0, 128, 256, 384, 509, 534, 539, 540, 544
C_COLS = 545


class Steps:

    def __init__(self, sem, base=0):
        self.sem, self.base, self.n = sem, base, 0

    def done(self, instruction):
        instruction.then_inc(self.sem, 1)
        self.n += 1

    def settled(self, engine):
        if self.n or not isinstance(self.base, int):
            engine.wait_ge(self.sem, self.base + self.n)


def phase_semaphores(nc, tag, ctx):
    sems = []

    def sem(name):
        sems.append(nc.alloc_semaphore(f"{tag}_{name}"))
        return sems[-1]

    ctx.callback(nc.all_engine_barrier)
    ctx.callback(nc.clear_and_free_semaphores, sems)
    return sem


def each_window(engine, body):
    with engine.Fori(0, WINDOWS // 2) as i:
        body(i * 2, 0)
        body(i * 2 + 1, 1)
    body(WINDOWS - 1, 0)


def split_bf16(v, whole, parts, rest, split):
    for n, part in enumerate(parts):
        v.tensor_copy(part, whole).then_inc(split, 1)
        if n < 2:
            v.wait_ge(split, 2 * n + 1)
            v.tensor_tensor(rest, whole, part, ALU.subtract).then_inc(split, 1)
            v.wait_ge(split, 2 * n + 2)
            whole = rest


def group_edges(nc, tag, cst, d, dram, g, nt):
    with ExitStack() as ctx:
        def sb(name, shape, dt=F32):
            return ctx.enter_context(nc.sbuf_tensor(f"{tag}_{name}", shape, dt))

        sem = phase_semaphores(nc, tag, ctx)

        rows_ps = ctx.enter_context(nc.psum_tensor(f"{tag}_rows_ps", [P, 512], F32))
        parts_ps = ctx.enter_context(nc.psum_tensor(f"{tag}_parts_ps", [P, 512], F32))
        pos_ps = [ctx.enter_context(nc.psum_tensor(f"{tag}_pos_ps{i}", [P, 512], F32)) for i in range(2)]
        lane_ps = [ctx.enter_context(nc.psum_tensor(f"{tag}_lane_ps{i}", [P, 512], F32)) for i in range(2)]

        src_e = sb("src_e", [EP, EJ], I32)
        dst_e = sb("dst_e", [EP, EJ], I32)
        typ_e = sb("typ_e", [EP, EJ], I32)
        flt_e = sb("flt_e", [EP, EJ])
        cmp_e = sb("cmp_e", [EP, EJ])
        win_i = sb("win_i", [EP, EJ], I32)
        win_f = sb("win_f", [EP, EJ])
        below = sb("below", [EP, WINDOWS + 1])
        hit = sb("hit", [EP, PART_LEN])
        rank = sb("rank", [EP, PART_LEN])
        place = sb("place", [PARTS, PART_LEN], I32)
        total = sb("total", [EP, 1])
        total_b = sb("total_b", [EP, P])
        base = sb("base", [EP, 1])
        pick = sb("pick", [EP, WINDOWS])
        zeros = sb("zeros", [P, WINDOWS])
        start = sb("start", [P, 2, WINDOWS + 1])
        n_i = sb("n_i", [P, 2, WINDOWS], I32)
        n_t = sb("n_t", [P, 2, WINDOWS])
        last_t = sb("last_t", [P, 2, WINDOWS])
        first_t = sb("first_t", [P, 2, WINDOWS])
        shift = sb("shift", [P, WINDOWS])
        jump = sb("jump", [P, WINDOWS])
        ge = sb("ge", [P, WINDOWS])
        gej = sb("gej", [P, WINDOWS])
        win_t = sb("win_t", [QT, 2, QUARTERS])
        win128, record, pos_i = g["win128"], g["record"], g["pos_i"]
        off_f = sb("off_f", [QT, QUARTERS])
        off_i = sb("off_i", [QT, QUARTERS], I32)
        pad = sb("pad", [P, TILES, 2], I32)
        r_dst = sb("r_dst", [QT, QUARTERS, P], I32)
        r_src = sb("r_src", [QT, QUARTERS, P], I32)
        r_typ = sb("r_typ", [QT, QUARTERS, P], I32)
        lanes = nt[0:QT, :, :].rearrange("q w c -> q (w c)")[:, 0:12 * QUARTERS * P]\
            .rearrange("q (n b e) -> q n b e", n=12, b=QUARTERS)
        r_att, att_rest = lanes[:, 0:3, :, :], lanes[:, 3:6, :, :]
        f_dst, f_src, f_idx, f_loc, f_val, f_key = [lanes[:, n, :, :] for n in range(6, 12)]
        att_part = sb("att_part", [QT, 3, 4, QUARTERS, P], BF16)
        edge_key = sb("edge_key", [1, P])

        loaded = sem("loaded")
        windows_out = sem("windows_out")
        windows_in = sem("windows_in")
        pad_out = sem("pad_out")
        places_out = sem("places_out")
        places_in = sem("places_in")
        blocks_in = g["landed"][tag][0]
        keys_out = sem("keys_out")
        rows_in = sem("rows_in")
        vec = sem("vec")
        src_windows = sem("src_windows")
        records_made = sem("records_made")
        pad_made = sem("pad_made")
        below_made = sem("below_made")
        total_made = sem("total_made")
        counts_done = sem("counts_done")
        parts_done = sem("parts_done")
        rank_made = sem("rank_made")
        sums_done = sem("sums_done")
        sums_taken = sem("sums_taken")
        offsets_made = sem("offsets_made")
        keys_made = sem("keys_made")
        lanes_ready = sem("lanes_ready")
        attrs_split = sem("attrs_split")
        lanes_done = sem("lanes_done")
        lanes_taken = sem("lanes_taken")
        pieces = [(a, min(512, PART_LEN - a)) for a in range(0, PART_LEN, 512)]

        block = ctx.enter_context(nc.Block())

        @block.sync
        def _(sp):
            sp.dma_start(cst[:, :], d["consts"]).then_inc(loaded, 16)
            sp.dma_start(src_e[:, :], d["src"].rearrange("(p j) -> p j", p=EP)).then_inc(loaded, 16)
            sp.dma_start(dst_e[:, :], d["dst"].rearrange("(p j) -> p j", p=EP)).then_inc(loaded, 16)
            sp.dma_start(typ_e[:, :], d["edge_type_16"].rearrange("(p j) -> p j", p=EP)).then_inc(loaded, 16)
            sp.wait_ge(src_windows, 1)
            sp.dma_start(dram["src_win"].rearrange("(p j) -> p j", p=EP), win_f[:, :]).then_inc(windows_out, 16)
            sp.wait_ge(windows_out, 16)
            for w in range(WINDOWS):
                sp.dma_start(hit[w * PARTS:(w + 1) * PARTS, :],
                             dram["src_win"].rearrange("(c j) -> c j", c=PARTS)).then_inc(windows_in, 16)
            sp.wait_ge(pad_made, 2)
            sp.dma_start(dram["records"].rearrange("(p t) c -> p t c", p=P), pad[:, :, :]).then_inc(pad_out, 16)
            sp.wait_ge(keys_made, 1)
            for q in range(QUARTERS):
                sp.dma_start(dram["keys"][1 + q * QT:1 + (q + 1) * QT, :], f_key[:, q, :]).then_inc(keys_out, 16)
                sp.dma_start(dram["slots"][q * QT:(q + 1) * QT, :], f_loc[:, q, :]).then_inc(keys_out, 16)
            for row in (0, TILES + 1):
                sp.dma_start(dram["keys"][row:row + 1, :], edge_key[:, :]).then_inc(keys_out, 16)
            sp.wait_ge(sums_taken, len(pieces))
            sp.dma_start(dram["places"].rearrange("(c j) -> c j", c=PARTS), place[:, :]).then_inc(places_out, 16)
            sp.wait_ge(places_out, 16)
            sp.dma_start(pos_i[:, :], dram["places"].rearrange("(p j) -> p j", p=EP)).then_inc(places_in, 16)
            sp.wait_ge(lanes_taken, 4)
            for way in range(2):
                sp.dma_start(dram["tile_win"][way].rearrange("(q p) -> q p", q=QUARTERS),
                             g["tile_win4"][:, way, :]).then_inc(rows_in, 16)
            sp.wait_ge(rows_in, 32)
            sp.dma_start(g["tile_win"][:, :, :], dram["tile_win"].rearrange("(a w) t -> a w t", a=1)).then_inc(rows_in, 16)
            sp.wait_ge(attrs_split, 5)
            for n in range(3):
                for a in range(4):
                    sp.dma_start(dram["attrs"][n * 4 + a].rearrange("(q p) e -> p q e", p=QT), att_part[:, n, a, :, :])\
                        .then_inc(keys_out, 16)
            sp.wait_ge(keys_out, 16 * (2 * QUARTERS + 2 + 3 * 4))
            sp.wait_ge(rows_in, 48)
            sp.wait_ge(pad_out, 16)
            sp.wait_ge(places_in, 16)

        @block.gpsimd
        def _(gp):
            gp.wait_ge(offsets_made, 1)
            for q in range(QUARTERS):
                at = bass.IndirectOffsetOnAxis(ap=off_i[:, q:q + 1], axis=1)
                for flat, to in ((d["dst_pad"], r_dst[:, q, :]), (d["src_pad"], r_src[:, q, :]),
                                 (d["type_pad"], r_typ[:, q, :]), (d["attr0"], r_att[:, 0, q, :]),
                                 (d["attr1"], r_att[:, 1, q, :]), (d["attr2"], r_att[:, 2, q, :])):
                    gp.indirect_dma_start(out=to, out_offset=None, in_=flat.rearrange("(a b) -> a b", a=1),
                                          in_offset=at).then_inc(blocks_in, 16)

        @block.tensor
        def _(pe):
            ones = cst[0:EP, C_ONES:C_ONES + P]
            pe.wait_ge(below_made, 1)
            pe.matmul(rows_ps[:, 0:WINDOWS + 1], ones, below[:, :], start=True, stop=True).then_inc(counts_done, 1)
            pe.wait_ge(total_made, 1)
            pe.matmul(rows_ps[:, 64:64 + WINDOWS], total_b[:, :], cst[0:EP, C_WINOH:C_WINOH + WINDOWS],
                      start=True, stop=True)
            pe.matmul(rows_ps[0:EP, 128:129], cst[0:EP, C_BEFORE:C_BEFORE + EP], total[:, :],
                      start=True, stop=True).then_inc(parts_done, 1)

            def lanes(n, views):
                pe.wait_ge(lanes_ready, n + 1)
                if n >= 2:
                    pe.wait_ge(lanes_taken, n - 1)
                for q, v in enumerate(views):
                    k, m = v.shape[0], v.shape[1]
                    mm = pe.transpose(lane_ps[n % 2][0:m, q * QT:q * QT + k], v, cst[0:k, C_IDENT:C_IDENT + k])
                mm.then_inc(lanes_done, 1)

            lanes(0, [win_t[:, 0, :]])
            lanes(1, [f_loc[:, q, :] for q in range(QUARTERS)])
            lanes(2, [f_src[:, q, :] for q in range(QUARTERS)])
            lanes(3, [win_t[:, 1, :]])
            lanes(4, [f_idx[:, q, :] for q in range(QUARTERS)])
            pe.wait_ge(rank_made, 1)
            for n, (a, m) in enumerate(pieces):
                if n >= 2:
                    pe.wait_ge(sums_taken, n - 1)
                pe.matmul(pos_ps[n % 2][0:PARTS, 0:m], cst[0:EP, C_PART:C_PART + PARTS], rank[:, a:a + m],
                          start=True, stop=True).then_inc(sums_done, 1)

        @block.scalar
        def _(act):
            for n, (a, m) in enumerate(pieces):
                act.wait_ge(sums_done, n + 1)
                act.copy(place[:, a:a + m], pos_ps[n % 2][0:PARTS, 0:m]).then_inc(sums_taken, 1)

        @block.vector
        def _(v):
            s = Steps(vec)
            v.memset(zeros[:, :], 0.0).then_inc(vec, 1)
            s.n += 1
            s.done(v.memset(below[:, 0:1], 0.0))
            s.done(v.memset(below[:, WINDOWS:WINDOWS + 1], float(EJ)))
            s.done(v.memset(edge_key[:, :], -2.0))
            s.done(v.memset(g["dst_slot"][:, TILES:], -1.0))
            s.done(v.memset(g["src_slot"][:, TILES:], -1.0))
            s.done(v.memset(att_part[:, 0, 3, :, :], 1.0))
            s.done(v.memset(att_part[:, 1:3, 3, :, :], 0.0))
            v.memset(pad[:, :, 0], -1).then_inc(pad_made, 1)
            v.memset(pad[:, :, 1], 0).then_inc(pad_made, 1)
            v.wait_ge(loaded, 64)
            s.done(v.tensor_scalar(win_i[:, :], src_e[:, :], 7, None, ALU.logical_shift_right))
            s.settled(v)
            v.tensor_copy(win_f[:, :], win_i[:, :]).then_inc(src_windows, 1)
            v.tensor_copy(record[:, :, 0], src_e[:, :]).then_inc(records_made, 1)
            v.scalar_tensor_tensor(out=record[:, :, 1], in0=dst_e[:, :], scalar=float(RELS), in1=typ_e[:, :],
                                   op0=ALU.mult, op1=ALU.add).then_inc(records_made, 1)
            s.done(v.tensor_copy(flt_e[:, :], dst_e[:, :]))
            s.settled(v)
            for w in range(1, WINDOWS):
                s.done(v.tensor_scalar(cmp_e[:, :], flt_e[:, :], float(w * P), None, ALU.is_lt))
                s.settled(v)
                s.done(v.tensor_reduce(below[:, w:w + 1], cmp_e[:, :], AX.X, ALU.add))
                s.settled(v)
            v.sem_inc(below_made, 1)

            def tiles_of(way):
                n = start[:, way, 1:] if way == 0 else start[:, way, 0:WINDOWS]
                if way == 0:
                    s.done(v.tensor_tensor(n_t[:, way, :], n, start[:, way, 0:WINDOWS], ALU.subtract))
                    s.settled(v)
                    n = n_t[:, way, :]
                s.done(v.tensor_scalar(n_i[:, way, :], n, float(P - 1), None, ALU.add))
                s.settled(v)
                s.done(v.tensor_scalar(n_i[:, way, :], n_i[:, way, :], 7, None, ALU.logical_shift_right))
                s.settled(v)
                s.done(v.tensor_scalar(n_t[:, way, :], n_i[:, way, :], 1.0, None, ALU.max))
                s.settled(v)
                s.done(v.tensor_tensor_scan(last_t[:, way, :], zeros[:, :], n_t[:, way, :], 0.0, ALU.add, ALU.add))
                s.settled(v)
                s.done(v.tensor_tensor(first_t[:, way, :], last_t[:, way, :], n_t[:, way, :], ALU.subtract))
                s.settled(v)

            def window_of_tiles(way):
                for q in range(QUARTERS):
                    tile = cst[0:QT, C_TILE + q:C_TILE + q + 1]
                    s.done(v.tensor_scalar(ge[0:QT, :], first_t[0:QT, way, :], tile, None, ALU.is_le))
                    s.settled(v)
                    s.done(v.tensor_reduce(win_t[:, way, q:q + 1], ge[0:QT, :], AX.X, ALU.add))
                    if way == 0:
                        s.done(v.tensor_tensor(gej[0:QT, :], ge[0:QT, :], jump[0:QT, :], ALU.mult))
                        s.settled(v)
                        s.done(v.tensor_reduce(off_f[:, q:q + 1], gej[0:QT, :], AX.X, ALU.add))
                    s.settled(v)
                s.done(v.tensor_scalar(win_t[:, way, :], win_t[:, way, :], -1.0, None, ALU.add))
                s.settled(v)
                s.done(v.tensor_scalar(win128[:, way, :], win_t[:, way, :], float(P), None, ALU.mult))
                s.settled(v)

            v.wait_ge(counts_done, 1)
            s.done(v.tensor_copy(start[:, 0, :], rows_ps[:, 0:WINDOWS + 1]))
            s.settled(v)
            tiles_of(0)
            s.done(v.scalar_tensor_tensor(out=shift[:, :], in0=first_t[:, 0, :], scalar=-float(P),
                                          in1=start[:, 0, 0:WINDOWS], op0=ALU.mult, op1=ALU.add))
            s.settled(v)
            s.done(v.tensor_copy(jump[:, 0:1], shift[:, 0:1]))
            s.done(v.tensor_tensor(jump[:, 1:], shift[:, 1:], shift[:, 0:WINDOWS - 1], ALU.subtract))
            s.settled(v)
            window_of_tiles(0)
            v.sem_inc(lanes_ready, 1)
            s.done(v.scalar_tensor_tensor(out=off_f[:, :], in0=cst[0:QT, C_TILE:C_TILE + QUARTERS], scalar=float(P),
                                          in1=off_f[:, :], op0=ALU.mult, op1=ALU.add))
            s.settled(v)
            v.tensor_scalar(off_i[:, :], off_f[:, :], float(EDGES), None, ALU.min).then_inc(offsets_made, 1)

            v.wait_ge(windows_in, 16 * WINDOWS)
            s.done(v.tensor_scalar(hit[:, :], hit[:, :], cst[0:EP, C_WIN:C_WIN + 1], None, ALU.is_equal))
            s.settled(v)
            s.done(v.tensor_tensor_scan(rank[:, :], hit[:, :], hit[:, :], 0.0, ALU.add, ALU.bypass))
            s.settled(v)
            s.done(v.tensor_copy(total[:, :], rank[:, PART_LEN - 1:PART_LEN]))
            s.settled(v)
            s.done(v.tensor_scalar(total_b[:, :], cst[0:EP, C_ONES:C_ONES + P], total[:, :], None, ALU.mult))
            s.settled(v)
            v.sem_inc(total_made, 1)

            v.wait_ge(lanes_done, 1)
            s.done(v.tensor_copy(g["tile_win4"][:, 0, :], lane_ps[0][0:QUARTERS, 0:QT]))
            s.settled(v)
            v.sem_inc(lanes_taken, 1)
            v.wait_ge(blocks_in, 16 * 6 * QUARTERS)
            s.done(v.tensor_copy(f_dst[:, :, :], r_dst[:, :, :]))
            s.done(v.tensor_copy(f_src[:, :, :], r_src[:, :, :]))
            s.settled(v)
            for q in range(QUARTERS):
                s.done(v.tensor_scalar(f_loc[:, q, :], f_dst[:, q, :], win128[:, 0, q:q + 1], None, ALU.subtract))
            s.settled(v)
            v.sem_inc(lanes_ready, 2)
            s.done(v.tensor_scalar(f_val[:, :, :], f_loc[:, :, :], 0.0, None, ALU.is_ge))
            s.settled(v)
            s.done(v.scalar_tensor_tensor(out=f_val[:, :, :], in0=f_loc[:, :, :], scalar=float(P), in1=f_val[:, :, :],
                                          op0=ALU.is_lt, op1=ALU.mult))
            s.settled(v)
            s.done(v.scalar_tensor_tensor(out=f_key[:, :, :], in0=f_dst[:, :, :], scalar=1.0, in1=f_val[:, :, :],
                                          op0=ALU.add, op1=ALU.mult))
            s.settled(v)
            v.tensor_scalar(f_key[:, :, :], f_key[:, :, :], -1.0, None, ALU.add).then_inc(keys_made, 1)
            s.done(v.scalar_tensor_tensor(out=f_idx[:, :, :], in0=f_src[:, :, :], scalar=float(RELS), in1=r_typ[:, :, :],
                                          op0=ALU.mult, op1=ALU.add))
            s.settled(v)

            v.wait_ge(parts_done, 1)
            s.done(v.tensor_copy(start[:, 1, 0:WINDOWS], rows_ps[:, 64:64 + WINDOWS]))
            s.done(v.tensor_copy(base[:, :], rows_ps[0:EP, 128:129]))
            s.settled(v)
            tiles_of(1)
            window_of_tiles(1)
            s.done(v.tensor_tensor(pick[:, :], cst[0:EP, C_WINOH:C_WINOH + WINDOWS], first_t[0:EP, 1, :], ALU.mult))
            s.settled(v)
            s.done(v.tensor_reduce(total[:, :], pick[:, :], AX.X, ALU.add))
            s.settled(v)
            s.done(v.scalar_tensor_tensor(out=base[:, :], in0=total[:, :], scalar=float(P), in1=base[:, :],
                                          op0=ALU.mult, op1=ALU.add))
            s.settled(v)
            s.done(v.tensor_scalar(base[:, :], base[:, :], -1.0, None, ALU.add))
            s.settled(v)
            v.scalar_tensor_tensor(out=rank[:, :], in0=rank[:, :], scalar=base[:, 0:1], in1=hit[:, :],
                                   op0=ALU.add, op1=ALU.mult).then_inc(rank_made, 1)

            def take(n, out):
                v.wait_ge(lanes_done, n + 1)
                k = out.shape[0]
                v.tensor_copy(out, lane_ps[n % 2][0:k, 0:out.shape[1]]).then_inc(lanes_taken, 1)

            take(1, g["dst_slot"][:, 0:TILES])
            take(2, g["src_idx"][:, :])
            v.sem_inc(lanes_ready, 2)
            take(3, g["tile_win4"][:, 1, :])
            take(4, g["fwd_idx"][:, :])
            split_bf16(v, r_att[:, :, :, :], [att_part[:, n, 0:3, :, :] for n in range(3)], att_rest[:, :, :, :], attrs_split)


def project_relations(nc, tag, cst, d, dram, g):
    with ExitStack() as ctx:
        def sb(name, shape, dt=F32):
            return ctx.enter_context(nc.sbuf_tensor(f"{tag}_{name}", shape, dt))

        sem = phase_semaphores(nc, tag, ctx)

        w_sb = sb("w_sb", [P, 2, 2, RELS, FEAT])
        xw = sb("xw", [P, 2, FEAT])
        xt = sb("xt", [P, 2, 2, P])
        stage = sb("stage", [P, 4, RELS // 2, FEAT])
        xt_ps = [ctx.enter_context(nc.psum_tensor(f"{tag}_xt_ps{i}", [P, 512], F32)) for i in range(2)]
        out_ps = [ctx.enter_context(nc.psum_tensor(f"{tag}_out_ps{i}", [P, 512], F32)) for i in range(4)]
        w_in = sem("w_in")
        x_in = [sem(f"x_in{i}") for i in range(2)]
        x_used = sem("x_used")
        xt_done = sem("xt_done")
        xt_taken = sem("xt_taken")
        xt_used = sem("xt_used")
        out_done = sem("out_done")
        out_taken = [sem("taken_vector"), sem("taken_scalar")]
        stored = [sem(f"stored{i}") for i in range(4)]
        stage_free = [sem(f"stage_free{i}") for i in range(4)]
        PAIRS = RELS
        AHEAD = 2
        block = ctx.enter_context(nc.Block())

        @block.sync
        def _(sp):
            for st in range(4):
                sp.sem_inc(stage_free[st], 1)
            for way, name in enumerate(("L0_gnn_Wf", "L0_gnn_Wb")):
                for r in range(RELS):
                    sp.dma_start(w_sb[:, way, :, r, :], d[name][r].rearrange("(k p) n -> p k n", p=P)).then_inc(w_in, 16)

            def load(w, par):
                sp.wait_ge(xt_done, w + AHEAD - 1)
                sp.dma_start(xw[:, par, :], d["x_pad"][bass.ds(w * P, P), :]).then_inc(x_in[par], 16)

            def store(w, par):
                for st in range(4):
                    way, half = st // 2, st % 2
                    for s in out_taken:
                        sp.wait_ge(s, w * (PAIRS // 2) + 2 * (st + 1) + AHEAD)
                    sp.dma_start(dram[("rel_table_f", "rel_table_b")[way]].rearrange("(n r) f -> n r f", r=RELS)
                                 [bass.ds(w * P, P), half * 8:half * 8 + 8, :],
                                 stage[:, st, :, :]).then_inc(stored[st], 16)
                for st in range(4):
                    sp.wait_ge(stored[st], (w + 1) * 16)
                    sp.sem_inc(stage_free[st], 1)

            load(0, 0)
            load(1, 1)
            with sp.Fori(0, WINDOWS // 2 - 1) as i:
                load(i * 2 + 2, 0)
                store(i * 2, 0)
                load(i * 2 + 3, 1)
                store(i * 2 + 1, 1)
            load(WINDOWS - 1, 0)
            for w in range(WINDOWS - 3, WINDOWS):
                store(w, w % 2)

        @block.gpsimd
        def _(gp):
            for j in range(EJ):
                gp.indirect_dma_start(out=dram["records"],
                                      out_offset=bass.IndirectOffsetOnAxis(ap=g["pos_i"][:, j:j + 1], axis=0),
                                      in_=g["record"][:, j, :], in_offset=None).then_inc(g["landed"][tag][0], 16)
            gp.wait_ge(g["landed"][tag][0], 16 * EJ)

        @block.tensor
        def _(pe):
            pe.sem_inc(xt_done, AHEAD)
            pe.sem_inc(out_done, AHEAD * PAIRS)
            pe.wait_ge(w_in, 16 * 2 * RELS)

            def turn_x(w, par):
                pe.wait_ge(x_in[par], (w + (2 - par)) * 8)
                pe.wait_ge(xt_taken, w + 1)
                for k in range(2):
                    mm = pe.transpose(xt_ps[par][:, k * P:(k + 1) * P], xw[:, par, k * P:(k + 1) * P],
                                      cst[:, C_IDENT:C_IDENT + P])
                mm.then_inc(xt_done, 1)

            def products(w, par):
                pe.wait_ge(xt_taken, w + 1 + AHEAD)
                for n in range(PAIRS):
                    way, r = n // 8, 2 * (n % 8)
                    pe.wait_ge(out_taken[n % 2], w * (PAIRS // 2) + n // 2 - 1 + AHEAD)
                    for k in range(2):
                        mm = pe.matmul(out_ps[n % 4][:, :], xt[:, par, k, :],
                                       w_sb[:, way, k, r:r + 2, :].rearrange("p r f -> p (r f)"),
                                       start=(k == 0), stop=(k == 1))
                    mm.then_inc(out_done, 1)

            turn_x(0, 0)
            with pe.Fori(0, WINDOWS // 2) as i:
                turn_x(i * 2 + 1, 1)
                products(i * 2, 0)
                turn_x(i * 2 + 2, 0)
                products(i * 2 + 1, 1)
            products(WINDOWS - 1, 0)

        def take(eng, copy, lane):
            def body(w, par):
                for n in range(lane, PAIRS, 2):
                    st = n // 4
                    eng.wait_ge(out_done, (w + AHEAD) * PAIRS + n + 1)
                    if n % 4 < 2:
                        eng.wait_ge(stage_free[st], w + 1)
                    copy(stage[:, st, 2 * (n % 4):2 * (n % 4) + 2, :].rearrange("p r f -> p (r f)"),
                         out_ps[n % 4][:, :]).then_inc(out_taken[lane], 1)
            return body

        @block.vector
        def _(v):
            v.sem_inc(out_taken[0], AHEAD)
            each_window(v, take(v, v.tensor_copy, 0))

        @block.scalar
        def _(act):
            act.sem_inc(out_taken[1], AHEAD)
            act.sem_inc(xt_taken, AHEAD)
            odd_banks = take(act, act.copy, 1)

            def take_x(w, par):
                act.wait_ge(xt_done, w + 1 + AHEAD)
                act.wait_ge(out_done, (w + AHEAD - 1) * PAIRS)
                act.copy(xt[:, par, :, :].rearrange("p k e -> p (k e)"), xt_ps[par][:, 0:2 * P]).then_inc(xt_taken, 1)

            take_x(0, 0)
            with act.Fori(0, WINDOWS // 2) as i:
                take_x(i * 2 + 1, 1)
                odd_banks(i * 2, 0)
                take_x(i * 2 + 2, 0)
                odd_banks(i * 2 + 1, 1)
            odd_banks(WINDOWS - 1, 0)


def grouped_slots(nc, tag, cst, dram, g):
    with ExitStack() as ctx:
        def sb(name, shape, dt=F32):
            return ctx.enter_context(nc.sbuf_tensor(f"{tag}_{name}", shape, dt))

        sem = phase_semaphores(nc, tag, ctx)
        rec = sb("rec", [QT, QUARTERS, P, 2], I32)
        field = sb("field", [QT, 2, QUARTERS, P])
        lane_ps = [ctx.enter_context(nc.psum_tensor(f"{tag}_lane_ps{i}", [P, 512], F32)) for i in range(2)]
        records_in = sem("records_in")
        fields_made = sem("fields_made")
        lanes_done = sem("lanes_done")
        lanes_taken = sem("lanes_taken")
        block = ctx.enter_context(nc.Block())

        @block.sync
        def _(sp):
            sp.dma_start(rec[:, :, :, :], dram["records"].rearrange("(q p e) c -> p q e c", q=QUARTERS, p=QT))\
                .then_inc(records_in, 16)

        @block.tensor
        def _(pe):
            pe.wait_ge(fields_made, 2 * QUARTERS)
            for i in range(2):
                for q in range(QUARTERS):
                    mm = pe.transpose(lane_ps[i][:, q * QT:(q + 1) * QT], field[:, i, q, :], cst[0:QT, C_IDENT:C_IDENT + QT])
                mm.then_inc(lanes_done, 1)

        @block.vector
        def _(v):
            v.wait_ge(records_in, 16)
            for q in range(QUARTERS):
                v.tensor_scalar(field[:, 0, q, :], rec[:, q, :, 0], g["win128"][:, 1, q:q + 1], None, ALU.subtract)\
                    .then_inc(fields_made, 1)
                v.tensor_copy(field[:, 1, q, :], rec[:, q, :, 1]).then_inc(fields_made, 1)
            for i, out in enumerate((g["src_slot"][:, 0:TILES], g["bwd_idx"][:, :])):
                v.wait_ge(lanes_done, i + 1)
                v.tensor_copy(out, lane_ps[i][:, 0:TILES]).then_inc(lanes_taken, 1)
            v.wait_ge(lanes_taken, 2)


def scan_tables(nc, tag, cst, dram, g):
    with ExitStack() as ctx:
        def sb(name, shape, dt=F32):
            return ctx.enter_context(nc.sbuf_tensor(f"{tag}_{name}", shape, dt))

        sem = phase_semaphores(nc, tag, ctx)

        key = sb("key", [SEG_ROWS, 3, SCAN_LEN])
        slots = sb("slots", [SEG_ROWS, SCAN_LEN])
        brk = sb("brk", [SEG_ROWS, 2, SCAN_LEN])
        brk_h = sb("brk_h", [SEG_ROWS, 2, SCAN_LEN], BF16)
        last = sb("last", [SEG_ROWS, SCAN_LEN])
        col = sb("col", [SEG_ROWS, 3])
        rows_ps = ctx.enter_context(nc.psum_tensor(f"{tag}_rows_ps", [P, 512], F32))
        last_ps = ctx.enter_context(nc.psum_tensor(f"{tag}_last_ps", [P, 512], F32))
        keys_in = sem("keys_in")
        vec = sem("vec")
        made = sem("made")
        turned = sem("turned")
        breaks_out = sem("breaks_out")
        breaks_in = sem("breaks_in")
        block = ctx.enter_context(nc.Block())

        @block.sync
        def _(sp):
            line = dram["keys"].rearrange("t e -> (t e)")
            for i, by in enumerate((0, -1, 1)):
                sp.dma_start(key[:, i, :], line[P + by:P + by + TILES * P].rearrange("(r e) -> r e", r=SEG_ROWS))\
                    .then_inc(keys_in, 16)
            sp.dma_start(slots[:, :], dram["slots"].rearrange("(r b) e -> r (b e)", b=SCAN_TILES)).then_inc(keys_in, 16)
            sp.wait_ge(made, 1)
            sp.wait_ge(made, 2)
            for way in range(2):
                sp.dma_start(dram["breaks"][way], brk_h[:, way, :]).then_inc(breaks_out, 16)
            sp.wait_ge(breaks_out, 32)
            for way, to in enumerate((g["break_f"], g["break_b"])):
                for h in range(8):
                    sp.dma_start(to[h * SCAN_ROWS:(h + 1) * SCAN_ROWS, :, :],
                                 dram["breaks"][way].rearrange("(k c) e -> c k e", c=SCAN_ROWS)).then_inc(breaks_in, 16)
            sp.wait_ge(breaks_in, 16 * 16)

        @block.tensor
        def _(pe):
            pe.wait_ge(made, 2)
            ident = cst[0:SEG_ROWS, C_IDENT:C_IDENT + SEG_ROWS]
            for i in range(3):
                pe.matmul(rows_ps[0:1, i * P:i * P + SEG_ROWS], col[:, i:i + 1], ident, start=True, stop=True)
            for b in range(SCAN_TILES):
                mm = pe.transpose(last_ps[:, b * P:b * P + SEG_ROWS], last[:, b * P:(b + 1) * P], ident)
            mm.then_inc(turned, 1)

        @block.vector
        def _(v):
            s = Steps(vec)
            s.done(v.memset(g["chain_f"][:, :, :, :], -BIG))
            s.done(v.memset(g["chain_b"][:, :, :, :], -BIG))
            v.wait_ge(keys_in, 64)
            s.done(v.tensor_copy(g["slot_rows"][:, :], slots[:, :]))
            s.done(v.tensor_copy(g["pick_row"][:, :], cst[0:SEG_ROWS, C_IDENT:C_IDENT + SEG_ROWS]))
            for i in range(2):
                s.done(v.tensor_tensor(brk[:, i, :], key[:, 0, :], key[:, 1 + i, :], ALU.is_equal))
            s.settled(v)
            s.done(v.tensor_scalar(brk[:, :, :], brk[:, :, :], -1.0, BIG, ALU.add, ALU.mult))
            s.settled(v)
            s.done(v.tensor_copy(brk_h[:, 0, :], brk[:, 0, :]))
            v.tensor_copy(brk_h[:, 1, ::-1], brk[:, 1, :]).then_inc(made, 1)
            s.done(v.tensor_scalar(last[:, :], brk[:, 1, :], -1.0, None, ALU.is_lt))
            s.done(v.tensor_reduce(col[:, 0:2], brk[:, :, :], AX.X, ALU.min))
            s.done(v.tensor_scalar(col[:, 2:3], brk[:, 0, 0:1], -1.0, None, ALU.is_ge))
            s.settled(v)
            v.wait_ge(made, 1)
            v.sem_inc(made, 1)
            v.wait_ge(turned, 1)
            for h in range(8):
                row = [rows_ps[0:1, i * P:i * P + SEG_ROWS].rearrange("a (k c) -> a k c", c=SCAN_ROWS) for i in range(3)]
                s.done(v.tensor_copy(g["chain_f"][:, :, h, 1:], row[0]))
                s.done(v.tensor_copy(g["chain_b"][:, :, h, 1:], row[1][:, :, ::-1]))
            s.done(v.tensor_copy(g["goes_on"][:, :], row[2][:, :, 0]))
            for b in range(SCAN_TILES):
                s.done(v.tensor_copy(
                    g["last"][:, :].rearrange("p (k c b) -> p (k c) b", c=SCAN_ROWS, b=SCAN_TILES)[:, :, b],
                    last_ps[:, b * P:b * P + SEG_ROWS]))
            s.settled(v)


def take_rows(gp, table, rows, cur, idx, free, ahead, landed, copied, width, before=0):
    def chunk(k, turn, half):
        gp.wait_ge(free, (k + (before - 1)) * CHUNK + ahead)
        gp.sem_inc(copied, 1)
        gp.tensor_copy(cur[:, half, :], idx[:, bass.ds(k * CHUNK, CHUNK)]).then_inc(copied, 1)
        gp.wait_ge(copied, (k + (before + 1)) * 3 - 1)
        gp.sem_inc(copied, 1)
        for j in range(CHUNK):
            gp.indirect_dma_start(out=rows[:, half, j, 0:width], out_offset=None, in_=table,
                                  in_offset=bass.IndirectOffsetOnAxis(ap=cur[:, half, j:j + 1], axis=0))\
                .then_inc(landed[half], 16)

    with gp.Fori(0, CHUNKS // 2) as i:
        for half in range(2):
            chunk(i * 2 + half, i, half)


def each_chunk(engine, body, last_apart=False):
    pairs = CHUNKS // 2 - (1 if last_apart else 0)
    with engine.Fori(0, pairs) as i:
        for half in range(2):
            body(i * 2 + half, i, half)
    for k in range(2 * pairs, CHUNKS):
        body(k, k // 2, k % 2)


def tile_windows(engine, regs, tile_win, way, tile):
    engine.reg_load(regs, tile_win[0:1, way, bass.ds(tile, len(regs))])
    return [engine.snap(r, min_val=0, max_val=WINDOWS - 1) for r in regs]


def each_turn(engine, k, regs, tile_win, body):
    with engine.Fori(0, TURNS // 2) as i:
        windows = tile_windows(engine, regs, tile_win, 0, k * CHUNK + i * (2 * STEP))
        for parity in range(2):
            body(i * 2 + parity, parity, windows[parity * STEP:(parity + 1) * STEP], True)
    body(TURNS - 1, 0, tile_windows(engine, regs[0:STEP], tile_win, 0, k * CHUNK + (TURNS - 1) * STEP), False)


def mean_with_bias(v, s, acc, bias, count):
    s.done(v.tensor_scalar(count, acc[:, :, FEAT], 1.0, None, ALU.max))
    for w in range(WINDOWS):
        s.done(v.scalar_tensor_tensor(out=acc[:, w, 0:FEAT], in0=bias, scalar=acc[:, w, FEAT:FEAT + 1],
                                      in1=acc[:, w, 0:FEAT], op0=ALU.mult, op1=ALU.add))
    s.settled(v)
    s.done(v.reciprocal(count, count))
    s.settled(v)
    s.done(v.tensor_tensor(acc[:, :, 0:FEAT], acc[:, :, 0:FEAT], count.unsqueeze(2).to_broadcast([P, WINDOWS, FEAT]),
                           ALU.mult))
    s.settled(v)


def relation_edges(nc, tag, cst, d, dram, g, rows, accs):
    with ExitStack() as ctx:
        sem = phase_semaphores(nc, tag, ctx)

        cur = ctx.enter_context(nc.sbuf_tensor(f"{tag}_cur", [P, 2, CHUNK], I32))
        onehot = ctx.enter_context(nc.sbuf_tensor(f"{tag}_onehot", [P, 2, 2, P], F32))
        sum_ps = [ctx.enter_context(nc.psum_tensor(f"{tag}_sum_ps{i}", [P, 512], F32)) for i in range(STEP)]
        ways = ((g["dst_slot"], g["fwd_idx"], dram["rel_table_f"]), (g["src_slot"], g["bwd_idx"], dram["rel_table_b"]))
        bias = ctx.enter_context(nc.sbuf_tensor(f"{tag}_bias", [P, FEAT], F32))
        count = ctx.enter_context(nc.sbuf_tensor(f"{tag}_count", [P, WINDOWS], F32))
        bias_in = sem("bias_in")
        x_in = sem("x_in")
        vec = sem("vec")
        landed = g["landed"][tag]
        copied = sem("copied")
        cleared = sem("cleared")
        onehot_made = sem("onehot_made")
        sum_made = sem("sum_made")
        sum_taken = sem("sum_taken")
        chunks_begun = sem("chunks_begun")
        AHEAD = 2 * CHUNK
        block = ctx.enter_context(nc.Block())

        @block.sync
        def _(sp):
            sp.dma_start(bias[:, :], d["L0_gnn_forward_bias"].rearrange("(a f) -> a f", a=1).to_broadcast([P, FEAT]))\
                .then_inc(bias_in, 16)
            sp.wait_ge(sum_made, (2 * CHUNKS - 1) * CHUNK + AHEAD)
            sp.dma_start(rows.rearrange("p a t f -> p (a t f)")[:, 0:WINDOWS * FEAT].rearrange("p (w f) -> p w f", f=FEAT),
                         d["x_pad"].rearrange("(w p) f -> p w f", p=P)).then_inc(x_in, 16)
            sp.wait_ge(x_in, 16)

        @block.gpsimd
        def _(gp):
            for way, (slot, idx, table) in enumerate(ways):
                take_rows(gp, table, rows, cur, idx, sum_made, AHEAD, landed, copied, FEAT, before=way * CHUNKS)

        @block.tensor
        def _(pe):
            pe.sem_inc(sum_made, AHEAD)
            pe.wait_ge(cleared, 3)

            def chunk(way, here, i, half):
                k = here + way * CHUNKS
                pe.wait_ge(landed[half], (i + (way * (CHUNKS // 2) + 1)) * (16 * CHUNK))
                pe.sem_inc(chunks_begun, 1)
                with pe.Fori(0, TURNS) as turn:
                    for j in range(STEP):
                        if j % 2 == 0:
                            pe.wait_ge(onehot_made, k * (2 * TURNS + 2) + turn * 2 + (j // 2 + 1))
                        pe.wait_ge(sum_taken, k * CHUNK + turn * STEP + (j + 1))
                        pe.matmul(sum_ps[j][:, 0:FEAT + 1], onehot[:, j // 2, j % 2, :],
                                  rows[:, half, bass.ds(turn * STEP + j, 1), 0:FEAT + 1].rearrange("p a f -> p (a f)"),
                                  start=True, stop=True).then_inc(sum_made, 1)

            for way in range(2):
                each_chunk(pe, lambda k, i, half: chunk(way, k, i, half))

        @block.vector
        def _(v):
            v.sem_inc(sum_taken, STEP)
            for acc in accs:
                v.memset(acc[:, :, :], 0.0).then_inc(cleared, 1)
            v.memset(rows[:, :, :, FEAT:FEAT + 1], 1.0).then_inc(cleared, 1)
            v.wait_ge(cleared, 3)
            regs = [v.alloc_register(f"{tag}_v_window{j}") for j in range(STEP)]

            def make(slot, tile, sub):
                for jj in range(2):
                    i = v.tensor_scalar(onehot[:, sub, jj, :], cst[:, C_IOTA:C_IOTA + P],
                                        slot[:, bass.ds(tile + (2 * sub + jj), 1)], None, ALU.is_equal)
                i.then_inc(onehot_made, 1)

            def chunk(way, here, i, half):
                k = here + way * CHUNKS
                slot, acc = ways[way][0], accs[way]
                v.wait_ge(sum_made, k * CHUNK + AHEAD)
                for sub in range(2):
                    make(slot, here * CHUNK, sub)
                with v.Fori(0, TURNS) as turn:
                    windows = tile_windows(v, regs, g["tile_win"], way, here * CHUNK + turn * STEP)
                    for sub in range(2):
                        v.wait_ge(sum_made, k * CHUNK + turn * STEP + (2 * sub + 2 + AHEAD))
                        make(slot, here * CHUNK + turn * STEP + STEP, sub)
                        for j in (2 * sub, 2 * sub + 1):
                            v.wait_ge(sum_taken, k * CHUNK + turn * STEP + (j + STEP))
                            a = acc[:, bass.ds(windows[j], 1), 0:FEAT + 1].rearrange("p a f -> p (a f)")
                            v.tensor_tensor(a, a, sum_ps[j][:, 0:FEAT + 1], ALU.add).then_inc(sum_taken, 1)

            each_chunk(v, lambda k, i, half: chunk(0, k, i, half))
            s = Steps(vec)
            v.wait_ge(bias_in, 16)
            v.wait_ge(sum_taken, CHUNKS * CHUNK + STEP)
            mean_with_bias(v, s, accs[0], bias[:, :], count[:, :])
            each_chunk(v, lambda k, i, half: chunk(1, k, i, half))


def logit_weights(v, s, w_sb, att, prod, heads, w_in, count):
    s.done(v.memset(w_sb[:, :, FEAT:NTC], 0.0))
    v.wait_ge(w_in, count)
    for i in range(2):
        for k in range(2):
            s.done(v.tensor_tensor(prod[:, i, k, :], w_sb[:, k, 0:FEAT], att[:, i, :], ALU.mult))
    s.settled(v)
    for i in range(2):
        for k in range(2):
            s.done(v.tensor_reduce(w_sb[:, k, FEAT + 8 * i:FEAT + 8 * i + heads],
                                   prod[:, i, k, :].rearrange("p (h d) -> p h d", h=heads), AX.X, ALU.add))
    s.settled(v)


def own_edges(v, s, nt, own):
    s.done(v.tensor_tensor(own[:, :, :], nt[:, :, 256:260], nt[:, :, 264:268], ALU.add))
    s.settled(v)
    s.done(v.scalar_tensor_tensor(out=nt[:, :, 268:272], in0=own[:, :, :], scalar=0.2, in1=own[:, :, :],
                                  op0=ALU.mult, op1=ALU.max))
    s.settled(v)


def finish(nc, tag, cst, kind, heads, d, dram, g, rows, acc, acc_b, nt, x_to, bias_name, out, following):
    D = FEAT // heads
    with ExitStack() as ctx:
        def sb(name, shape, dt=F32):
            return ctx.enter_context(nc.sbuf_tensor(f"{tag}_{name}", shape, dt))

        sem = phase_semaphores(nc, tag, ctx)

        flat = rows.rearrange("p a t f -> p (a t f)")
        x = flat[:, 0:WINDOWS * FEAT].rearrange("p (w f) -> p w f", f=FEAT)
        t = flat[:, WINDOWS * FEAT:2 * WINDOWS * FEAT].rearrange("p (w f) -> p w f", f=FEAT)
        bias = sb("bias", [P, 3, FEAT])
        loop_w = sb("loop_w", [P, 2, FEAT]) if kind == "relations" else None
        xt = sb("xt", [P, 2, 2, P]) if kind == "relations" or following else None
        den = sb("den", [P, 2, WINDOWS * 8])
        m = sb("m", [P, WINDOWS * 4])
        mean = sb("mean", [P, WINDOWS])
        var = sb("var", [P, WINDOWS])
        ps = [ctx.enter_context(nc.psum_tensor(f"{tag}_fin_ps{i}", [P, 512], F32)) for i in range(4)]
        x_in = sem("x_in")
        vec = sem("vec")
        to_scalar = sem("to_scalar")
        from_scalar = sem("from_scalar")
        turned = sem("turned")
        turned_out = sem("turned_out")
        looped = sem("looped")
        loop_taken = sem("loop_taken")
        y_ready = sem("y_ready")
        stored = sem("stored")
        groups = ((0, 9), (9, 17), (17, WINDOWS)) if following else ((0, WINDOWS),)
        ready_at = lambda w: 1 + max(i for i, (lo, hi) in enumerate(groups) if lo <= w)
        if following:
            w_sb = sb("w_sb", [P, 2, NTC])
            att = sb("att", [P, 2, FEAT])
            prod = sb("prod", [P, 2, 2, FEAT])
            own = sb("own", [P, WINDOWS, 4]) if following["self_edge"] else None
            w_in = sem("w_in")
            w_ready = sem("w_ready")
            h_done = sem("h_done")
            h_taken = sem("h_taken")
        block = ctx.enter_context(nc.Block())
        y = acc[:, :, 0:FEAT]
        norm = kind != "elu"

        @block.sync
        def _(sp):
            names = bias_name if isinstance(bias_name, tuple) else (bias_name,)
            for i in range(3):
                name = names[i] if i < len(names) else names[0]
                sp.dma_start(bias[:, i, :], d[name].rearrange("(a f) -> a f", a=1).to_broadcast([P, FEAT]))\
                    .then_inc(x_in, 16)
            if kind == "relations":
                sp.dma_start(loop_w[:, :, :], d["L0_gnn_loop_weight"].rearrange("(k p) n -> p k n", p=P)).then_inc(x_in, 16)
            if following:
                sp.dma_start(w_sb[:, :, 0:FEAT], d[following["w"]].rearrange("(k p) n -> p k n", p=P)).then_inc(w_in, 16)
                for i, name in enumerate((following["a_src"], following["a_dst"])):
                    sp.dma_start(att[:, i, :], d[name].rearrange("(a f) -> a f", a=1).to_broadcast([P, FEAT]))\
                        .then_inc(w_in, 16)
                for i, (lo, hi) in enumerate(groups):
                    sp.wait_ge(y_ready, i + 1)
                    sp.dma_start(x_to.rearrange("(w p) f -> p w f", p=P)[:, lo:hi, :], y[:, lo:hi, :]).then_inc(stored, 16)
                    sp.wait_ge(h_taken, hi)
                    sp.dma_start(dram["nodes"].rearrange("(w p) f -> p w f", p=P)[:, lo:hi, :], nt[:, lo:hi, 0:ROW])\
                        .then_inc(stored, 16)
                sp.wait_ge(stored, 32 * len(groups))
                return
            sp.wait_ge(y_ready, 1)
            if out is None:
                sp.dma_start(x_to.rearrange("(w p) f -> p w f", p=P), y).then_inc(stored, 16)
                sp.wait_ge(stored, 16)
            else:
                whole = NODES // P
                sp.dma_start(out[0:whole * P, :].rearrange("(w p) f -> p w f", p=P), y[:, 0:whole, :]).then_inc(stored, 16)
                sp.dma_start(out[whole * P:NODES, :], y[0:NODES - whole * P, whole, :]).then_inc(stored, 16)
                sp.wait_ge(stored, 32)

        loads = 16 * (4 if kind == "relations" else 3)

        before = WINDOWS if kind == "relations" else 0

        @block.tensor
        def _(pe):
            if kind == "relations":
                pe.wait_ge(x_in, loads)
                for w in range(WINDOWS):
                    if w >= 2:
                        pe.wait_ge(turned_out, w - 1)
                    for k in range(2):
                        mm = pe.transpose(ps[w % 2][:, k * P:(k + 1) * P], x[:, w, k * P:(k + 1) * P],
                                          cst[:, C_IDENT:C_IDENT + P])
                    mm.then_inc(turned, 1)
                    pe.wait_ge(turned_out, w + 1)
                    if w >= 2:
                        pe.wait_ge(loop_taken, w - 1)
                    for k in range(2):
                        mm = pe.matmul(ps[2 + w % 2][:, 0:FEAT], xt[:, w % 2, k, :], loop_w[:, k, :],
                                       start=(k == 0), stop=(k == 1))
                    mm.then_inc(looped, 1)
                pe.wait_ge(loop_taken, WINDOWS)
            if following:
                def turn_x(w):
                    pe.wait_ge(y_ready, ready_at(w))
                    if before + w >= 2:
                        pe.wait_ge(turned_out, before + w - 1)
                    for k in range(2):
                        mm = pe.transpose(ps[w % 2][:, k * P:(k + 1) * P], acc[:, w, k * P:(k + 1) * P],
                                          cst[:, C_IDENT:C_IDENT + P])
                    mm.then_inc(turned, 1)

                pe.wait_ge(w_ready, 1)
                turn_x(0)
                for w in range(WINDOWS):
                    if w + 1 < WINDOWS:
                        turn_x(w + 1)
                    pe.wait_ge(turned_out, before + w + 1)
                    if w >= 2:
                        pe.wait_ge(h_taken, w - 1)
                    for k in range(2):
                        mm = pe.matmul(ps[2 + w % 2][:, 0:NTC], xt[:, w % 2, k, :], w_sb[:, k, :],
                                       start=(k == 0), stop=(k == 1))
                    mm.then_inc(h_done, 1)

        @block.scalar
        def _(act):
            if kind == "relations":
                for w in range(WINDOWS):
                    act.wait_ge(turned, w + 1)
                    if w >= 2:
                        act.wait_ge(looped, w - 1)
                    act.copy(xt[:, w % 2, :, :].rearrange("p k e -> p (k e)"), ps[w % 2][:, 0:2 * P]).then_inc(turned_out, 1)
            def take_xt(w):
                act.wait_ge(turned, before + w + 1)
                if w >= 2:
                    act.wait_ge(h_done, w - 1)
                elif before:
                    act.wait_ge(looped, before)
                act.copy(xt[:, w % 2, :, :].rearrange("p k e -> p (k e)"), ps[w % 2][:, 0:2 * P]).then_inc(turned_out, 1)

            def take_h(w):
                act.wait_ge(h_done, w + 1)
                act.copy(nt[:, w, :], ps[2 + w % 2][:, 0:NTC]).then_inc(h_taken, 1)

            def take_next():
                w = taken[0]
                if w < WINDOWS:
                    take_xt(w)
                if w >= 1:
                    take_h(w - 1)
                taken[0] += 1

            taken = [0]
            n = 0
            if kind in ("self", "elu"):
                act.wait_ge(to_scalar, 1)
                act.activation(m[:, :], m[:, :], ACT.Exp).then_inc(from_scalar, 1)
                n = 1
            for group, (lo, hi) in enumerate(groups):
                calls = []
                if kind in ("self", "elu"):
                    calls.append((t[:, lo:hi, :], t[:, lo:hi, :], ACT.Exp))
                if norm:
                    calls.append((t[:, lo:hi, :], y[:, lo:hi, :], ACT.Square))
                    calls.append((var[:, lo:hi], var[:, lo:hi], ACT.Sqrt))
                for i, (to, of, function) in enumerate(calls):
                    if group and following:
                        start = groups[group - 1][0]
                        while taken[0] < start + (lo - start) * (i + 1) // (len(calls) + 1):
                            take_next()
                    n += 1
                    act.wait_ge(to_scalar, n)
                    act.activation(to, of, function).then_inc(from_scalar, 1)
            if following:
                while taken[0] <= WINDOWS:
                    take_next()

        @block.vector
        def _(v):
            s = Steps(vec)
            over_w = lambda a: a.unsqueeze(1).to_broadcast([P, WINDOWS, FEAT])
            called = [0]

            def scalar_part():
                called[0] += 1
                v.sem_inc(to_scalar, 1)
                v.wait_ge(from_scalar, called[0])

            def rest_of_group(lo, hi):
                n = hi - lo
                yg, xg, tg = y[:, lo:hi, :], x[:, lo:hi, :], t[:, lo:hi, :]
                over = lambda a: a.unsqueeze(2).to_broadcast([P, n, FEAT])
                heads_of = lambda a: a.rearrange("p w (h d) -> p w h d", h=heads)
                per_head = lambda a: a[:, lo * heads:hi * heads].rearrange("p (w h) -> p w h", h=heads).unsqueeze(3)\
                    .to_broadcast([P, n, heads, D])
                if kind != "relations":
                    if kind in ("self", "elu"):
                        s.done(v.tensor_tensor(heads_of(tg), heads_of(nt[:, lo:hi, 0:FEAT]), per_head(m), ALU.mult))
                        s.settled(v)
                        s.done(v.tensor_tensor(yg, yg, tg, ALU.add))
                        s.settled(v)
                    s.done(v.tensor_tensor(heads_of(yg), heads_of(yg), per_head(den[:, 0, :]), ALU.mult))
                    s.settled(v)
                    s.done(v.tensor_tensor(yg, yg, bias[:, 0, :].unsqueeze(1).to_broadcast([P, n, FEAT]), ALU.add))
                    s.settled(v)
                if kind in ("self", "elu"):
                    s.done(v.tensor_scalar(tg, yg, 0.0, None, ALU.min))
                    s.settled(v)
                    v.sem_inc(to_scalar, 1)
                    s.done(v.tensor_scalar(yg, yg, 0.0, -1.0, ALU.max, ALU.add))
                    s.settled(v)
                    called[0] += 1
                    v.wait_ge(from_scalar, called[0])
                    s.done(v.tensor_tensor(yg, yg, tg, ALU.add))
                    s.settled(v)
                if norm:
                    s.done(v.tensor_tensor(yg, yg, xg, ALU.add))
                    s.settled(v)
                    s.done(v.tensor_reduce(mean[:, lo:hi], yg, AX.X, ALU.add))
                    s.settled(v)
                    s.done(v.tensor_scalar(mean[:, lo:hi], mean[:, lo:hi], 1.0 / FEAT, None, ALU.mult))
                    s.settled(v)
                    s.done(v.tensor_tensor(yg, yg, over(mean[:, lo:hi]), ALU.subtract))
                    s.settled(v)
                    scalar_part()
                    s.done(v.tensor_reduce(var[:, lo:hi], tg, AX.X, ALU.add))
                    s.settled(v)
                    s.done(v.tensor_scalar(var[:, lo:hi], var[:, lo:hi], 1.0 / FEAT, EPS, ALU.mult, ALU.add))
                    s.settled(v)
                    scalar_part()
                    s.done(v.reciprocal(var[:, lo:hi], var[:, lo:hi]))
                    s.settled(v)
                    s.done(v.tensor_tensor(yg, yg, over(var[:, lo:hi]), ALU.mult))
                    s.settled(v)

            v.wait_ge(x_in, loads)
            if kind == "relations":
                mean_with_bias(v, s, acc_b, bias[:, 1, :], den[:, 0, 0:WINDOWS])
                s.done(v.tensor_tensor(y, y, acc_b[:, :, 0:FEAT], ALU.add))
                s.settled(v)
                s.done(v.tensor_tensor(y, y, over_w(bias[:, 2, :]), ALU.add))
                s.settled(v)
                for w in range(WINDOWS):
                    v.wait_ge(looped, w + 1)
                    v.scalar_tensor_tensor(out=acc[:, w, 0:FEAT], in0=ps[2 + w % 2][:, 0:FEAT], scalar=2.0,
                                           in1=acc[:, w, 0:FEAT], op0=ALU.mult, op1=ALU.add).then_inc(loop_taken, 1)
                v.wait_ge(loop_taken, WINDOWS)
            else:
                c = den[:, 0, 0:WINDOWS * heads]
                c3 = c.rearrange("p (w h) -> p w h", h=heads)
                if kind in ("self", "elu"):
                    m3 = m[:, :].rearrange("p (w h) -> p w h", h=heads)
                    c1 = den[:, 1, 0:WINDOWS * heads].rearrange("p (w h) -> p w h", h=heads)
                    zs = nt[:, :, 268:272]
                    has = acc[:, :, 264:265].to_broadcast([P, WINDOWS, heads])
                    s.done(v.tensor_tensor(c1, has, zs, ALU.mult))
                    s.settled(v)
                    s.done(v.tensor_tensor(m3, c1, acc[:, :, 260:264], ALU.subtract))
                    s.settled(v)
                    v.sem_inc(to_scalar, 1)
                    v.wait_ge(from_scalar, 1)
                    called[0] = 1
                    s.done(v.tensor_tensor(c3, acc[:, :, 256:260], m3, ALU.add))
                    s.settled(v)
                    s.done(v.tensor_scalar(c, c, 1e-16, None, ALU.add))
                else:
                    s.done(v.tensor_scalar(c3, acc[:, :, 256:256 + heads], 1e-10, None, ALU.max))
                s.settled(v)
                s.done(v.reciprocal(c, c))
                s.settled(v)
            for i, (lo, hi) in enumerate(groups):
                rest_of_group(lo, hi)
                v.sem_inc(y_ready, 1)
                if following and i == 0:
                    logit_weights(v, s, w_sb, att, prod, following["heads"], w_in, 48)
                    v.sem_inc(w_ready, 1)
            if following and following["self_edge"]:
                v.wait_ge(h_taken, WINDOWS)
                own_edges(v, s, nt, own)


def attention_edges(nc, tag, cst, kind, heads, d, dram, g, rows, acc, nt, rest):
    D = FEAT // heads
    Q = heads * SCAN_ROWS
    own_edge = kind in ("self", "elu")
    with_attr = kind == "edge"
    width = ROW + 1 if own_edge else FEAT + heads
    CHAIN = 22 + (3 if own_edge else 0) + (0 if with_attr else 5)
    with ExitStack() as ctx:
        def sb(name, shape, dt=F32):
            return ctx.enter_context(nc.sbuf_tensor(f"{tag}_{name}", shape, dt))

        sem = phase_semaphores(nc, tag, ctx)

        def bank(name):
            return ctx.enter_context(nc.psum_tensor(f"{tag}_{name}", [P, 512], F32))

        cur = sb("cur", [P, 2, CHUNK], I32)
        onehot = sb("onehot", [P, 2, STEP, P])
        hot_t = sb("hot_t", [P, 2, 2, P]) if with_attr else sb("hot_t", [P, 2, SCAN_LEN], BF16)
        distance = sb("distance", [P, STEP, P], BF16)
        z = sb("z", [P, heads * CHUNK])
        top = sb("top", [P, heads * CHUNK])
        scan_a = sb("scan_a", [Q, SCAN_LEN])
        scan_b = sb("scan_b", [Q, SCAN_LEN])
        entry = sb("entry", [Q, 1])
        chain_in = sb("chain_in", [1, 2, heads, SCAN_ROWS + 1])
        chain = sb("chain", [1, 2, heads, SCAN_ROWS + 1])
        chain_row = sb("chain_row", [1, 2, Q])
        carried = sb("carried", [1, 2, heads])
        fall = sb("fall", [1, heads])
        first_hot = sb("first_hot", [P, P])
        first_col = sb("first_col", [P, 1])
        factor = sb("factor", [P, heads])
        turn_ps = [bank("turn_ps0"), bank("turn_ps1")]
        dst_ps = [bank("dst_ps0"), bank("dst_ps1")]
        attr_ps = [bank("attr_ps0"), bank("attr_ps1")]
        scan_ps = bank("scan_ps")
        small_ps = bank("small_ps")
        sum_ps = [turn_ps[0], turn_ps[1], attr_ps[0], attr_ps[1]]
        spread_ps = [scan_ps, small_ps]
        TERMS_AT = 512 - (TURNS - 1) * 24
        assert width <= TERMS_AT
        row_ps = [dst_ps[0], dst_ps[1], scan_ps, small_ps]
        ROW_AT, COL_AT, FALL_AT, FIRST_AT = 352, 448, 456, 472
        if with_attr:
            attr = sb("attr", [9 * 4, 2, 2 * P], BF16)
            attr_w = sb("attr_w", [9 * 4, FEAT], BF16)
            gap = sb("gap", [P, 3, 2 * P], BF16)
            attr_w_part = gap[0:4, :, :]
            encoded = sb("encoded", [P, 2, 2 * FEAT])
            prod = sb("prod", [P, 2, FEAT])
            part = sb("part", [P, 2, 8])
            dst_part = sb("dst_part", [P, CHUNK, 8])
        else:
            nt_part = sb("nt_part", [P, WINDOWS, 3, 8], BF16)
            gap = sb("gap", [P, 2, SCAN_LEN], BF16)
            terms = sb("terms", [P, CHUNK, 8]) if own_edge else top[:, :].rearrange("p (t h) -> p t h", h=8)
            nt_rest = terms[:, 0:WINDOWS, :]

        landed = g["landed"][tag]
        copied = sem("copied")
        cleared = sem("cleared")
        spread = sem("spread")
        hot_t_made = sem("hot_t_made")
        dst_done = sem("dst_done")
        dst_taken = sem("dst_taken")
        weights_in = sem("weights_in")
        attr_in = [sem(f"attr_in{i}") for i in range(2)]
        enc_done = sem("enc_done")
        enc_out = sem("enc_out")
        enc_used = sem("enc_used")
        vec = sem("vec")
        z_ready = sem("z_ready")
        z_turned = sem("z_turned")
        ends_ready = sem("ends_ready")
        ends_row = sem("ends_row")
        entry_ready = sem("entry_ready")
        entry_col = sem("entry_col")
        first_ready = sem("first_ready")
        first_done = sem("first_done")
        first_out = sem("first_out")
        factor_ready = sem("factor_ready")
        top_ready = sem("top_ready")
        top_turned = sem("top_turned")
        less_top = sem("less_top")
        weights_made = sem("weights_made")
        hot_made = sem("hot_made")
        distances = sem("distances")
        gaps = sem("gaps")
        residual_in = sem("residual_in")
        terms_done = sem("terms_done")
        parts_split = sem("parts_split")
        part_made = sem("part_made")
        weighted = sem("weighted")
        sum_made = sem("sum_made")
        sum_taken = sem("sum_taken")
        chunks_begun = sem("chunks_begun")
        AHEAD = 2 * CHUNK
        PAIRS = 2 * TURNS
        block = ctx.enter_context(nc.Block())

        def residual(sp):
            sp.wait_ge(sum_made, (CHUNKS - 1) * CHUNK + AHEAD)
            sp.dma_start(rows.rearrange("p a t f -> p (a t f)")[:, 0:WINDOWS * FEAT].rearrange("p (w f) -> p w f", f=FEAT),
                         rest.rearrange("(w p) f -> p w f", p=P)).then_inc(residual_in, 16)
            sp.wait_ge(residual_in, 16)

        if not with_attr:
            @block.sync
            def _(sp):
                residual(sp)
        else:
            @block.sync
            def _(sp):
                sp.dma_start(prod[0:3, 0, :], d["L1_gnn_edge_W"]).then_inc(weights_in, 16)
                sp.dma_start(prod[3:4, 0, :], d["L1_gnn_edge_b"].rearrange("(a f) -> a f", a=1)).then_inc(weights_in, 16)
                sp.wait_ge(parts_split, 5)
                for n in range(9):
                    sp.dma_start(attr_w[n * 4:(n + 1) * 4, :], attr_w_part[:, n // 3, :]).then_inc(weights_in, 16)
                with sp.Fori(0, CHUNKS * TURNS) as turn:
                    for sub in range(2):
                        sp.wait_ge(enc_done, turn * 2 + (sub + 1))
                        for n in range(3):
                            sp.dma_start(attr[n * 12:(n + 1) * 12, sub, :].rearrange("a (t e) -> a t e", e=P),
                                         dram["attrs"][:, bass.ds(turn * STEP + 2 * sub, 2), :]).then_inc(attr_in[sub], 16)
                residual(sp)

        @block.gpsimd
        def _(gp):
            take_rows(gp, dram["nodes"], rows, cur, g["src_idx"], sum_made, AHEAD, landed, copied, ROW)

        @block.tensor
        def _(pe):
            ident = cst[:, C_IDENT:C_IDENT + P]
            pe.sem_inc(sum_made, AHEAD)
            pe.sem_inc(dst_done, STEP)
            if with_attr:
                pe.sem_inc(enc_done, 2)
                pe.wait_ge(weights_in, 16 * (2 + 9))
            else:
                pe.wait_ge(parts_split, 5)
            pe.wait_ge(cleared, 1)
            regs = [pe.alloc_register(f"{tag}_pe_window{j}") for j in range(2 * STEP)]

            def spread_pair(k, turn, sub):
                pe.wait_ge(hot_t_made, k * PAIRS + turn * 2 + (sub + 1))
                pe.sem_inc(chunks_begun, 1)
                pe.matmul(turn_ps[sub][:, 0:2 * P],
                          g["pick_row"][:, bass.ds(k * TURNS + turn, 1)].to_broadcast([SEG_ROWS, P]),
                          g["slot_rows"][:, sub * 2 * P:(sub + 1) * 2 * P], start=True, stop=True).then_inc(spread, 1)
                pe.wait_ge(attr_in[sub], (k * TURNS + turn + 1) * 48)
                pe.wait_ge(enc_out, k * PAIRS + turn * 2 + (sub + 1))
                for jj in range(2):
                    mm = pe.matmul(attr_ps[sub][:, jj * FEAT:(jj + 1) * FEAT],
                                   attr[:, sub, jj * P:(jj + 1) * P], attr_w[:, :], start=True, stop=True)
                mm.then_inc(enc_done, 1)

            def destination_rows(k):
                def turn_rows(turn, parity, windows, more):
                    for sub in range(2):
                        pe.wait_ge(hot_t_made, k * PAIRS + turn * 2 + (sub + 3))
                        for jj in range(2):
                            j = 2 * sub + jj
                            pe.wait_ge(dst_taken, k * CHUNK + turn * STEP + (j + 1))
                            pe.matmul(row_ps[j][:, 0:NTC], hot_t[:, sub, jj, :],
                                      nt[:, bass.ds(windows[j], 1), :].rearrange("p a f -> p (a f)"),
                                      start=True, stop=True).then_inc(dst_done, 1)
                        if more:
                            spread_pair(k, turn + 1, sub)

                for sub in range(2):
                    spread_pair(k, 0, sub)
                each_turn(pe, k, regs, g["tile_win"], turn_rows)

            def spread_turn(k, turn, parity):
                pe.wait_ge(hot_t_made, k * TURNS + (turn + 1))
                pe.sem_inc(chunks_begun, 1)
                pe.matmul(spread_ps[parity][:, :],
                          g["pick_row"][:, bass.ds(k * TURNS + turn, 1)].to_broadcast([SEG_ROWS, P]),
                          g["slot_rows"][:, :], start=True, stop=True).then_inc(spread, 1)

            def tile_terms(k, turn, parity, j, window):
                if j == 0:
                    pe.wait_ge(hot_t_made, k * TURNS + (turn + 3))
                pe.sem_inc(chunks_begun, 1)
                last = isinstance(turn, int) and turn == TURNS - 1
                mm = pe.matmul(dst_ps[0][:, j * 24:(j + 1) * 24] if last else sum_ps[j][:, bass.ds(turn * 24 + TERMS_AT, 24)],
                               hot_t[:, parity, j * P:(j + 1) * P],
                               nt_part[:, bass.ds(window, 1), :, :].rearrange("p a n f -> p (a n f)"),
                               start=True, stop=True)
                if j == STEP - 1:
                    mm.then_inc(terms_done, 1)

            if not with_attr:
                def first_terms(turn, parity, windows, more):
                    if more:
                        spread_turn(0, turn + 1, 1 - parity)
                    for j in range(STEP):
                        tile_terms(0, turn, parity, j, windows[j])

                spread_turn(0, 0, 0)
                each_turn(pe, 0, regs, g["tile_win"], first_terms)

            def chunk(k, i, half):
                if with_attr:
                    pe.wait_ge(sum_taken, k * CHUNK + STEP)
                    destination_rows(k)
                pe.wait_ge(z_ready, k + 2)
                pe.sem_inc(chunks_begun, 1)
                for b in range(SCAN_TILES):
                    mm = pe.transpose(scan_ps[0:Q, b * P:(b + 1) * P], (top if own_edge else z)[:, b::SCAN_TILES], ident)
                mm.then_inc(z_turned, 1)
                pe.wait_ge(ends_ready, k * 2 + 1)
                pe.sem_inc(chunks_begun, 1)
                pe.matmul(small_ps[0:1, ROW_AT:ROW_AT + Q], scan_a[:, SCAN_LEN - 1:SCAN_LEN], ident[0:Q, 0:Q],
                          start=True, stop=True).then_inc(ends_row, 1)
                pe.wait_ge(entry_ready, k * 2 + 1)
                pe.sem_inc(chunks_begun, 1)
                pe.matmul(small_ps[0:Q, COL_AT:COL_AT + 1], chain_row[:, 0, :], cst[0:1, C_ONES:C_ONES + 1],
                          start=True, stop=True).then_inc(entry_col, 1)
                pe.wait_ge(first_ready, k + 1)
                pe.matmul(dst_ps[1][:, FIRST_AT:FIRST_AT + 1], first_hot[:, :], ident[:, 0:1],
                          start=True, stop=True).then_inc(first_done, 1)
                pe.wait_ge(ends_ready, k * 2 + 2)
                pe.sem_inc(chunks_begun, 1)
                pe.matmul(small_ps[0:1, ROW_AT:ROW_AT + Q], scan_b[:, 0:1], ident[0:Q, 0:Q],
                          start=True, stop=True).then_inc(ends_row, 1)
                terms_too = not with_attr and not (isinstance(k, int) and k == CHUNKS - 1)
                if terms_too:
                    spread_turn(k + 1, 0, 0)
                pe.wait_ge(entry_ready, k * 2 + 2)
                pe.wait_ge(first_out, k + 1)
                pe.sem_inc(chunks_begun, 1)
                pe.matmul(dst_ps[1][:, FALL_AT:FALL_AT + heads], cst[0:1, C_ONES:C_ONES + P], fall[:, :],
                          start=True, stop=True)
                pe.matmul(small_ps[0:Q, COL_AT:COL_AT + 1], chain_row[:, 1, :], cst[0:1, C_ONES:C_ONES + 1],
                          start=True, stop=True).then_inc(entry_col, 1)
                pe.wait_ge(top_ready, k + 1)
                pe.sem_inc(chunks_begun, 1)
                for b in range(SCAN_TILES):
                    mm = pe.transpose(small_ps[:, b * Q:(b + 1) * Q], scan_b[:, b * P:(b + 1) * P], ident[0:Q, 0:Q])
                mm.then_inc(top_turned, 1)
                def sums(turn, parity, windows, more):
                    if terms_too and more:
                        spread_turn(k + 1, turn + 1, 1 - parity)
                    for j in range(STEP):
                        pe.wait_ge(weighted, k * CHUNK + turn * STEP + (j + 1))
                        if j == 0:
                            pe.wait_ge(hot_made, k * TURNS + (turn + 2))
                        pe.wait_ge(sum_taken, k * CHUNK + turn * STEP + (j + 1))
                        if terms_too:
                            tile_terms(k + 1, turn, parity, j, windows[j])
                        pe.matmul(sum_ps[j][:, 0:width], onehot[:, parity, j, :],
                                  rows[:, half, bass.ds(turn * STEP + j, 1), 0:width].rearrange("p a f -> p (a f)"),
                                  start=True, stop=True).then_inc(sum_made, 1)

                if terms_too:
                    pe.wait_ge(weighted, k * CHUNK + 1)
                    pe.sem_inc(chunks_begun, 1)
                    each_turn(pe, k + 1, regs, g["tile_win"], sums)
                else:
                    with pe.Fori(0, TURNS // 2) as pair:
                        for parity in range(2):
                            sums(pair * 2 + parity, parity, None, True)
                    sums(TURNS - 1, 0, None, False)

            each_chunk(pe, chunk, last_apart=not with_attr)

        @block.scalar
        def _(act):
            act.sem_inc(hot_made, 1)
            if with_attr:
                act.sem_inc(enc_out, 2)
                act.sem_inc(hot_t_made, 2)

            def make_hot(k, turn, parity):
                act.wait_ge(hot_made, k * TURNS + (turn + 1))
                act.sem_inc(chunks_begun, 1)
                for j in range(STEP):
                    act.activation(distance[:, j, :], cst[:, C_IOTA:C_IOTA + P], ACT.Abs, scale=-1.0,
                                   bias=g["dst_slot"][:, bass.ds(k * CHUNK + turn * STEP + j, 1)]).then_inc(distances, 1)
                act.wait_ge(sum_made, k * CHUNK + turn * STEP + (AHEAD - STEP))
                act.wait_ge(distances, k * CHUNK + turn * STEP + STEP)
                act.activation(onehot[:, parity, :, :].rearrange("p a n -> p (a n)"),
                               distance[:, :, :].rearrange("p a n -> p (a n)"), ACT.Relu, scale=-1.0,
                               bias=cst[:, C_ONES:C_ONES + 1]).then_inc(hot_made, 1)

            def encode(k, turn, sub):
                act.wait_ge(enc_done, k * PAIRS + turn * 2 + (sub + 3))
                act.wait_ge(enc_used, k * CHUNK + turn * STEP + (2 * sub + 2))
                act.activation(encoded[:, sub, :], attr_ps[sub][:, :], ACT.Relu).then_inc(enc_out, 1)

            def pair_hot_t(k, turn, sub):
                pair = k * PAIRS + turn * 2 + sub
                act.wait_ge(spread, pair + 1)
                act.wait_ge(hot_t_made, pair + 1)
                act.activation(gap[:, sub, :], turn_ps[sub][:, 0:2 * P], ACT.Abs, scale=-1.0,
                               bias=cst[:, C_ROW:C_ROW + 1]).then_inc(gaps, 1)
                act.wait_ge(gaps, pair + 1)
                act.wait_ge(dst_done, k * CHUNK + turn * STEP + (2 * sub + 2))
                act.activation(hot_t[:, sub, :, :].rearrange("p a n -> p (a n)"), gap[:, sub, :], ACT.Relu, scale=-1.0,
                               bias=cst[:, C_ONES:C_ONES + 1]).then_inc(hot_t_made, 1)

            def turn_hot_t(k, turn, parity):
                number = k * TURNS + turn
                act.wait_ge(spread, number + 1)
                act.wait_ge(hot_t_made, number + 1)
                act.activation(gap[:, parity, :], spread_ps[parity][:, :], ACT.Abs, scale=-1.0,
                               bias=cst[:, C_ROW:C_ROW + 1]).then_inc(gaps, 1)
                act.wait_ge(gaps, number + 1)
                act.wait_ge(terms_done, number + 1)
                act.activation(hot_t[:, parity, :], gap[:, parity, :], ACT.Relu, scale=-1.0,
                               bias=cst[:, C_ONES:C_ONES + 1]).then_inc(hot_t_made, 1)

            if not with_attr:
                act.sem_inc(hot_t_made, 2)
                act.sem_inc(terms_done, 2)
                with act.Fori(0, TURNS // 2) as pair:
                    for parity in range(2):
                        turn_hot_t(0, pair * 2 + parity, parity)
                turn_hot_t(0, TURNS - 1, 0)

            def chunk(k, i, half):
                if with_attr:
                    for sub in range(2):
                        pair_hot_t(k, 0, sub)
                    with act.Fori(0, TURNS - 1) as turn:
                        for sub in range(2):
                            encode(k, turn, sub)
                            pair_hot_t(k, turn + 1, sub)
                    for sub in range(2):
                        encode(k, TURNS - 1, sub)
                act.wait_ge(sum_made, k * CHUNK + AHEAD)
                make_hot(k, 0, 0)
                act.wait_ge(first_done, k + 1)
                act.copy(first_col[:, :], dst_ps[1][:, FIRST_AT:FIRST_AT + 1]).then_inc(first_out, 1)
                act.wait_ge(first_out, k + 1)
                act.wait_ge(entry_col, k * 2 + 2)
                act.activation(factor[:, :], dst_ps[1][:, FALL_AT:FALL_AT + heads], ACT.Exp,
                               scale=first_col[:, 0:1]).then_inc(factor_ready, 1)
                terms_too = not with_attr and not (isinstance(k, int) and k == CHUNKS - 1)
                if terms_too:
                    act.wait_ge(terms_done, (k + 1) * TURNS + 2)
                    act.sem_inc(chunks_begun, 1)
                    turn_hot_t(k + 1, 0, 0)
                act.wait_ge(less_top, k + 1)
                act.activation(rows[:, half, :, FEAT:FEAT + heads].rearrange("p t h -> p h t"),
                               z[:, :].rearrange("p (h t) -> p h t", h=heads), ACT.Exp).then_inc(weights_made, 1)
                with act.Fori(0, TURNS // 2) as pair:
                    for parity in range(2):
                        make_hot(k, pair * 2 + (parity + 1), 1 - parity)
                        if terms_too:
                            turn_hot_t(k + 1, pair * 2 + (parity + 1), 1 - parity)

            each_chunk(act, chunk, last_apart=not with_attr)

        @block.vector
        def _(v):
            v.sem_inc(sum_taken, STEP)
            v.sem_inc(z_ready, 1)
            if with_attr:
                v.sem_inc(dst_taken, STEP)
                v.sem_inc(enc_used, STEP)
            v.memset(acc[:, :, :], 0.0).then_inc(cleared, 1)
            v.memset(chain_in[:, :, :, :], -BIG).then_inc(cleared, 1)
            v.memset(carried[:, :, :], -BIG).then_inc(cleared, 1)
            v.wait_ge(cleared, 3)
            if with_attr:
                v.wait_ge(weights_in, 32)
                split_bf16(v, prod[0:4, 0, :], [attr_w_part[:, n, :] for n in range(3)], prod[0:4, 1, :], parts_split)
                v.wait_ge(parts_split, 5)
            else:
                split_bf16(v, nt[:, :, ROW:NTC], [nt_part[:, :, n, :] for n in range(3)], nt_rest, parts_split)
            regs = [v.alloc_register(f"{tag}_v_window{j}") for j in range(2 * STEP)]
            slot = g["dst_slot"]

            def edge_logits(k, turn, sub):
                tile = k * CHUNK + turn * STEP
                v.wait_ge(enc_out, k * PAIRS + turn * 2 + (sub + 3))
                for jj in range(2):
                    v.wait_ge(dst_done, tile + (2 * sub + jj + 1 + STEP))
                    v.tensor_tensor(prod[:, jj, :], row_ps[2 * sub + jj][:, 0:FEAT],
                                    encoded[:, sub, jj * FEAT:(jj + 1) * FEAT], ALU.mult).then_inc(enc_used, 1)
                for jj in range(2):
                    v.wait_ge(enc_used, tile + (2 * sub + jj + 1 + STEP))
                    v.wait_ge(dst_taken, tile + (2 * sub + jj - 1 + STEP))
                    v.tensor_reduce(part[:, jj, :], prod[:, jj, :].rearrange("p (h d) -> p h d", h=8), AX.X, ALU.add)\
                        .then_inc(part_made, 1)
                for jj in range(2):
                    v.wait_ge(part_made, tile + (2 * sub + jj + 1))
                    v.tensor_tensor(dst_part[:, bass.ds(turn * STEP + (2 * sub + jj), 1), :].rearrange("p a h -> p (a h)"),
                                    row_ps[2 * sub + jj][:, ROW:NTC], part[:, jj, :], ALU.add).then_inc(dst_taken, 1)

            def chunk(k, i, half):
                s = Steps(vec, k * CHAIN)
                zh = z[:, :].rearrange("p (h t) -> p h t", h=heads)
                hr = lambda a: a.rearrange("p t h -> p h t")
                if with_attr:
                    def logits(turn):
                        for sub in range(2):
                            edge_logits(k, turn, sub)

                    with v.Fori(0, TURNS // 2) as pair:
                        for parity in range(2):
                            logits(pair * 2 + parity)
                    for sub in range(2):
                        edge_logits(k, TURNS - 1, sub)
                v.tensor_scalar(first_hot[:, :], cst[:, C_IOTA:C_IOTA + P], slot[:, bass.ds(k * CHUNK, 1)], None,
                                ALU.is_equal).then_inc(first_ready, 1)
                v.wait_ge(landed[half], (i + 1) * (16 * CHUNK))
                if with_attr:
                    v.wait_ge(dst_taken, (k + 1) * CHUNK + STEP)
                    term = dst_part[:, :, :]
                else:
                    v.wait_ge(terms_done, (k + 1) * TURNS + 2)
                    full = (TURNS - 1) * STEP
                    parts = [(terms[:, j:full:STEP, :], sum_ps[j][:, TERMS_AT:512]) for j in range(STEP)]
                    for to, of in parts + [(terms[:, full:CHUNK, :], dst_ps[0][:, 0:STEP * 24])]:
                        s.done(v.tensor_reduce(to, of.rearrange("p (t n h) -> p t h n", n=3, h=8), AX.X, ALU.add))
                    s.settled(v)
                    term = terms[:, :, :]
                s.done(v.tensor_tensor(zh, hr(rows[:, half, :, FEAT:FEAT + heads]), hr(term[:, :, 0:heads]), ALU.add))
                s.settled(v)
                s.done(v.scalar_tensor_tensor(out=z[:, :], in0=z[:, :], scalar=0.2, in1=z[:, :], op0=ALU.mult, op1=ALU.max))
                s.settled(v)
                if own_edge:
                    s.done(v.tensor_tensor(top[:, :].rearrange("p (h t) -> p h t", h=heads), zh, hr(term[:, :, 4:8]), ALU.max))
                    s.settled(v)
                v.sem_inc(z_ready, 1)
                breaks = g["break_f"][0:Q, bass.ds(k, 1), :].rearrange("q a e -> q (a e)")
                v.wait_ge(z_turned, k + 1)
                s.done(v.tensor_tensor_scan(scan_a[:, :], breaks, scan_ps[0:Q, :], -BIG, ALU.add, ALU.max))
                s.settled(v)
                v.sem_inc(ends_ready, 1)
                v.wait_ge(ends_row, k * 2 + 1)
                ends = small_ps[0:1, ROW_AT:ROW_AT + Q].rearrange("a (h c) -> a h c", h=heads)
                s.done(v.tensor_copy(chain_in[:, 0, :, 1:], ends))
                s.done(v.tensor_copy(chain_in[:, 0, :, 0], carried[:, half, :]))
                s.settled(v)
                s.done(v.tensor_tensor_scan(chain[:, 0, :, :].rearrange("a h c -> a (h c)"),
                                            g["chain_f"][:, bass.ds(k, 1), 0:heads, :].rearrange("a b h c -> a (b h c)"),
                                            chain_in[:, 0, :, :].rearrange("a h c -> a (h c)"), -BIG, ALU.add, ALU.max))
                s.settled(v)
                s.done(v.tensor_copy(chain_row[:, 0, :].rearrange("a (h c) -> a h c", h=heads), chain[:, 0, :, 0:SCAN_ROWS]))
                s.done(v.tensor_copy(carried[:, 1 - half, :], chain[:, 0, :, SCAN_ROWS]))
                s.settled(v)
                v.sem_inc(entry_ready, 1)
                v.wait_ge(entry_col, k * 2 + 1)
                s.done(v.tensor_copy(entry[:, :], small_ps[0:Q, COL_AT:COL_AT + 1]))
                s.settled(v)
                s.done(v.tensor_tensor_scan(scan_a[:, :], breaks, scan_ps[0:Q, :], entry[:, :], ALU.add, ALU.max))
                s.settled(v)
                breaks = g["break_b"][0:Q, bass.ds(k, 1), :].rearrange("q a e -> q (a e)")
                s.done(v.tensor_tensor_scan(scan_b[:, ::-1], breaks, scan_a[:, ::-1], -BIG, ALU.add, ALU.max))
                s.settled(v)
                v.sem_inc(ends_ready, 1)
                v.wait_ge(ends_row, k * 2 + 2)
                s.done(v.tensor_copy(chain_in[:, 1, :, 0:SCAN_ROWS], ends))
                s.settled(v)
                s.done(v.tensor_tensor_scan(chain[:, 1, :, :].rearrange("a h c -> a (h c)")[:, ::-1],
                                            g["chain_b"][:, bass.ds(k, 1), 0:heads, :].rearrange("a b h c -> a (b h c)"),
                                            chain_in[:, 1, :, :].rearrange("a h c -> a (h c)")[:, ::-1], -BIG, ALU.add, ALU.max))
                s.settled(v)
                s.done(v.tensor_copy(chain_row[:, 1, :].rearrange("a (h c) -> a h c", h=heads), chain[:, 1, :, 1:]))
                s.done(v.tensor_tensor(fall[:, :], carried[:, half, :], chain[:, 1, :, 0], ALU.subtract))
                s.settled(v)
                s.done(v.tensor_scalar(fall[:, :], fall[:, :], g["goes_on"][:, bass.ds(k, 1)], None, ALU.mult))
                s.settled(v)
                v.sem_inc(entry_ready, 1)
                v.wait_ge(entry_col, k * 2 + 2)
                s.done(v.tensor_copy(entry[:, :], small_ps[0:Q, COL_AT:COL_AT + 1]))
                s.settled(v)
                s.done(v.tensor_tensor_scan(scan_b[:, ::-1], breaks, scan_a[:, ::-1], entry[:, :], ALU.add, ALU.max))
                s.settled(v)
                v.sem_inc(top_ready, 1)
                v.reg_load(regs[0], g["tile_win"][0:1, 0, bass.ds(k * CHUNK, 1)])
                window = v.snap(regs[0], min_val=0, max_val=WINDOWS - 1)
                v.wait_ge(factor_ready, k + 1)
                v.wait_ge(sum_taken, k * CHUNK + STEP)
                a = acc[:, bass.ds(window, 1), :].rearrange("p a f -> p (a f)")
                s.done(v.tensor_tensor(a[:, 0:FEAT].rearrange("p (h d) -> p h d", h=heads),
                                       a[:, 0:FEAT].rearrange("p (h d) -> p h d", h=heads),
                                       factor[:, :].unsqueeze(2).to_broadcast([P, heads, D]), ALU.mult))
                s.done(v.tensor_tensor(a[:, FEAT:FEAT + heads], a[:, FEAT:FEAT + heads], factor[:, :], ALU.mult))
                s.settled(v)
                v.wait_ge(top_turned, k + 1)
                s.done(v.tensor_copy(top[:, :].rearrange("p (q b) -> p b q", b=SCAN_TILES),
                                     small_ps[:, 0:SCAN_TILES * Q].rearrange("p (b q) -> p b q", b=SCAN_TILES)))
                s.settled(v)
                s.done(v.tensor_tensor(z[:, :], z[:, :], top[:, :], ALU.subtract))
                s.settled(v)
                v.sem_inc(less_top, 1)
                if own_edge:
                    lasts = g["last"][:, bass.ds(k * CHUNK, CHUNK)]
                    s.done(v.tensor_tensor(hr(rows[:, half, :, 260:264]), top[:, :].rearrange("p (h t) -> p h t", h=heads),
                                           lasts.unsqueeze(1).to_broadcast([P, heads, CHUNK]), ALU.mult))
                    s.done(v.tensor_scalar(rows[:, half, :, ROW:ROW + 1].rearrange("p t a -> p (t a)"), lasts, 1.0, None, ALU.mult))
                    s.settled(v)
                assert s.n == CHAIN, s.n
                v.wait_ge(weights_made, k + 1)

                def weigh(tile):
                    r = rows[:, half, bass.ds(tile, 1), :]
                    v.tensor_tensor(r[:, :, 0:FEAT].rearrange("p t (h d) -> p (t h) d", h=heads),
                                    r[:, :, 0:FEAT].rearrange("p t (h d) -> p (t h) d", h=heads),
                                    r[:, :, FEAT:FEAT + heads].rearrange("p t h -> p (t h)").unsqueeze(2)
                                    .to_broadcast([P, heads, D]), ALU.mult).then_inc(weighted, 1)

                def turn_sums(turn, parity, windows, more):
                    tile = k * CHUNK + turn * STEP
                    for j in range(STEP):
                        if more:
                            weigh(turn * STEP + (STEP + j))
                        v.wait_ge(sum_made, tile + (j + 1 + AHEAD))
                        v.wait_ge(sum_taken, tile + (j + STEP))
                        a = acc[:, bass.ds(windows[j], 1), 0:width].rearrange("p a f -> p (a f)")
                        v.tensor_tensor(a, a, sum_ps[j][:, 0:width], ALU.add).then_inc(sum_taken, 1)

                for tile in range(STEP):
                    weigh(tile)
                each_turn(v, k, regs, g["tile_win"], turn_sums)

            each_chunk(v, chunk)


def build(nc, d, out):
    dram = {}
    for name, shape, dt in (("src_win", [EDGES], F32), ("places", [EDGES], I32), ("records", [TILES * P, 2], I32),
                            ("keys", [TILES + 2, P], F32), ("slots", [TILES, P], F32), ("attrs", [3 * 4, TILES, P], BF16),
                            ("tile_win", [2, TILES], I32),
                            ("breaks", [2, SEG_ROWS, SCAN_LEN], BF16), ("rel_table_f", [NODES_PAD * RELS, FEAT], F32),
                            ("rel_table_b", [NODES_PAD * RELS, FEAT], F32),
                            ("nodes", [NODES_PAD, ROW], F32), ("x1", [NODES_PAD, FEAT], F32),
                            ("x2", [NODES_PAD, FEAT], F32)):
        dram[name] = nc.dram_tensor(f"dram_{name}", shape, dt, kind="Internal").ap()
    with ExitStack() as ctx:
        def sb(name, shape, dt=F32):
            return ctx.enter_context(nc.sbuf_tensor(name, shape, dt))

        cst = sb("cst", [P, C_COLS])
        g = {}
        g["landed"] = {tag: [ctx.enter_context(nc.semaphore(f"{tag}_landed{i}")) for i in range(2)]
                       for tag in ("group", "rel", "edges", "att0", "att1", "att2", "att3")}
        g["src_idx"] = sb("src_idx", [P, TILES], I32)
        g["dst_slot"] = sb("dst_slot", [P, TILES + STEP])
        g["tile_win"] = sb("tile_win", [1, 2, TILES], I32)
        nt = sb("nt", [P, WINDOWS, NTC])
        plan = (
            ("edge", 8, "x1", "x2", "L1_gnn_W", "L1_gnn_a_src", "L1_gnn_a_dst", "L1_gnn_bias"),
            ("elu", 4, "x2", "x1", "L2_gnn_W1", "L2_gnn_att_src1", "L2_gnn_att_dst1", "L2_gnn_b1"),
            ("self", 4, "x2", "x1", "L2_gnn_W2", "L2_gnn_att_src2", "L2_gnn_att_dst2", "L2_gnn_b2"),
            ("plain", 8, "x1", "x2", "L3_gnn_W", "L3_gnn_a_src", "L3_gnn_a_dst", "L3_gnn_bias"))

        def following(n):
            if n == len(plan):
                return None
            kind, heads, rest, x_to, w, a_src, a_dst, bias = plan[n]
            return {"heads": heads, "self_edge": kind in ("self", "elu"), "w": w, "a_src": a_src, "a_dst": a_dst}

        with ExitStack() as relations:
            for name, shape, dt in (("fwd_idx", [P, TILES], I32), ("bwd_idx", [P, TILES], I32),
                                    ("src_slot", [P, TILES + STEP], F32), ("tile_win4", [QUARTERS, 2, QT], I32),
                                    ("win128", [QT, 2, QUARTERS], F32), ("record", [EP, EJ, 2], I32),
                                    ("pos_i", [EP, EJ], I32)):
                g[name] = relations.enter_context(nc.sbuf_tensor(name, shape, dt))
            group_edges(nc, "group", cst, d, dram, g, nt)
            project_relations(nc, "rel", cst, d, dram, g)
            grouped_slots(nc, "slots", cst, dram, g)
            rows = relations.enter_context(nc.sbuf_tensor("rel_rows", [P, 2, CHUNK, COLS], F32))
            acc = relations.enter_context(nc.sbuf_tensor("acc_f", [P, WINDOWS, COLS], F32))
            acc_b = relations.enter_context(nc.sbuf_tensor("acc_b", [P, WINDOWS, COLS], F32))
            relation_edges(nc, 'edges', cst, d, dram, g, rows, (acc, acc_b))
            finish(nc, "fin0", cst, "relations", 1, d, dram, g, rows, acc, acc_b, nt, dram["x1"],
                   ("L0_gnn_forward_bias", "L0_gnn_backward_bias", "L0_gnn_self_bias"), None, following(0))
        g["break_f"] = sb("break_f", [8 * SCAN_ROWS, CHUNKS, SCAN_LEN], BF16)
        g["break_b"] = sb("break_b", [8 * SCAN_ROWS, CHUNKS, SCAN_LEN], BF16)
        g["chain_f"] = sb("chain_f", [1, CHUNKS, 8, SCAN_ROWS + 1], BF16)
        g["chain_b"] = sb("chain_b", [1, CHUNKS, 8, SCAN_ROWS + 1], BF16)
        g["goes_on"] = sb("goes_on", [1, CHUNKS])
        g["last"] = sb("last", [P, TILES])
        g["slot_rows"] = sb("slot_rows", [SEG_ROWS, SCAN_LEN], BF16)
        g["pick_row"] = sb("pick_row", [SEG_ROWS, SEG_ROWS], BF16)
        scan_tables(nc, 'scan', cst, dram, g)
        acc = sb("acc", [P, WINDOWS, COLS])
        rows = sb("rows", [P, 2, CHUNK, COLS])
        for n, (kind, heads, rest, x_to, w, a_src, a_dst, bias) in enumerate(plan):
            attention_edges(nc, f'att{n}', cst, kind, heads, d, dram, g, rows, acc, nt, dram[rest])
            then = following(n + 1)
            finish(nc, f'fin{n + 1}', cst, kind, heads, d, dram, g, rows, acc, None, nt, dram[x_to], bias,
                   None if then else out, then)



def constants():
    import numpy as np
    c = np.zeros((P, C_COLS), np.float32)
    p = np.arange(EP)
    c[:, C_IDENT:C_IDENT + P] = np.eye(P)
    c[:, C_IOTA:C_IOTA + P] = np.arange(P)
    c[:, C_ONES:C_ONES + P] = 1
    c[:, C_ROW] = np.arange(P)
    c[:EP, C_BEFORE:C_BEFORE + EP] = (p[:, None] // PARTS == p // PARTS) & (p[:, None] < p)
    c[:EP, C_WINOH:C_WINOH + WINDOWS] = p[:, None] // PARTS == np.arange(WINDOWS)
    c[:EP, C_PART:C_PART + PARTS] = p[:, None] % PARTS == np.arange(PARTS)
    c[:EP, C_WIN] = p // PARTS
    c[:QT, C_TILE:C_TILE + QUARTERS] = np.arange(QT)[:, None] + QT * np.arange(QUARTERS)
    return c


def kernel(**inputs):
    import numpy as _np
    import concourse.bacc as _bacc
    from concourse import mybir as _mybir
    from concourse.bass_utils import run_bass_kernel_spmd as _run

    def padded(a, value):
        return _np.concatenate([a, _np.full((P,) + a.shape[1:], value, a.dtype)])

    inputs = {name: _np.asarray(a) for name, a in inputs.items()}
    given = {name: inputs[name] for name in (
        "src", "dst", "edge_type_16", "L0_gnn_Wf", "L0_gnn_Wb", "L0_gnn_loop_weight", "L0_gnn_forward_bias",
        "L0_gnn_backward_bias", "L0_gnn_self_bias", "L1_gnn_edge_b", "L1_gnn_bias", "L2_gnn_W1", "L2_gnn_b1",
        "L2_gnn_W2", "L2_gnn_b2", "L3_gnn_bias")}
    for name in ("L1_gnn_a_src", "L1_gnn_a_dst", "L2_gnn_att_src1", "L2_gnn_att_dst1", "L2_gnn_att_src2",
                 "L2_gnn_att_dst2", "L3_gnn_a_src", "L3_gnn_a_dst"):
        given[name] = inputs[name].reshape(-1)
    for name in ("L1_gnn_W", "L1_gnn_edge_W", "L3_gnn_W"):
        given[name] = inputs[name].T
    x = inputs["x"]
    given["x_pad"] = _np.concatenate([x, _np.zeros((NODES_PAD - NODES, FEAT), x.dtype)])
    given["src_pad"] = padded(inputs["src"], 0)
    given["dst_pad"] = padded(inputs["dst"], int(FAR))
    given["type_pad"] = padded(inputs["edge_type_16"], 0)
    for i in range(3):
        given[f"attr{i}"] = padded(inputs["edge_attr_3"][:, i], 0)
    given["consts"] = constants()

    nc = _bacc.Bacc("TRN2", target_bir_lowering=False, num_devices=1)
    arrays, d = {}, {}
    for name, a in given.items():
        a = _np.ascontiguousarray(a)
        arrays[f"in_{name}"] = a
        d[name] = nc.dram_tensor(f"in_{name}", a.shape, _mybir.dt.from_np(a.dtype), kind="ExternalInput").ap()
    out = nc.dram_tensor("out", (NODES, FEAT), F32, kind="ExternalOutput").ap()
    build(nc, d, out)
    r = _run(nc, [arrays], core_ids=[0])
    return r.results[0]["out"]
```
